# Optimizing a Trainium2 kernel written in Bass

```python
import numpy as np
import jax
import jax.numpy as jnp

def _softmax(x, axis=-1):
    return jax.nn.softmax(x, axis=axis)

def _gelu(x):
    return jax.nn.gelu(x, approximate=True)

def _silu(x):
    return jax.nn.silu(x)

def _sigmoid(x):
    return jax.nn.sigmoid(x)

def _layernorm(x, axis=-1, eps=1e-05):
    m = jnp.mean(x, axis=axis, keepdims=True)
    v = jnp.var(x, axis=axis, keepdims=True)
    return (x - m) / jnp.sqrt(v + eps)

def _scatter_add(tgt, idx, src, axis=0):
    return tgt.at[idx].add(src)

def _segment_sum(src, seg, n):
    return jax.ops.segment_sum(src, seg, n)
kernel_name = 'mk_xattn_ffn_d2_seqx_r4_5e1875'

def setup_inputs(seed: int=0):
    np.random.seed(seed)
    _w = jnp.asarray

    def _rec_inputs():
        import jax
        import jax.numpy as jnp
        _rk = jax.random.key(seed)
        x = 7.22e-05 + 1 * jax.random.normal(jax.random.fold_in(_rk, 1), (4, 512, 256), jnp.float32)
        _lenS = 512 - jax.random.randint(jax.random.fold_in(_rk, 7), (4,), 0, max(1, 512 // 4) + 1, jnp.int32)
        _lenS2 = 512 - jax.random.randint(jax.random.fold_in(_rk, 8), (4,), 0, max(1, 512 // 4) + 1, jnp.int32)
        _ctx_1024P = jax.random.normal(jax.random.fold_in(_rk, 11), (4, 16, 256), jnp.float32)
        _ctx_1024c = jax.random.dirichlet(jax.random.fold_in(_rk, 511), 0.3 * jnp.ones((16,), jnp.float32), (4, 512))
        _ctx_1024t = jnp.einsum('bsk,bkd->bsd', _ctx_1024c, _ctx_1024P)
        _ctx_1024t = _ctx_1024t * jax.lax.rsqrt(jnp.mean(jnp.square(_ctx_1024t)) + 1e-12) * 0.953939
        ctx_1024 = 4.13588e-05 + 0.999923 * (_ctx_1024t + 0.3 * jax.random.normal(jax.random.fold_in(_rk, 611), (4, 512, 256), jnp.float32))
        return (x, ctx_1024)
    x, ctx_1024 = _rec_inputs()

    def _L0_xattn_setup():
        import jax, jax.numpy as jnp
        import numpy as np
        N_HEADS = 16
        D_MODEL = 256
        HEAD_DIM = D_MODEL // N_HEADS
        B, S = (4, 512)
        key = jax.random.key(seed)
        ks = jax.random.split(key, 11)
        sc = 0.02
        return {'query': jax.random.normal(ks[0], (B, S, D_MODEL), jnp.float32), 'key': jax.random.normal(ks[1], (B, S, D_MODEL), jnp.float32), 'value': jax.random.normal(ks[2], (B, S, D_MODEL), jnp.float32), 'Wq': jax.random.normal(ks[3], (D_MODEL, HEAD_DIM), jnp.float32) * sc, 'bq': jnp.zeros((HEAD_DIM,), jnp.float32), 'Wk': jax.random.normal(ks[4], (D_MODEL, HEAD_DIM), jnp.float32) * sc, 'bk': jnp.zeros((HEAD_DIM,), jnp.float32), 'Wv': jax.random.normal(ks[5], (D_MODEL, HEAD_DIM), jnp.float32) * sc, 'bv': jnp.zeros((HEAD_DIM,), jnp.float32), 'Wc': jax.random.normal(ks[6], (D_MODEL, D_MODEL), jnp.float32) * sc, 'bc': jnp.zeros((D_MODEL,), jnp.float32), 'Wo': jax.random.normal(ks[7], (D_MODEL, D_MODEL), jnp.float32) * sc, 'bo': jnp.zeros((D_MODEL,), jnp.float32)}
    _L0_xattn_all = _L0_xattn_setup()
    _L0_xattn_in = {k: v for k, v in _L0_xattn_all.items() if k in ('Wq', 'bq', 'Wk', 'bk', 'Wv', 'bv', 'Wc', 'bc', 'Wo', 'bo')}
    del _L0_xattn_all

    def _L0_ffn_setup():
        import jax, jax.numpy as jnp
        import numpy as np
        DIM = 256
        NUM_EXPERTS = 8
        TOP_K = 2
        HIDDEN = 4 * DIM // TOP_K
        BS, SLEN = (1, 512)

        def _moe(x, gate_w, w_up, w_down, expert_bias):
            bs, slen, dim = x.shape
            xf = x.reshape(-1, dim)
            scores = jax.nn.sigmoid(xf @ gate_w.T)
            biased = scores + expert_bias
            _, sel = jax.lax.top_k(biased, TOP_K)
            top_scores = jnp.take_along_axis(scores, sel, axis=-1)

            def body(acc, ew):
                e, wu, wd = ew
                w_t = jnp.sum(jnp.where(sel == e, top_scores, 0.0), axis=-1)
                xe = xf * w_t[:, None]
                h = jnp.square(jax.nn.relu(xe @ wu.T))
                return (acc + h @ wd.T, None)
            out0 = jnp.zeros_like(xf)
            out, _ = jax.lax.scan(body, out0, (jnp.arange(NUM_EXPERTS), w_up, w_down))
            return out.reshape(bs, slen, dim)
        key = jax.random.key(seed)
        k0, k1, k2, k3 = jax.random.split(key, 4)
        x = jax.random.normal(k0, (BS, SLEN, DIM), dtype=jnp.float32)
        gate_w = jax.random.normal(k1, (NUM_EXPERTS, DIM), dtype=jnp.float32) * 0.02
        w_up = jax.random.normal(k2, (NUM_EXPERTS, HIDDEN, DIM), dtype=jnp.float32) * 0.02
        w_down = jax.random.normal(k3, (NUM_EXPERTS, DIM, HIDDEN), dtype=jnp.float32) * 0.02
        expert_bias = jnp.zeros((NUM_EXPERTS,), dtype=jnp.float32)
        return {'x': x, 'gate_w': gate_w, 'w_up': w_up, 'w_down': w_down, 'expert_bias': expert_bias}
    _L0_ffn_all = _L0_ffn_setup()
    _L0_ffn_in = {k: v for k, v in _L0_ffn_all.items() if k in ('gate_w', 'w_up', 'w_down', 'expert_bias')}
    del _L0_ffn_all

    def _L1_xattn_setup():
        import jax, jax.numpy as jnp
        import numpy as np
        N_HEAD = 16
        key = jax.random.key(seed)
        ks = jax.random.split(key, 8)
        B, S, D = (2, 512, 256)
        s = 1.0 / np.sqrt(D)
        return {'Q': jax.random.normal(ks[0], (B, S, D), jnp.float32), 'K': jax.random.normal(ks[1], (B, S, D), jnp.float32), 'V': jax.random.normal(ks[2], (B, S, D), jnp.float32), 'Wq': jax.random.normal(ks[3], (D, D), jnp.float32) * s, 'bq': jnp.zeros((D,), jnp.float32), 'Wk': jax.random.normal(ks[4], (D, D), jnp.float32) * s, 'bk': jnp.zeros((D,), jnp.float32), 'Wv': jax.random.normal(ks[5], (D, D), jnp.float32) * s, 'bv': jnp.zeros((D,), jnp.float32), 'Wo': jax.random.normal(ks[6], (D, D), jnp.float32) * s, 'bo': jnp.zeros((D,), jnp.float32)}
    _L1_xattn_all = _L1_xattn_setup()
    _L1_xattn_in = {k: v for k, v in _L1_xattn_all.items() if k in ('Wq', 'bq', 'Wk', 'bk', 'Wv', 'bv', 'Wo', 'bo')}
    del _L1_xattn_all

    def _L1_ffn_setup():
        import jax, jax.numpy as jnp
        import numpy as np
        D = 256
        H = 1024
        E = 12
        K = 3
        B, S = (1, 512)
        key = jax.random.key(seed)
        ks = jax.random.split(key, 6)
        scale = 0.02
        x = jax.random.normal(ks[0], (B, S, D), dtype=jnp.float32)
        Wg = jax.random.normal(ks[1], (D, E), dtype=jnp.float32) * scale
        Wup = jax.random.normal(ks[2], (E, D, H), dtype=jnp.float32) * scale
        bup = jax.random.normal(ks[3], (E, H), dtype=jnp.float32) * scale
        Wdown = jax.random.normal(ks[4], (E, H, D), dtype=jnp.float32) * scale
        bdown = jax.random.normal(ks[5], (E, D), dtype=jnp.float32) * scale
        return {'x': x, 'Wg': Wg, 'Wup': Wup, 'bup': bup, 'Wdown': Wdown, 'bdown': bdown}
    _L1_ffn_all = _L1_ffn_setup()
    _L1_ffn_in = {k: v for k, v in _L1_ffn_all.items() if k in ('Wg', 'Wup', 'bup', 'Wdown', 'bdown')}
    del _L1_ffn_all
    return {'x': x, 'ctx_1024': ctx_1024, 'L0_xattn_Wq': _L0_xattn_in['Wq'], 'L0_xattn_bq': _L0_xattn_in['bq'], 'L0_xattn_Wk': _L0_xattn_in['Wk'], 'L0_xattn_bk': _L0_xattn_in['bk'], 'L0_xattn_Wv': _L0_xattn_in['Wv'], 'L0_xattn_bv': _L0_xattn_in['bv'], 'L0_xattn_Wc': _L0_xattn_in['Wc'], 'L0_xattn_bc': _L0_xattn_in['bc'], 'L0_xattn_Wo': _L0_xattn_in['Wo'], 'L0_xattn_bo': _L0_xattn_in['bo'], 'L0_ffn_gate_w': _L0_ffn_in['gate_w'], 'L0_ffn_w_up': _L0_ffn_in['w_up'], 'L0_ffn_w_down': _L0_ffn_in['w_down'], 'L0_ffn_expert_bias': _L0_ffn_in['expert_bias'], 'L1_xattn_Wq': _L1_xattn_in['Wq'], 'L1_xattn_bq': _L1_xattn_in['bq'], 'L1_xattn_Wk': _L1_xattn_in['Wk'], 'L1_xattn_bk': _L1_xattn_in['bk'], 'L1_xattn_Wv': _L1_xattn_in['Wv'], 'L1_xattn_bv': _L1_xattn_in['bv'], 'L1_xattn_Wo': _L1_xattn_in['Wo'], 'L1_xattn_bo': _L1_xattn_in['bo'], 'L1_ffn_Wg': _L1_ffn_in['Wg'], 'L1_ffn_Wup': _L1_ffn_in['Wup'], 'L1_ffn_bup': _L1_ffn_in['bup'], 'L1_ffn_Wdown': _L1_ffn_in['Wdown'], 'L1_ffn_bdown': _L1_ffn_in['bdown']}

def reference(x, ctx_1024, L0_xattn_Wq, L0_xattn_bq, L0_xattn_Wk, L0_xattn_bk, L0_xattn_Wv, L0_xattn_bv, L0_xattn_Wc, L0_xattn_bc, L0_xattn_Wo, L0_xattn_bo, L0_ffn_gate_w, L0_ffn_w_up, L0_ffn_w_down, L0_ffn_expert_bias, L1_xattn_Wq, L1_xattn_bq, L1_xattn_Wk, L1_xattn_bk, L1_xattn_Wv, L1_xattn_bv, L1_xattn_Wo, L1_xattn_bo, L1_ffn_Wg, L1_ffn_Wup, L1_ffn_bup, L1_ffn_Wdown, L1_ffn_bdown):
    import jax
    import jax.numpy as jnp

    def _L0_xattn_ref(query, key, value, Wq, bq, Wk, bk, Wv, bv, Wc, bc, Wo, bo):
        import jax, jax.numpy as jnp
        import numpy as np
        N_HEADS = 16
        D_MODEL = 256
        HEAD_DIM = D_MODEL // N_HEADS
        B, S = (4, 512)
        q = query @ Wq + bq
        k = key @ Wk + bk
        v = value @ Wv + bv
        scores = jnp.einsum('bqd,bkd->bqk', q, k) / jnp.sqrt(jnp.asarray(HEAD_DIM, q.dtype))
        attn = jax.nn.softmax(scores, axis=-1)
        ctx = jnp.einsum('bqk,bkd->bqd', attn, v)
        cat = jnp.tile(ctx, (1, 1, N_HEADS))
        out = cat @ Wc + bc
        out = out @ Wo + bo
        return out

    def _L0_ffn_ref(x, gate_w, w_up, w_down, expert_bias):
        import jax, jax.numpy as jnp
        import numpy as np
        DIM = 256
        NUM_EXPERTS = 8
        TOP_K = 2
        HIDDEN = 4 * DIM // TOP_K
        BS, SLEN = (1, 512)

        def _moe(x, gate_w, w_up, w_down, expert_bias):
            bs, slen, dim = x.shape
            xf = x.reshape(-1, dim)
            scores = jax.nn.sigmoid(xf @ gate_w.T)
            biased = scores + expert_bias
            _, sel = jax.lax.top_k(biased, TOP_K)
            top_scores = jnp.take_along_axis(scores, sel, axis=-1)

            def body(acc, ew):
                e, wu, wd = ew
                w_t = jnp.sum(jnp.where(sel == e, top_scores, 0.0), axis=-1)
                xe = xf * w_t[:, None]
                h = jnp.square(jax.nn.relu(xe @ wu.T))
                return (acc + h @ wd.T, None)
            out0 = jnp.zeros_like(xf)
            out, _ = jax.lax.scan(body, out0, (jnp.arange(NUM_EXPERTS), w_up, w_down))
            return out.reshape(bs, slen, dim)
        return _moe(x, gate_w, w_up, w_down, expert_bias)

    def _L1_xattn_ref(Q, K, V, Wq, bq, Wk, bk, Wv, bv, Wo, bo):
        import jax, jax.numpy as jnp
        import numpy as np
        N_HEAD = 16
        B, S, D = Q.shape
        H = N_HEAD
        dh = D // H
        scale = dh ** 0.25

        def proj(x, W, b):
            return (x @ W + b).reshape(B, S, H, dh).transpose(0, 2, 1, 3)
        q = proj(Q, Wq, bq) / scale
        k = proj(K, Wk, bk) / scale
        v = proj(V, Wv, bv)
        scores = jnp.einsum('bhqd,bhkd->bhqk', q, k)
        i = jnp.arange(S)[:, None]
        j = jnp.arange(S)[None, :]
        scores = jnp.where(j <= i, scores, -jnp.inf)
        attn = jax.nn.softmax(scores, axis=-1)
        out = jnp.einsum('bhqk,bhkd->bhqd', attn, v)
        out = out.transpose(0, 2, 1, 3).reshape(B, S, D)
        return out @ Wo + bo

    def _L1_ffn_ref(x, Wg, Wup, bup, Wdown, bdown):
        import jax, jax.numpy as jnp
        import numpy as np
        D = 256
        H = 1024
        E = 12
        K = 3
        B, S = (1, 512)
        gate_logits = jnp.einsum('bsd,de->bse', x, Wg)
        topw, sel = jax.lax.top_k(gate_logits, K)
        topw = jax.nn.softmax(topw.astype(jnp.float32), axis=-1).astype(x.dtype)
        cw = jnp.einsum('bsk,bske->bse', topw, jax.nn.one_hot(sel, E, dtype=x.dtype))
        h = jax.nn.gelu(jnp.einsum('bsd,edh->ebsh', x, Wup) + bup[:, None, None, :], approximate=False)
        y = jnp.einsum('ebsh,ehd->ebsd', h, Wdown) + bdown[:, None, None, :]
        return jnp.einsum('bse,ebsd->bsd', cw, y)
    x = x + _L0_xattn_ref(_layernorm(x, axis=-1), ctx_1024, ctx_1024, L0_xattn_Wq, L0_xattn_bq, L0_xattn_Wk, L0_xattn_bk, L0_xattn_Wv, L0_xattn_bv, L0_xattn_Wc, L0_xattn_bc, L0_xattn_Wo, L0_xattn_bo)
    x = x + _L0_ffn_ref(_layernorm(x, axis=-1), L0_ffn_gate_w, L0_ffn_w_up, L0_ffn_w_down, L0_ffn_expert_bias)
    x = x + _L1_xattn_ref(_layernorm(x, axis=-1), ctx_1024, ctx_1024, L1_xattn_Wq, L1_xattn_bq, L1_xattn_Wk, L1_xattn_bk, L1_xattn_Wv, L1_xattn_bv, L1_xattn_Wo, L1_xattn_bo)
    x = x + _L1_ffn_ref(_layernorm(x, axis=-1), L1_ffn_Wg, L1_ffn_Wup, L1_ffn_bup, L1_ffn_Wdown, L1_ffn_bdown)
    return x

_drawn_inputs = setup_inputs


def setup_inputs(seed=0):
    import zlib

    import numpy as np

    out = dict(_drawn_inputs(seed))
    spreads = {'L0_xattn_bq': (0.0, 0.8),
     'L0_xattn_bk': (0.0, 0.8),
     'L0_xattn_bv': (0.0, 0.671),
     'L0_xattn_bc': (0.0, 0.28),
     'L0_xattn_bo': (0.0, 0.1),
     'L0_ffn_expert_bias': (0.0, 0.338),
     'L1_xattn_bq': (0.0, 0.365),
     'L1_xattn_bk': (0.0, 0.8),
     'L1_xattn_bv': (0.0, 0.1),
     'L1_xattn_bo': (0.0, 0.1)}
    factors = {'L0_xattn_Wq': 8.0,
     'L0_xattn_Wk': 8.0,
     'L0_xattn_Wv': 4.242,
     'L0_xattn_Wc': 3.597,
     'L0_ffn_gate_w': 3.303,
     'L1_ffn_bup': 8.0,
     'L1_ffn_bdown': 5.622}
    for name, (base, spread) in spreads.items():
        noise = np.random.default_rng([zlib.crc32(name.encode()), seed]).standard_normal(out[name].shape)
        drawn = base * np.exp(spread * noise) if base else spread * noise
        out[name] = jnp.asarray(drawn.astype(out[name].dtype))
    for name, factor in factors.items():
        out[name] = (out[name] * factor).astype(out[name].dtype)
    return out
```

```python
from contextlib import ExitStack

import numpy as np

import concourse.bass as bass
from concourse import mybir

F32 = mybir.dt.float32
F32R = mybir.dt.float32r
BF16 = mybir.dt.bfloat16
I32 = mybir.dt.int32
U32 = mybir.dt.uint32
ALU = mybir.AluOpType
ACT = mybir.ActivationFunctionType
AX = mybir.AxisListType

P = 128
B, S, D = 4, 512, 256
NT = B * S // P
TB = S // P
KC = D // P
NH = 16
DH = D // NH
HG = 4
SLOTW = 32
EPS = 1e-5
BT = 256
E0, K0, H0 = 8, 2, 512
E1, K1, H1 = 12, 3, 1024
NB0 = (B * S * K0 // BT + E0 - 1 + 1) // 2 * 2
NB1 = (B * S * K1 // BT + E1 - 1 + 1) // 2 * 2

C_ID, C_TRI, C_ONE, C_CAUSAL, C_HEAD, C_FOLD, C_IE, C_IB, C_SEL, C_END = np.cumsum(
    [0, P, P, P, P, 8, DH, E1, NB1, DH + 1]).tolist()


def constants():
    c = np.zeros((P, C_END), np.float32)
    p = np.arange(P)
    c[:, C_ID:C_TRI] = np.eye(P)
    c[:, C_TRI:C_ONE] = p[:, None] < p[None, :]
    c[:, C_ONE:C_CAUSAL] = 1.0
    c[:, C_CAUSAL:C_HEAD] = np.where(p[None, :] <= p[:, None], 0.0, -1e30)
    c[:, C_HEAD:C_FOLD] = p[:, None] // DH == np.arange(8)[None, :]
    c[:, C_FOLD:C_IE] = p[:, None] % DH == np.arange(DH)[None, :]
    c[:, C_IE:C_IB] = np.arange(E1)[None, :]
    c[:, C_IB:C_SEL] = np.arange(NB1)[None, :]
    c[:, C_SEL:C_END] = np.arange(DH + 1)[None, :] == DH
    return c


class Chain:

    def __init__(self, engine, sem):
        self.engine, self.sem, self.base, self.turn, self.per, self.n = engine, sem, 0, 0, 0, 0

    def enter(self, turn, per):
        self.base, self.turn, self.per, self.n = self.base + self.n, turn, per, 0

    def leave(self, turns):
        assert self.n == self.per, (self.n, self.per)
        self.base, self.turn, self.per, self.n = self.base + turns * self.per, 0, 0, 0

    def link(self, ins):
        self.n += 1
        ins.then_inc(self.sem, 1)
        self.engine.wait_ge(self.sem, self.turn * self.per + (self.base + self.n))


STOP = 9


def build(nc, A, out):
    with ExitStack() as ctx:
        def sb(name, shape, dt=F32):
            return ctx.enter_context(nc.sbuf_tensor(name, shape, dt))

        def sem(name):
            return ctx.enter_context(nc.semaphore(name))

        bank = [ctx.enter_context(nc.psum_tensor(f"bank{i}", [P, 512], F32)) for i in range(8)]
        sorted_x = nc.dram_tensor("sorted_x", (NB1 * BT, D), F32, kind="Internal").ap()
        sorted_y = nc.dram_tensor("sorted_y", (NB1 * BT, D), F32, kind="Internal").ap()

        con = sb("con", [P, C_END])
        ident = con[:, C_ID:C_TRI]
        before = con[:, C_TRI:C_ONE]
        ones = con[:, C_ONE:C_CAUSAL]
        headmask = con[:, C_HEAD:C_FOLD]
        fold = con[:, C_FOLD:C_IE]
        ident_b = sb("ident_b", [P, P], BF16)
        causal_b = sb("causal_b", [P, P], BF16)
        eps = sb("eps", [P, 1])
        zeros = sb("zeros", [P, 1024])
        wq0, wk0, wv0 = sb("wq0", [P, KC, DH]), sb("wk0", [P, KC, DH]), sb("wv0", [P, KC, DH])
        wc0, wo0 = sb("wc0", [P, KC, D]), sb("wo0", [P, KC, D])
        bq0, bk0 = sb("bq0", [DH, 1]), sb("bk0", [DH, 1])
        bv0 = sb("bv0", [P, DH])
        bo0 = sb("bo0", [1, D])
        wcT = sb("wcT", [P, KC, DH + 1])
        weff = sb("weff", [DH + 1, D])
        gw0 = sb("gw0", [P, KC, E0])
        eb0 = sb("eb0", [P, E0])
        wq1, wk1, wv1, wo1 = (sb(n, [P, KC, D]) for n in ("wq1", "wk1", "wv1", "wo1"))
        bq1, bk1 = sb("bq1", [P, KC]), sb("bk1", [P, KC])
        bv1, bo1 = sb("bv1", [P, D]), sb("bo1", [P, D])
        gw1 = sb("gw1", [P, KC, E1])

        x = sb("x", [P, NT, D])
        xn = sb("xn", [P, NT, D])
        stats = sb("stats", [P, TB, 6])
        mv = sb("mv", [P, TB, 2])
        std = sb("std", [P, TB])
        rstd = sb("rstd", [P, TB])
        negmax = sb("negmax", [P, 2, TB])
        rowsum = sb("rowsum", [P, TB])
        rinv = sb("rinv", [P, TB])

        logits = sb("logits", [P, NT, E1])
        keys = sb("keys", [P, NT, E1])
        top8 = sb("top8", [P, NT, 8])
        idx8 = sb("idx8", [P, NT, 8], U32)
        idxf = sb("idxf", [P, NT, 8])
        hot = [sb(f"hot{k}", [P, NT, E1]) for k in range(K1)]
        sel = sb("sel", [P, NT, E1])
        slot = sb("slot", [P, NT, E1])
        runs = sb("runs", [P, NT + 1, E1])
        work = sb("work", [P, NT, E1])
        wtop = sb("wtop", [P, K1, NT])
        wsum = sb("wsum", [P, NT])
        slotf = sb("slotf", [P, K1, NT])
        sloti = sb("sloti", [P, K1, NT], I32)
        nblk = sb("nblk", [P, E1])
        nblki = sb("nblki", [P, E1], I32)
        upto = sb("upto", [P, E1])
        past = sb("past", [1, NB1, E1])
        owner = sb("owner", [1, NB1])
        owneri = sb("owneri", [1, NB1], I32)

        with ExitStack() as scope:
            def ab(name, shape, dt=F32):
                return scope.enter_context(nc.sbuf_tensor(name, shape, dt))

            regA = ab("regA", [P, 16 * S])
            kz = regA[:, :].rearrange("p (h k) -> p h k", h=NH)
            qT0, kT0 = regA[0:DH, 0:512], regA[0:DH, 512:1024]
            v0 = regA[:, 1024:1024 + TB * 17].rearrange("p (k d) -> p k d", k=TB)
            p0 = regA[:, 2048:4096].rearrange("p (q k) -> p q k", q=TB)
            pT0 = regA[:, 4096:6144].rearrange("p (k q) -> p k q", k=TB)
            oT0 = regA[0:DH + 1, 6144:6656]
            xw = [regA[:, 0:4096].rearrange("p (t d) -> p t d", t=NT),
                  regA[:, 4096:8192].rearrange("p (t d) -> p t d", t=NT)]
            PW = S * (TB + 1) // 2
            pT1 = ab("pT1", [P, 8, PW])
            gat = pT1[:, :, :].rearrange("p s w -> p (s w)")[:, 0:4 * K1 * D].rearrange("p (r k d) -> p r k d", r=4, k=K1)
            p1 = ab("p1", [P, 2, PW])
            qT1, kT1 = ab("qT1", [P, KC, S]), ab("kT1", [P, KC, S])
            v1 = ab("v1", [P, TB, NH, SLOTW])
            oTs = ab("oTs", [P, S])
            o1 = ab("o1", [P, TB, D])
            oT1 = ab("oT1", [P, KC, S])
            orec = ab("orec", [P, TB, HG])
            ctxT = ab("ctxT", [P, KC, S])
            xnb = ab("xnb", [P, TB, D])
            xnT = ab("xnT", [P, KC, S])

        with ExitStack() as scope:
            def mb(name, shape, dt=F32):
                return scope.enter_context(nc.sbuf_tensor(name, shape, dt))

            xT = [mb(f"xT{i}", [P, 2, 512], F32R) for i in range(2)]
            hid = [mb(f"hid{i}", [P, 2, 2048], F32R) for i in range(2)]
            hraw = [mb(f"hraw{i}", [P, 512]) for i in range(2)]
            xsc = [mb(f"xsc{i}", [P, 512]) for i in range(2)]
            ysb = [mb(f"ysb{i}", [P, 512]) for i in range(2)]
            bup = [mb(f"bup{i}", [P, H1 // P]) for i in range(2)]
            bdn = [mb(f"bdn{i}", [P, D]) for i in range(2)]
            wraw = [mb("wraw_up", [P, 2048]), mb("wraw_down", [P, 2048])]
            wup = [mb(f"wup{i}", [P, 2, 2048], F32R) for i in range(2)]
            wdn = [mb(f"wdn{i}", [P, 2, 2048], F32R) for i in range(2)]

        weights_in = sem("weights_in")
        ctx_in = sem("ctx_in")
        dve_step = sem("dve_step")
        setup_done = sem("setup_done")
        dve_turn, sp_turn = sem("dve_turn"), sem("sp_turn")
        zeroed = sem("zeroed")
        fold_psum, fold_ready = sem("fold_psum"), sem("fold_ready")
        var_ready, std_ready, xn_ready = sem("var_ready"), sem("std_ready"), sem("xn_ready")
        xt_psum, xnT_ready = sem("xt_psum"), sem("xnT_ready")
        kv_psum, q_psum = sem("kv_psum"), sem("q_psum")
        qk_ready, v_ready = sem("qk_ready"), sem("v_ready")
        scores0, negmax0, probs0 = sem("scores0"), sem("negmax0"), sem("probs0")
        pt0_psum, pt0_act, pt0_dve = sem("pt0_psum"), sem("pt0_act"), sem("pt0_dve")
        o0_psum, o0_ready, attn0 = sem("o0_psum"), sem("o0_ready"), sem("attn0")
        logits_psum, logits_ready = sem("logits_psum"), sem("logits_ready")
        kv1_psum, q1_psum, k1_ready, q1_ready, v1_ready, kz_ready = (
            sem(n) for n in ("kv1_psum", "q1_psum", "k1_ready", "q1_ready", "v1_ready", "kz_ready"))
        scores1, negmax1, probs1 = sem("scores1"), sem("negmax1"), sem("probs1")
        pt1_psum, pt1_act, pt1_dve = sem("pt1_psum"), sem("pt1_act"), sem("pt1_dve")
        ot_psum, ot_taken, o_psum, o_taken = (sem(n) for n in ("ot_psum", "ot_taken", "o_psum", "o_taken"))
        on_psum, on_ready, attn1 = sem("on_psum"), sem("on_ready"), sem("attn1")
        v1_cleared = sem("v1_cleared")
        out_done, out_stored = sem("out_done"), sem("out_stored")
        route = []
        moe = []
        for i in range(2):
            route.append({n: sem(f"{n}_{i}") for n in (
                "gate_ready", "sel_ready", "rank_psum", "slots_ready", "owner_ready", "scattered",
                "exp_in", "exp_ready", "gathered0", "gathered1", "gathered2", "gathered3", "combined")})
            moe.append({n: sem(f"{n}_{i}") for n in (
                "up_in", "down_in", "x_even", "x_odd", "bias_even", "bias_odd", "dbias_even", "dbias_odd",
                "xt_psum", "x_high", "xT_ready", "up_high", "up_ready", "down_high", "down_ready",
                "up_psum", "relu_ready", "h_raw", "h_ready", "y_psum",
                "y_ready", "store_even", "store_odd")})

        block = ctx.enter_context(nc.Block())
        x_in = A["x"].rearrange("b (t p) d -> p (b t) d", p=P)
        out_v = out.rearrange("b (t p) d -> p (b t) d", p=P)

        def row(ap, n, parts=P):
            return ap.rearrange("(a n) -> a n", a=1).broadcast_to((parts, n)) if parts > 1 else ap.rearrange("(a n) -> a n", a=1)

        loads = [
            (con[:, :], A["con"]),
            (x[:, :, :], x_in),
            (wq0[:, :, :], A["L0_xattn_Wq"].rearrange("(c p) n -> p c n", p=P)),
            (wk0[:, :, :], A["L0_xattn_Wk"].rearrange("(c p) n -> p c n", p=P)),
            (wv0[:, :, :], A["L0_xattn_Wv"].rearrange("(c p) n -> p c n", p=P)),
            (wc0[:, :, :], A["L0_xattn_Wc"].rearrange("(c p) n -> p c n", p=P)),
            (wo0[:, :, :], A["L0_xattn_Wo"].rearrange("(c p) n -> p c n", p=P)),
            (bq0[:, :], A["L0_xattn_bq"].rearrange("(p a) -> p a", a=1)),
            (bk0[:, :], A["L0_xattn_bk"].rearrange("(p a) -> p a", a=1)),
            (bv0[:, :], row(A["L0_xattn_bv"], DH)),
            (bo0[:, :], row(A["L0_xattn_bo"], D, 1)),
            (wcT[:, 0, DH:DH + 1], A["L0_xattn_bc"][0:P].rearrange("(p a) -> p a", a=1)),
            (wcT[:, 1, DH:DH + 1], A["L0_xattn_bc"][P:D].rearrange("(p a) -> p a", a=1)),
            (gw0[:, :, :], A["gate0T"].rearrange("(c p) n -> p c n", p=P)),
            (eb0[:, :], row(A["L0_ffn_expert_bias"], E0)),
            (wq1[:, :, :], A["L1_xattn_Wq"].rearrange("(c p) n -> p c n", p=P)),
            (wk1[:, :, :], A["L1_xattn_Wk"].rearrange("(c p) n -> p c n", p=P)),
            (wv1[:, :, :], A["L1_xattn_Wv"].rearrange("(c p) n -> p c n", p=P)),
            (wo1[:, :, :], A["L1_xattn_Wo"].rearrange("(c p) n -> p c n", p=P)),
            (bq1[:, :], A["bq1T"]),
            (bk1[:, :], A["bk1T"]),
            (bv1[:, :], row(A["L1_xattn_bv"], D)),
            (bo1[:, :], row(A["L1_xattn_bo"], D)),
            (gw1[:, :, :], A["L1_ffn_Wg"].rearrange("(c p) n -> p c n", p=P)),
        ]

        LAYERS = [dict(E=E0, K=K0, H=H0, NB=NB0, up=A["up0"], dn=A["dn0"]),
                  dict(E=E1, K=K1, H=H1, NB=NB1, up=A["up1"], dn=A["L1_ffn_Wdown"])]

        @block.sync
        def _(sp):
            for dst, src in loads:
                sp.dma_start(dst, src).then_inc(weights_in, 16)

            def ctx_load(b, layer):
                sp.dma_start(ctxT[:, :, :], A["ctxT"].rearrange("(c p) n -> p c n", p=P)[:, :, bass.ts(b, S)]).then_inc(ctx_in, 16)

            ctx_load(0, 0)
            with sp.Fori(1, B) as b:
                sp.wait_ge(v_ready, b)
                sp.sem_inc(sp_turn, 1)
                sp.wait_ge(qk_ready, 2 * b)
                sp.sem_inc(sp_turn, 1)
                ctx_load(b, 0)

            def expert_loads(i):
                L, M, R = LAYERS[i], moe[i], route[i]
                HT, NB = L["H"] // P, L["NB"]
                CH = HT // 2
                NW = KC * L["H"]

                def hold(s, value):
                    sp.wait_ge(s, value)
                    sp.sem_inc(sp_turn, 1)

                def expert(j):
                    return sp.value_load(owneri[0:1, bass.ds(j, 1)], min_val=0, max_val=L["E"] - 1)

                def load_up(j, par):
                    first = isinstance(j, int)
                    e = expert(j)
                    if not first or j >= 1:
                        hold(M["up_ready"], 2 * j)
                    sp.dma_start(wraw[0][:, 0:NW].rearrange("p (c n) -> p c n", c=KC),
                                 L["up"][bass.ds(e, 1)].rearrange("a (c p) n -> p (a c) n", p=P)).then_inc(M["up_in"], 16)
                    if first and j == 0:
                        sp.wait_ge(R["scattered"], 16 * NT * L["K"])
                    if not first or j >= 2:
                        hold(M["xt_psum"], j + (-1))
                    sp.dma_start(xsc[par][:, :].rearrange("p (i d) -> p i d", i=2),
                                 sorted_x[bass.ts(j, BT), :].rearrange("(i p) d -> p i d", p=P)).then_inc(M[("x_even", "x_odd")[par]], 16)
                    if i == 1:
                        hold(M["h_raw"], j * CH if (not first or j) else CH)
                        sp.dma_start(bup[par][:, :], A["bup1T"][bass.ds(e, 1)].rearrange("a p n -> p (a n)")).then_inc(M[("bias_even", "bias_odd")[par]], 16)

                def load_down(j, par):
                    e = expert(j)
                    if not isinstance(j, int) or j >= 1:
                        hold(M["down_ready"], 2 * j)
                    sp.dma_start(wraw[1][:, 0:NW].rearrange("p (c n) -> p c n", c=HT),
                                 L["dn"][bass.ds(e, 1)].rearrange("a (c p) n -> p (a c) n", p=P)).then_inc(M["down_in"], 16)
                    return e

                def load_bias(j, par, e):
                    hold(M["y_ready"], j + 1)
                    if i == 1:
                        sp.dma_start(bdn[par][:, :], A["L1_ffn_bdown"][bass.ds(e, 1)].broadcast_to((P, D))).then_inc(M[("dbias_even", "dbias_odd")[par]], 16)

                def store(j, par):
                    sp.dma_start(sorted_y[bass.ts(j, BT), :].rearrange("(i p) d -> p i d", p=P),
                                 ysb[par][:, :].rearrange("p (i d) -> p i d", i=2)).then_inc(M[("store_even", "store_odd")[par]], 16)

                sp.sem_inc(M["store_even"], 16)
                sp.sem_inc(M["store_odd"], 16)
                sp.wait_ge(R["owner_ready"], 1)
                load_up(0, 0)
                load_bias(0, 0, load_down(0, 0))
                load_up(1, 1)
                load_bias(1, 1, load_down(1, 1))
                load_up(2, 0)

                def step(s, par, last=False):
                    e = load_down(s + 2, par)
                    if not last:
                        load_up(s + 3, 1 - par)
                    load_bias(s + 2, par, e)
                    store(s, par)

                with sp.Fori(0, (NB - 4) // 2) as t:
                    step(2 * t, 0)
                    step(2 * t + 1, 1)
                step(NB - 4, 0)
                step(NB - 3, 1, last=True)
                sp.wait_ge(M["y_ready"], NB + 1)
                store(NB - 2, 0)
                sp.wait_ge(M["y_ready"], NB + 2)
                store(NB - 1, 1)

            if STOP >= 2:
                expert_loads(0)
            if STOP >= 3:
                sp.wait_ge(route[0]["combined"], 1)
                ctx_load(0, 1)
                with sp.Fori(1, B) as b:
                    sp.wait_ge(k1_ready, 2 * b)
                    sp.sem_inc(sp_turn, 1)
                    sp.wait_ge(v1_ready, 2 * b)
                    sp.sem_inc(sp_turn, 1)
                    ctx_load(b, 1)
            if STOP >= 4:
                expert_loads(1)

        @block.tensor
        def _(pe):
            def ln_transposes(n, b, src, lo):
                pe.wait_ge(xn_ready, n + 1)
                for c in range(KC):
                    for t in range(TB):
                        last = pe.transpose(bank[lo + c][:, t * P:(t + 1) * P], src(t, c), ident)
                    last.then_inc(xt_psum, 1)
                pe.wait_ge(xnT_ready, 2 * n + 2)

            def gate(n, gw, E, bk):
                for t in range(TB):
                    for c in range(KC):
                        last = pe.matmul(bank[bk][:, t * E:(t + 1) * E], xnT[:, c, t * P:(t + 1) * P], gw[:, c, :],
                                         start=(c == 0), stop=(c == KC - 1))
                last.then_inc(logits_psum, 1)

            pe.wait_ge(weights_in, 16 * len(loads))
            pe.wait_ge(setup_done, 1)
            for n in range(KC):
                for c in range(KC):
                    last = pe.matmul(bank[n][:, 0:DH], wc0[:, c, n * P:(n + 1) * P], fold, start=(c == 0), stop=(c == KC - 1))
            last.then_inc(fold_psum, 1)
            pe.wait_ge(fold_ready, 1)
            for c in range(KC):
                pe.matmul(bank[2][0:DH + 1, 0:D], wcT[:, c, :], wo0[:, c, :], start=(c == 0), stop=False)
            pe.matmul(bank[2][0:DH + 1, 0:D], con[0:1, C_SEL:C_END], bo0[:, :], start=False, stop=True).then_inc(fold_psum, 1)
            pe.wait_ge(fold_ready, 2)

            with pe.Fori(0, B) as b:
                pe.wait_ge(ctx_in, b * 16 + 16)
                for c in range(KC):
                    last = pe.matmul(bank[1][0:DH, :], wk0[:, c, :], ctxT[:, c, :], start=(c == 0), stop=(c == KC - 1))
                last.then_inc(kv_psum, 1)
                for k in range(TB):
                    for c in range(KC):
                        last = pe.matmul(bank[2][:, k * DH:(k + 1) * DH], ctxT[:, c, k * P:(k + 1) * P], wv0[:, c, :],
                                         start=(c == 0), stop=(c == KC - 1))
                last.then_inc(kv_psum, 1)
                ln_transposes(2 * b, b, lambda t, c: xnb[:, t, c * P:(c + 1) * P], 6)
                for c in range(KC):
                    last = pe.matmul(bank[0][0:DH, :], wq0[:, c, :], xnT[:, c, :], start=(c == 0), stop=(c == KC - 1))
                last.then_inc(q_psum, 1)
                pe.wait_ge(qk_ready, 2 * b + 2)
                pe.wait_ge(v_ready, b + 1)
                for q in range(TB):
                    pe.matmul(bank[q][:, :], qT0[:, q * P:(q + 1) * P], kT0, start=True, stop=True).then_inc(scores0, 1)
                for q in range(TB):
                    pe.wait_ge(probs0, 4 * b + q + 1)
                    for k in range(TB):
                        last = pe.transpose(bank[4 + k][:, q * P:(q + 1) * P], p0[:, q, k * P:(k + 1) * P], ident)
                last.then_inc(pt0_psum, 1)
                pe.wait_ge(pt0_act, 2 * b + 2)
                pe.wait_ge(pt0_dve, 2 * b + 2)
                for k in range(TB):
                    last = pe.matmul(bank[0][0:DH + 1, :], v0[:, k, :], pT0[:, k, :], start=(k == 0), stop=(k == TB - 1))
                last.then_inc(o0_psum, 1)
                pe.wait_ge(o0_ready, b + 1)
                for q in range(TB):
                    last = pe.matmul(bank[1 + q // 2][:, (q % 2) * D:(q % 2 + 1) * D], oT0[:, q * P:(q + 1) * P], weff[:, :],
                                     start=True, stop=True)
                    if q % 2:
                        last.then_inc(attn0, 1)
                ln_transposes(2 * b + 1, b, lambda t, c: xnb[:, t, c * P:(c + 1) * P], 6)
                gate(b, gw0, E0, 3)

            def ranks(i):
                L, R = LAYERS[i], route[i]
                pe.wait_ge(R["sel_ready"], 1)
                n = NT * L["E"]
                s = sel[:, :, :].rearrange("p t e -> p (t e)")[:, 0:n]
                pe.matmul(bank[0][:, 0:n], before, s, start=True, stop=True)
                pe.matmul(bank[1][:, 0:n], ones, s, start=True, stop=True).then_inc(R["rank_psum"], 1)

            def experts(i):
                L, M, R = LAYERS[i], moe[i], route[i]
                HT, NB = L["H"] // P, L["NB"]
                CH = HT // 2
                PARTS = ((0, 0), (0, 1), (1, 0))
                pe.nop().then_inc(M["y_psum"], 2)
                pe.nop().then_inc(M["up_psum"], 2 * CH)
                pe.wait_ge(R["slots_ready"], 1)

                def turn(j, n, par):
                    pe.wait_ge(M[("x_even", "x_odd")[par]], n * 16 + 16)
                    for c in range(KC):
                        for t in range(2):
                            last = pe.transpose(bank[0][:, c * BT + t * P:c * BT + (t + 1) * P],
                                                xsc[par][:, t * D + c * P:t * D + (c + 1) * P], ident)
                    last.then_inc(M["xt_psum"], 1)

                def up(j, par):
                    pe.wait_ge(M["xT_ready"], j + 1)
                    pe.wait_ge(M["up_ready"], 2 * j + 2)
                    for ch in range(CH):
                        pe.wait_ge(M["h_raw"], j * CH + (ch + 1))
                        for m in range(2):
                            h = 2 * ch + m
                            for c in range(KC):
                                for w, v in PARTS:
                                    last = pe.matmul(bank[1 + ch][:, m * BT:(m + 1) * BT],
                                                     wup[par][:, w, c * L["H"] + h * P:c * L["H"] + (h + 1) * P],
                                                     xT[par][:, v, c * BT:(c + 1) * BT],
                                                     start=(c == 0 and w + v == 0), stop=(c == KC - 1 and w == 1))
                        last.then_inc(M["up_psum"], 1)

                def down(j, par):
                    pe.wait_ge(M["down_ready"], 2 * j + 2)
                    pe.wait_ge(M["h_ready"], j * CH + (CH + 2))
                    pe.wait_ge(M["y_ready"], j + 1)
                    for t in range(2):
                        for h in range(HT):
                            for v, w in PARTS:
                                last = pe.matmul(bank[5 + par][:, t * D:(t + 1) * D],
                                                 hid[par][:, v, h * BT + t * P:h * BT + (t + 1) * P],
                                                 wdn[par][:, w, h * D:(h + 1) * D],
                                                 start=(h == 0 and w + v == 0), stop=(h == HT - 1 and v == 1))
                    last.then_inc(M["y_psum"], 1)

                turn(0, 0, 0)
                up(0, 0)
                turn(1, 0, 1)
                with pe.Fori(0, NB // 2 - 1) as t:
                    up(2 * t + 1, 1)
                    turn(2 * t + 2, t + 1, 0)
                    down(2 * t, 0)
                    up(2 * t + 2, 0)
                    turn(2 * t + 3, t + 1, 1)
                    down(2 * t + 1, 1)
                up(NB - 1, 1)
                down(NB - 2, 0)
                down(NB - 1, 1)

            if STOP >= 2:
                ranks(0)
                experts(0)
            if STOP >= 3:
                pe.nop().then_inc(pt1_psum, 6)
                pe.nop().then_inc(ot_psum, 2)
                with pe.Fori(0, B) as b:
                    pe.wait_ge(ctx_in, b * 16 + 16 * (B + 1))
                    for c in range(KC):
                        for kc in range(KC):
                            last = pe.matmul(bank[5 + c][:, :], wk1[:, kc, c * P:(c + 1) * P], ctxT[:, kc, :],
                                             start=(kc == 0), stop=(kc == KC - 1))
                        last.then_inc(kv1_psum, 1)
                    for k in range(TB):
                        for kc in range(KC):
                            last = pe.matmul(bank[k // 2][:, (k % 2) * D:(k % 2 + 1) * D], ctxT[:, kc, k * P:(k + 1) * P],
                                             wv1[:, kc, :], start=(kc == 0), stop=(kc == KC - 1))
                        if k % 2:
                            last.then_inc(kv1_psum, 1)
                    ln_transposes(2 * b + 2 * B, b, lambda t, c: xnb[:, t, c * P:(c + 1) * P], 3)
                    for c in range(KC):
                        for kc in range(KC):
                            last = pe.matmul(bank[7 if c else 2][:, :], wq1[:, kc, c * P:(c + 1) * P], xnT[:, kc, :],
                                             start=(kc == 0), stop=(kc == KC - 1))
                        last.then_inc(q1_psum, 1)
                    pe.wait_ge(q1_ready, 2 * b + 2)
                    pe.wait_ge(k1_ready, 2 * b + 2)
                    pe.wait_ge(v1_ready, 2 * b + 2)

                    def scores(h):
                        c = h // 8
                        pe.wait_ge(kz_ready, b * NH + (h + 1))
                        for part, tiles in enumerate(((3,), (2,), (1, 0))):
                            pe.wait_ge(probs1, b * (3 * NH) + (3 * h + part + 1))
                            at = 0
                            for q in tiles:
                                w = (q + 1) * P
                                pe.matmul(bank[part][:, at:at + w], qT1[:, c, q * P:(q + 1) * P], kz[:, h, 0:w], start=True, stop=False)
                                last = pe.matmul(bank[part][:, at + q * P:at + w], ident_b[:, :], causal_b[:, :], start=False, stop=True)
                                at += w
                            last.then_inc(scores1, 1)

                    def turn_probs(h):
                        pe.wait_ge(probs1, b * (3 * NH) + (3 * h + 6))
                        pe.wait_ge(pt1_dve, b * NH + (h + 1))
                        for k in range(TB):
                            if k == 1:
                                pe.wait_ge(pt1_act, b * (2 * NH) + (2 * h + 2))
                            at = (k == 3) * 256
                            for q in range(k, TB):
                                src = p1[:, h % 2, QOFF[q] + k * P:QOFF[q] + (k + 1) * P]
                                last = pe.transpose(bank[3 + min(k, 2)][:, at + (q - k) * P:at + (q - k + 1) * P], src, ident)
                            if k != 2:
                                last.then_inc(pt1_psum, 1)

                    def values(g):
                        pe.wait_ge(pt1_dve, b * NH + (4 * g + 5))
                        pe.wait_ge(pt1_act, b * (2 * NH) + (8 * g + 10))
                        pe.wait_ge(ot_taken, b * 4 + (g + 1))
                        for k in range(TB):
                            for i in range(HG):
                                last = pe.matmul(bank[6][32 * i:32 * i + 32, k * P:S], v1[:, k, HG * g + i, :],
                                                 pT1[:, (g % 2) * HG + i, QOFF2[k]:QOFF2[k] + S - k * P],
                                                 start=(k == 0), stop=(k == TB - 1))
                        last.then_inc(ot_psum, 1)

                    def turn_out(g):
                        pe.wait_ge(ot_taken, b * 4 + (g + 2))
                        pe.wait_ge(o_taken, b * 4 + (g + 1))
                        for q in range(TB):
                            last = pe.transpose(bank[7][:, q * P:(q + 1) * P], oTs[:, q * P:(q + 1) * P], ident)
                        last.then_inc(o_psum, 1)

                    QOFF = {3: 0, 2: 512, 1: 896, 0: 1152}
                    QOFF2 = {0: 0, 1: 512, 2: 896, 3: 1152}
                    scores(0)
                    for h in range(NH):
                        if h < NH - 1:
                            scores(h + 1)
                        turn_probs(h)
                        if h % HG == 0 and h:
                            values(h // HG - 1)
                        if h % HG == 1 and h > 1:
                            turn_out(h // HG - 1)
                    values(3)
                    turn_out(3)
                    pe.wait_ge(o_taken, b * 4 + 5)
                    for c in range(KC):
                        for q in range(TB):
                            last = pe.transpose(bank[3 + c][:, q * P:(q + 1) * P], o1[:, q, c * P:(c + 1) * P], ident)
                        last.then_inc(on_psum, 1)
                    pe.wait_ge(on_ready, 2 * b + 2)
                    for q in range(TB):
                        for c in range(KC):
                            last = pe.matmul(bank[5 + q // 2][:, (q % 2) * D:(q % 2 + 1) * D], oT1[:, c, q * P:(q + 1) * P],
                                             wo1[:, c, :], start=(c == 0), stop=(c == KC - 1))
                        if q % 2:
                            last.then_inc(attn1, 1)
                    ln_transposes(2 * b + (2 * B + 1), b, lambda t, c: xnb[:, t, c * P:(c + 1) * P], 3)
                    gate(b, gw1, E1, 7)
            if STOP >= 4:
                ranks(1)
                experts(1)

        @block.scalar
        def _(act):
            def ln_std(n):
                act.wait_ge(var_ready, n + 1)
                act.activation(std[:, :], mv[:, :, 1], ACT.Sqrt, bias=eps[:, :]).then_inc(std_ready, 1)

            def ln_turned(n, lo):
                for c in range(KC):
                    act.wait_ge(xt_psum, 2 * n + (c + 1))
                    act.activation(xnT[:, c, :], bank[lo + c][:, :], ACT.Copy).then_inc(xnT_ready, 1)

            act.wait_ge(setup_done, 1)
            with act.Fori(0, B) as b:
                act.wait_ge(kv_psum, 2 * b + 1)
                act.activation(kT0, bank[1][0:DH, :], ACT.Identity, bias=bk0[:, :]).then_inc(qk_ready, 1)
                ln_std(2 * b)
                ln_turned(2 * b, 6)
                act.wait_ge(q_psum, b + 1)
                act.activation(qT0, bank[0][0:DH, :], ACT.Identity, bias=bq0[:, :], scale=0.25).then_inc(qk_ready, 1)
                for q in range(TB):
                    act.wait_ge(negmax0, 4 * b + q + 1)
                    act.activation(p0[:, q, :], bank[q][:, :], ACT.Exp, bias=negmax[:, 0, q:q + 1],
                                   accum_out=rowsum[:, q:q + 1]).then_inc(probs0, 1)
                act.wait_ge(pt0_psum, b + 1)
                for k in range(2):
                    act.activation(pT0[:, k, :], bank[4 + k][:, :], ACT.Copy).then_inc(pt0_act, 1)
                act.wait_ge(o0_psum, b + 1)
                act.activation(oT0, bank[0][0:DH + 1, :], ACT.Copy).then_inc(o0_ready, 1)
                ln_std(2 * b + 1)
                ln_turned(2 * b + 1, 6)

            def gates(i):
                R = route[i]
                if i == 0:
                    act.wait_ge(logits_ready, B)
                    n = NT * E0
                    act.activation(keys[:, :, :].rearrange("p t e -> p (t e)")[:, 0:n],
                                   logits[:, :, :].rearrange("p t e -> p (t e)")[:, 0:n], ACT.Sigmoid).then_inc(R["exp_ready"], 1)
                else:
                    act.wait_ge(R["exp_in"], 1)
                    act.activation(wtop[:, :, :], wtop[:, :, :], ACT.Exp).then_inc(R["exp_ready"], 1)

            def experts(i):
                L, M = LAYERS[i], moe[i]
                HT, NB = L["H"] // P, L["NB"]
                CH = HT // 2
                HALF = KC * L["H"] // 2

                def high_up(j, par, half):
                    if half == 0:
                        act.wait_ge(M["up_in"], j * 16 + 16)
                        act.wait_ge(M["up_psum"], j * CH + CH)
                    cols = slice(half * HALF, (half + 1) * HALF)
                    act.activation(wup[par][:, 0, cols], wraw[0][:, cols], ACT.Copy).then_inc(M["up_high"], 1)

                def high_down(j, par, half):
                    if half == 0:
                        act.wait_ge(M["down_in"], j * 16 + 16)
                        act.wait_ge(M["y_psum"], j + 1)
                    cols = slice(half * HALF, (half + 1) * HALF)
                    act.activation(wdn[par][:, 0, cols], wraw[1][:, cols], ACT.Copy).then_inc(M["down_high"], 1)

                def high_x(j, par):
                    act.wait_ge(M["xt_psum"], j + 1)
                    act.activation(xT[par][:, 0, :], bank[0][:, :], ACT.Copy).then_inc(M["x_high"], 1)

                def hidden(j, n, par, ch):
                    act.wait_ge(M["up_psum"], j * CH + (2 * CH + ch + 1))
                    act.wait_ge(M["h_ready"], j * CH + (ch + 1))
                    if i == 0:
                        act.activation(hraw[ch % 2][:, :], bank[1 + ch][:, :], ACT.Relu).then_inc(M["relu_ready"], 1)
                        act.wait_ge(M["relu_ready"], j * CH + (ch + 1))
                        act.activation(hraw[ch % 2][:, :], hraw[ch % 2][:, :], ACT.Square).then_inc(M["h_raw"], 1)
                    else:
                        if ch == 0:
                            act.wait_ge(M[("bias_even", "bias_odd")[par]], n * 16 + 16)
                        for m in range(2):
                            h = 2 * ch + m
                            last = act.activation(hraw[ch % 2][:, m * BT:(m + 1) * BT], bank[1 + ch][:, m * BT:(m + 1) * BT],
                                                  ACT.Gelu, bias=bup[par][:, h:h + 1])
                        last.then_inc(M["h_raw"], 1)

                def step(j, n, par, more=True):
                    work = [lambda: high_down(j + 1, 1 - par, 0), lambda: high_down(j + 1, 1 - par, 1)]
                    if more:
                        work += [lambda: high_up(j + 2, par, 0), lambda: high_up(j + 2, par, 1)]
                    for ch in range(CH):
                        for w in work[ch * len(work) // CH:(ch + 1) * len(work) // CH]:
                            w()
                        hidden(j + 1, n, 1 - par, ch)
                    if more:
                        high_x(j + 2, par)

                act.nop().then_inc(M["h_raw"], CH)
                high_up(0, 0, 0)
                high_up(0, 0, 1)
                high_x(0, 0)
                step(-1, 0, 1)
                with act.Fori(0, NB // 2 - 1) as t:
                    step(2 * t, t, 0)
                    step(2 * t + 1, t + 1, 1)
                step(NB - 2, NB // 2 - 1, 0, more=False)

            if STOP >= 2:
                gates(0)
                experts(0)
            if STOP >= 3:
                act.nop().then_inc(probs1, 3)
                act.nop().then_inc(pt1_act, 2)
                act.nop().then_inc(ot_taken, 1)
                with act.Fori(0, B) as b:
                    for c in range(KC):
                        act.wait_ge(kv1_psum, 4 * b + (c + 1))
                        act.activation(kT1[:, c, :], bank[5 + c][:, :], ACT.Identity, bias=bk1[:, c:c + 1]).then_inc(k1_ready, 1)
                    ln_std(2 * b + 2 * B)
                    ln_turned(2 * b + 2 * B, 3)
                    for c in range(KC):
                        act.wait_ge(q1_psum, 2 * b + (c + 1))
                        act.activation(qT1[:, c, :], bank[7 if c else 2][:, :], ACT.Identity, bias=bq1[:, c:c + 1],
                                       scale=0.25).then_inc(q1_ready, 1)
                    QOFF = {3: 0, 2: 512, 1: 896, 0: 1152}

                    def exps(h):
                        act.wait_ge(pt1_psum, b * (3 * NH) + (3 * h + 3))
                        for part, tiles in enumerate(((3,), (2,), (1, 0))):
                            act.wait_ge(negmax1, b * (3 * NH) + (3 * h + part + 1))
                            at = 0
                            for q in tiles:
                                w = (q + 1) * P
                                last = act.activation(p1[:, h % 2, QOFF[q]:QOFF[q] + w], bank[part][:, at:at + w], ACT.Exp,
                                                      bias=negmax[:, h % 2, q:q + 1])
                                at += w
                            last.then_inc(probs1, 1)

                    def take_probs(h):
                        s = (h // HG % 2) * HG + h % HG
                        act.wait_ge(ot_psum, b * 4 + (h // HG + 1))
                        for part in (1, 2):
                            act.wait_ge(pt1_psum, b * (3 * NH) + (3 * h + part + 7))
                            at = 512 + (part - 1) * 384
                            act.activation(pT1[:, s, at:at + 384], bank[3 + part][:, 0:384], ACT.Copy).then_inc(pt1_act, 1)

                    def take_out(g):
                        act.wait_ge(ot_psum, b * 4 + (g + 3))
                        act.activation(oTs[:, :], bank[6][:, :], ACT.Copy).then_inc(ot_taken, 1)

                    exps(0)
                    for h in range(NH):
                        if h < NH - 1:
                            exps(h + 1)
                        take_probs(h)
                        if h % HG == 0 and h:
                            take_out(h // HG - 1)
                    take_out(3)
                    for c in range(KC):
                        act.wait_ge(on_psum, 2 * b + (c + 1))
                        act.activation(oT1[:, c, :], bank[3 + c][:, :], ACT.Copy).then_inc(on_ready, 1)
                    ln_std(2 * b + (2 * B + 1))
                    ln_turned(2 * b + (2 * B + 1), 3)
            if STOP >= 4:
                gates(1)
                experts(1)
            act.wait_ge(out_done, 1)
            act.dma_start(out_v, x[:, :, :]).then_inc(out_stored, 16)
            act.wait_ge(out_stored, 16)

        @block.gpsimd
        def _(pool):
            pool.wait_ge(setup_done, 1)
            zrows = sorted_x.rearrange("(n p r) d -> n p (r d)", p=P, r=4)
            nz = NB1 * BT // (4 * P)
            for n in range(nz):
                pool.dma_start(zrows[n], zeros[:, :]).then_inc(zeroed, 16)

            def scatter(i):
                L, R = LAYERS[i], route[i]
                pool.wait_ge(R["slots_ready"], 1)
                if i == 0:
                    pool.wait_ge(zeroed, 16 * nz)
                for k in range(L["K"]):
                    for t in range(NT):
                        src = xw[k][:, t, :] if i == 0 else xn[:, t, :]
                        pool.indirect_dma_start(sorted_x, bass.IndirectOffsetOnAxis(sloti[:, k, t:t + 1].bitcast(U32), 0),
                                                src, None).then_inc(R["scattered"], 16)

            def gather(i):
                L, R = LAYERS[i], route[i]
                pool.wait_ge(moe[i]["store_even"], 16 * (L["NB"] // 2 + 1))
                pool.wait_ge(moe[i]["store_odd"], 16 * (L["NB"] // 2 + 1))
                for t in range(NT):
                    if t >= 4:
                        pool.wait_ge(R["combined"], t - 3)
                    for k in range(L["K"]):
                        pool.indirect_dma_start(gat[:, t % 4, k, :], None, sorted_y[0:L["NB"] * BT, :],
                                                bass.IndirectOffsetOnAxis(sloti[:, k, t:t + 1].bitcast(U32), 0)).then_inc(R[f"gathered{t % 4}"], 16)

            if STOP >= 2:
                scatter(0)
                gather(0)
            if STOP >= 4:
                scatter(1)
                gather(1)

        @block.vector
        def _(dve):
            chn = Chain(dve, dve_step)

            def layer_norm(n, src, dsts):
                dve.sem_inc(dve_turn, 1)
                for t in range(TB):
                    last = dve.bn_stats(stats[:, t, :], src(t))
                chn.link(last)
                dve.sem_inc(dve_turn, 1)
                for t in range(TB):
                    last = dve.bn_aggr(mv[:, t, :], stats[:, t, :])
                last.then_inc(var_ready, 1)
                dve.wait_ge(std_ready, n + 1)
                chn.link(dve.reciprocal(rstd[:, :], std[:, :]))
                for dst in dsts:
                    for t in range(TB):
                        last = dve.tensor_scalar(dst(t), src(t), mv[:, t, 0:1], rstd[:, t:t + 1], ALU.subtract, ALU.mult)
                last.then_inc(xn_ready, 1)

            dve.memset(eps[:, :], EPS)
            dve.memset(zeros[:, :], 0.0)
            dve.memset(v0[:, :, DH:DH + 1], 1.0)
            dve.wait_ge(weights_in, 16 * len(loads))
            dve.tensor_copy(ident_b[:, :], ident)
            dve.tensor_copy(causal_b[:, :], con[:, C_CAUSAL:C_HEAD])
            dve.tensor_scalar(bq1[:, :], bq1[:, :], 0.25, None, ALU.mult)
            dve.tensor_scalar(bq0[:, :], bq0[:, :], 0.25, None, ALU.mult).then_inc(setup_done, 1)
            dve.wait_ge(fold_psum, 1)
            dve.tensor_copy(wcT[:, 0, 0:DH], bank[0][:, 0:DH])
            dve.tensor_copy(wcT[:, 1, 0:DH], bank[1][:, 0:DH]).then_inc(fold_ready, 1)
            dve.wait_ge(fold_psum, 2)
            dve.tensor_copy(weff[:, :], bank[2][0:DH + 1, 0:D]).then_inc(fold_ready, 1)

            with dve.Fori(0, B) as b:
                chn.enter(b, STEPS_ATTN0)
                tile = lambda t: x[:, bass.ds(b * TB + t, 1), :].rearrange("p a d -> p (a d)")
                ntile = lambda t: xn[:, bass.ds(b * TB + t, 1), :].rearrange("p a d -> p (a d)")
                layer_norm(2 * b, tile, [lambda t: xnb[:, t, :]])
                dve.wait_ge(kv_psum, 2 * b + 2)
                dve.tensor_tensor(v0[:, :, 0:DH], bank[2][:, 0:TB * DH].rearrange("p (k d) -> p k d", k=TB),
                                  bv0[:, :].unsqueeze(1).broadcast_to((P, TB, DH)), ALU.add).then_inc(v_ready, 1)
                for q in range(TB):
                    dve.wait_ge(scores0, 4 * b + q + 1)
                    dve.tensor_reduce(negmax[:, 0, q:q + 1], bank[q][:, :], AX.X, ALU.max, negate=True).then_inc(negmax0, 1)
                dve.wait_ge(pt0_psum, b + 1)
                for k in range(2, 4):
                    dve.tensor_copy(pT0[:, k, :], bank[4 + k][:, :]).then_inc(pt0_dve, 1)
                dve.wait_ge(probs0, 4 * b + 4)
                chn.link(dve.reciprocal(rinv[:, :], rowsum[:, :]))
                for q in range(TB):
                    if q % 2 == 0:
                        dve.wait_ge(attn0, 2 * b + (q // 2 + 1))
                    last = dve.scalar_tensor_tensor(tile(q), bank[1 + q // 2][:, (q % 2) * D:(q % 2 + 1) * D],
                                                    rinv[:, q:q + 1], tile(q), ALU.mult, ALU.add)
                chn.link(last)
                layer_norm(2 * b + 1, tile, [ntile, lambda t: xnb[:, t, :]])
                dve.wait_ge(logits_psum, b + 1)
                lo = logits[:, :, :].rearrange("p t e -> p (t e)")[:, 0:NT * E0].rearrange("p (b n) -> p b n", b=B)
                chn.link(dve.tensor_copy(lo[:, bass.ds(b, 1), :].rearrange("p a n -> p (a n)"), bank[3][:, 0:TB * E0]))
            chn.leave(B)
            dve.nop().then_inc(logits_ready, B)

            def router(i):
                L, R = LAYERS[i], route[i]
                E, K, NB = L["E"], L["K"], L["NB"]

                def view(t):
                    return t[:, :, :].rearrange("p t e -> p (t e)")[:, 0:NT * E].rearrange("p (t e) -> p t e", t=NT)

                lg, ky, se, sl, wk = (view(t) for t in (logits, keys, sel, slot, work))
                hots = [view(h) for h in hot]
                if i == 0:
                    dve.wait_ge(R["exp_ready"], 1)
                    chn.link(dve.tensor_tensor(lg, ky, eb0[:, :].unsqueeze(1).broadcast_to((P, NT, E)), ALU.add))
                for t in range(NT):
                    last = dve.max(top8[:, t, :], lg[:, t, :])
                chn.link(last)
                for t in range(NT):
                    last = dve.max_index(idx8[:, t, :], top8[:, t, :], lg[:, t, :])
                chn.link(last)
                chn.link(dve.tensor_copy(idxf[:, :, :], idx8[:, :, :]))
                for k in range(K):
                    last = dve.tensor_tensor(hots[k], con[:, C_IE:C_IE + E].unsqueeze(1).broadcast_to((P, NT, E)),
                                             idxf[:, :, k:k + 1].broadcast_to((P, NT, E)), ALU.is_equal)
                chn.link(last)
                chn.link(dve.tensor_tensor(se, hots[0], hots[1], ALU.add))
                if K == 3:
                    chn.link(dve.tensor_tensor(se, se, hots[2], ALU.add))
                dve.nop().then_inc(R["sel_ready"], 1)
                if i == 0:
                    for k in range(K):
                        chn.link(dve.tensor_tensor(wk, hots[k], ky, ALU.mult))
                        chn.link(dve.tensor_reduce(wtop[:, k, :], wk, AX.X, ALU.add))
                    for k in range(K):
                        dve.tensor_tensor(xw[k], xn[:, :, :], wtop[:, k, :].unsqueeze(2).broadcast_to((P, NT, D)), ALU.mult)
                else:
                    for k in range(K):
                        last = dve.tensor_tensor(wtop[:, k, :], top8[:, :, k], top8[:, :, 0], ALU.subtract)
                    last.then_inc(R["exp_in"], 1)
                    dve.wait_ge(R["exp_ready"], 1)
                    chn.link(dve.tensor_tensor(wsum[:, :], wtop[:, 0, :], wtop[:, 1, :], ALU.add))
                    chn.link(dve.tensor_tensor(wsum[:, :], wsum[:, :], wtop[:, 2, :], ALU.add))
                    chn.link(dve.reciprocal(wsum[:, :], wsum[:, :]))
                    chn.link(dve.tensor_tensor(wtop[:, :, :], wtop[:, :, :], wsum[:, :].unsqueeze(1).broadcast_to((P, K1, NT)), ALU.mult))
                dve.wait_ge(R["rank_psum"], 1)
                chn.link(dve.memset(runs[:, 0, 0:E], 0.0))
                for t in range(NT):
                    chn.link(dve.tensor_tensor(runs[:, t + 1, 0:E], bank[1][:, t * E:(t + 1) * E], runs[:, t, 0:E], ALU.add))
                chn.link(dve.tensor_scalar(nblki[:, 0:E], runs[:, NT, 0:E], 1.0 / BT, (BT / 2 - 0.5) / BT, ALU.mult, ALU.add))
                chn.link(dve.tensor_copy(nblk[:, 0:E], nblki[:, 0:E]))
                chn.link(dve.tensor_copy(upto[:, 0:1], nblk[:, 0:1]))
                for e in range(1, E):
                    chn.link(dve.tensor_tensor(upto[:, e:e + 1], upto[:, e - 1:e], nblk[:, e:e + 1], ALU.add))
                chn.link(dve.tensor_tensor(past[:, 0:NB, 0:E], con[0:1, C_IB:C_IB + NB].unsqueeze(2).broadcast_to((1, NB, E)),
                                          upto[0:1, 0:E].unsqueeze(1).broadcast_to((1, NB, E)), ALU.is_ge))
                chn.link(dve.tensor_reduce(owner[:, 0:NB], past[:, 0:NB, 0:E], AX.X, ALU.add))
                dve.tensor_scalar(owneri[:, 0:NB], owner[:, 0:NB], float(E - 1), None, ALU.min).then_inc(R["owner_ready"], 1)
                chn.link(dve.tensor_tensor(upto[:, 0:E], upto[:, 0:E], nblk[:, 0:E], ALU.subtract))
                chn.link(dve.tensor_scalar(upto[:, 0:E], upto[:, 0:E], float(BT), None, ALU.mult))
                chn.link(dve.tensor_tensor(sl, bank[0][:, 0:NT * E].rearrange("p (t e) -> p t e", t=NT), runs[:, 0:NT, 0:E], ALU.add))
                chn.link(dve.tensor_tensor(sl, sl, upto[:, 0:E].unsqueeze(1).broadcast_to((P, NT, E)), ALU.add))
                for k in range(K):
                    chn.link(dve.tensor_tensor(wk, hots[k], sl, ALU.mult))
                    chn.link(dve.tensor_reduce(slotf[:, k, :], wk, AX.X, ALU.add))
                dve.tensor_copy(sloti[:, 0:K, :], slotf[:, 0:K, :]).then_inc(R["slots_ready"], 1)

            def experts(i):
                L, M, R = LAYERS[i], moe[i], route[i]
                HT, NB = L["H"] // P, L["NB"]
                CH = HT // 2
                HALF = KC * L["H"] // 2
                dve.nop().then_inc(M["y_ready"], 2)
                dve.nop().then_inc(M["h_ready"], 2)

                def low_up(j, par, half):
                    cols = slice(half * HALF, (half + 1) * HALF)
                    dve.wait_ge(M["up_high"], 2 * j + (half + 1))
                    dve.tensor_tensor(wup[par][:, 1, cols], wraw[0][:, cols], wup[par][:, 0, cols].bitcast(F32),
                                      ALU.subtract).then_inc(M["up_ready"], 1)

                def low_down(j, par, half):
                    cols = slice(half * HALF, (half + 1) * HALF)
                    dve.wait_ge(M["down_high"], 2 * j + (half + 1))
                    dve.tensor_tensor(wdn[par][:, 1, cols], wraw[1][:, cols], wdn[par][:, 0, cols].bitcast(F32),
                                      ALU.subtract).then_inc(M["down_ready"], 1)

                def low_x(j, par):
                    dve.wait_ge(M["x_high"], j + 1)
                    dve.tensor_tensor(xT[par][:, 1, :], bank[0][:, :], xT[par][:, 0, :].bitcast(F32), ALU.subtract).then_inc(M["xT_ready"], 1)

                def hidden(j, par, ch):
                    cols = slice(ch * 512, (ch + 1) * 512)
                    dve.wait_ge(M["h_raw"], j * CH + (CH + ch + 1))
                    dve.wait_ge(M["y_psum"], j + 1)
                    chn.link(dve.tensor_copy(hid[par][:, 0, cols], hraw[ch % 2][:, :]))
                    dve.tensor_tensor(hid[par][:, 1, cols], hraw[ch % 2][:, :], hid[par][:, 0, cols].bitcast(F32),
                                      ALU.subtract).then_inc(M["h_ready"], 1)

                def take_y(j, n, par):
                    dve.wait_ge(M["y_psum"], j + 3)
                    dve.wait_ge(M[("store_even", "store_odd")[par]], n * 16 + 16)
                    if i == 0:
                        last = dve.tensor_copy(ysb[par][:, :], bank[5 + par][:, :])
                    else:
                        dve.wait_ge(M[("dbias_even", "dbias_odd")[par]], n * 16 + 16)
                        last = dve.tensor_tensor(ysb[par][:, :].rearrange("p (i d) -> p i d", i=2),
                                                 bank[5 + par][:, :].rearrange("p (i d) -> p i d", i=2),
                                                 bdn[par][:, :].unsqueeze(1).broadcast_to((P, 2, D)), ALU.add)
                    last.then_inc(M["y_ready"], 1)

                def step(j, n, par, first=False, more=True):
                    work = [lambda: low_down(j + 1, 1 - par, 0), lambda: low_down(j + 1, 1 - par, 1)]
                    if more:
                        work += [lambda: low_up(j + 2, par, 0), lambda: low_up(j + 2, par, 1)]
                    for ch in range(CH):
                        for w in work[ch * len(work) // CH:(ch + 1) * len(work) // CH]:
                            w()
                        hidden(j + 1, 1 - par, ch)
                    if more:
                        low_x(j + 2, par)
                    if not first:
                        take_y(j, n, par)

                low_up(0, 0, 0)
                low_up(0, 0, 1)
                low_x(0, 0)
                step(-1, 0, 1, first=True)
                with dve.Fori(0, NB // 2 - 1) as t:
                    chn.enter(t, 2 * CH)
                    step(2 * t, t, 0)
                    step(2 * t + 1, t, 1)
                chn.leave(NB // 2 - 1)
                step(NB - 2, NB // 2 - 1, 0, more=False)
                take_y(NB - 1, NB // 2 - 1, 1)

            def combine(i):
                L, R = LAYERS[i], route[i]
                K = L["K"]
                for t in range(NT):
                    dve.wait_ge(R[f"gathered{t % 4}"], 16 * K * (t // 4 + 1))
                    for k in range(K):
                        g = gat[:, t % 4, k, :]
                        if i == 0:
                            last = dve.tensor_tensor(x[:, t, :], x[:, t, :], g, ALU.add)
                        else:
                            last = dve.scalar_tensor_tensor(x[:, t, :], g, wtop[:, k, t:t + 1], x[:, t, :], ALU.mult, ALU.add)
                        if k < K - 1:
                            chn.link(last)
                    last.then_inc(R["combined"], 1)
                dve.wait_ge(R["combined"], NT)

            if STOP >= 2:
                router(0)
                experts(0)
                combine(0)
            if STOP >= 3:
                dve.memset(v1[:, :, :, :], 0.0).then_inc(v1_cleared, 1)
                dve.wait_ge(v1_cleared, 1)
                dve.memset(v1[:, :, :, DH:DH + 1], 1.0)
                dve.nop().then_inc(pt1_dve, 1)
                dve.nop().then_inc(o_taken, 1)
                with dve.Fori(0, B) as b:
                    chn.enter(b, STEPS_ATTN1)
                    tile = lambda t: x[:, bass.ds(b * TB + t, 1), :].rearrange("p a d -> p (a d)")
                    ntile = lambda t: xn[:, bass.ds(b * TB + t, 1), :].rearrange("p a d -> p (a d)")
                    layer_norm(2 * b + 2 * B, tile, [lambda t: xnb[:, t, :]])
                    for k in range(2):
                        dve.wait_ge(kv1_psum, 4 * b + (3 + k))
                        for j in range(2):
                            last = dve.tensor_tensor(v1[:, 2 * k + j, :, 0:DH],
                                                     bank[k][:, j * D:(j + 1) * D].rearrange("p (h d) -> p h d", h=NH),
                                                     bv1[:, :].rearrange("p (h d) -> p h d", h=NH), ALU.add)
                        last.then_inc(v1_ready, 1)
                    dve.wait_ge(k1_ready, 2 * b + 2)
                    for h in range(NH):
                        dve.tensor_scalar(kz[:, h, :], kT1[:, h // 8, :], headmask[:, h % 8:h % 8 + 1], None, ALU.mult).then_inc(kz_ready, 1)

                    def maxima(h):
                        for part, tiles in enumerate(((3,), (2,), (1, 0))):
                            dve.wait_ge(scores1, b * (3 * NH) + (3 * h + part + 1))
                            at = 0
                            for q in tiles:
                                w = (q + 1) * P
                                last = dve.tensor_reduce(negmax[:, h % 2, q:q + 1], bank[part][:, at:at + w], AX.X, ALU.max, negate=True)
                                at += w
                            last.then_inc(negmax1, 1)

                    def take_probs(h):
                        s = (h // HG % 2) * HG + h % HG
                        dve.wait_ge(ot_psum, b * 4 + (h // HG + 1))
                        dve.wait_ge(pt1_psum, b * (3 * NH) + (3 * h + 7))
                        dve.tensor_copy(pT1[:, s, 0:512], bank[3][:, :]).then_inc(pt1_dve, 1)

                    def normalise(g):
                        dve.wait_ge(o_psum, b * 4 + (g + 1))
                        o = bank[7][:, :].rearrange("p (q i d) -> p q i d", q=TB, i=HG)
                        chn.link(dve.reciprocal(orec[:, :, :], o[:, :, :, DH]))
                        dve.tensor_tensor(o1[:, :, g * HG * DH:(g + 1) * HG * DH].rearrange("p q (i d) -> p q i d", i=HG),
                                          o[:, :, :, 0:DH], orec[:, :, :].unsqueeze(3).broadcast_to((P, TB, HG, DH)),
                                          ALU.mult).then_inc(o_taken, 1)

                    maxima(0)
                    for h in range(NH):
                        if h < NH - 1:
                            maxima(h + 1)
                        take_probs(h)
                        if h % HG == 1 and h > 1:
                            normalise(h // HG - 1)
                    normalise(3)
                    for q in range(TB):
                        if q % 2 == 0:
                            dve.wait_ge(attn1, 2 * b + (q // 2 + 1))
                        last = dve.tensor_tensor(tile(q), bank[5 + q // 2][:, (q % 2) * D:(q % 2 + 1) * D], tile(q), ALU.add)
                    chn.link(last)
                    for q in range(TB):
                        last = dve.tensor_tensor(tile(q), tile(q), bo1[:, :], ALU.add)
                    chn.link(last)
                    layer_norm(2 * b + (2 * B + 1), tile, [ntile, lambda t: xnb[:, t, :]])
                    dve.wait_ge(logits_psum, b + (B + 1))
                    lo = logits[:, :, :].rearrange("p (b t) e -> p b (t e)", b=B)
                    chn.link(dve.tensor_copy(lo[:, bass.ds(b, 1), :].rearrange("p a n -> p (a n)"), bank[7][:, 0:TB * E1]))
                chn.leave(B)
            if STOP >= 4:
                router(1)
                experts(1)
                combine(1)
            dve.nop().then_inc(out_done, 1)


STEPS_ATTN0 = 7
STEPS_ATTN1 = 11


def kernel(**inputs):
    import numpy as np
    import concourse.bacc as bacc
    from concourse import mybir as mb
    from concourse.bass_utils import run_bass_kernel_spmd as run

    a = {k: np.ascontiguousarray(v) for k, v in inputs.items()}
    a["con"] = constants()
    a["ctxT"] = np.ascontiguousarray(a.pop("ctx_1024").reshape(B * S, D).T)
    a["gate0T"] = np.ascontiguousarray(a.pop("L0_ffn_gate_w").T)
    a["up0"] = np.ascontiguousarray(a.pop("L0_ffn_w_up").transpose(0, 2, 1))
    a["dn0"] = np.ascontiguousarray(a.pop("L0_ffn_w_down").transpose(0, 2, 1))
    a["up1"] = a.pop("L1_ffn_Wup")
    a["bup1T"] = np.ascontiguousarray(a.pop("L1_ffn_bup").reshape(E1, H1 // P, P).transpose(0, 2, 1))
    a["bq1T"] = np.ascontiguousarray(a.pop("L1_xattn_bq").reshape(KC, P).T)
    a["bk1T"] = np.ascontiguousarray(a.pop("L1_xattn_bk").reshape(KC, P).T)

    nc = bacc.Bacc("TRN2", target_bir_lowering=False, num_devices=1)
    aps = {k: nc.dram_tensor(f"in_{k}", v.shape, mb.dt.from_np(v.dtype), kind="ExternalInput").ap() for k, v in a.items()}
    out = nc.dram_tensor("out_0", (B, S, D), F32, kind="ExternalOutput").ap()
    build(nc, aps, out)
    r = run(nc, [{f"in_{k}": v for k, v in a.items()}], core_ids=[0])
    return r.results[0]["out_0"]
```

```python
from contextlib import ExitStack

import numpy as np

import concourse.bass as bass
from concourse import mybir

F32 = mybir.dt.float32
F32R = mybir.dt.float32r
BF16 = mybir.dt.bfloat16
I32 = mybir.dt.int32
U32 = mybir.dt.uint32
ALU = mybir.AluOpType
ACT = mybir.ActivationFunctionType
AX = mybir.AxisListType

P = 128
B, S, D = 4, 512, 256
NT = B * S // P
TB = S // P
KC = D // P
NH = 16
DH = D // NH
HG = 4
SLOTW = 32
EPS = 1e-5
BT = 256
E0, K0, H0 = 8, 2, 512
E1, K1, H1 = 12, 3, 1024
NB0 = (B * S * K0 // BT + E0 - 1 + 1) // 2 * 2
NB1 = (B * S * K1 // BT + E1 - 1 + 1) // 2 * 2

C_ID, C_TRI, C_ONE, C_CAUSAL, C_HEAD, C_FOLD, C_IE, C_IB, C_SEL, C_PLACE, C_TOK, C_SPARE, C_END = np.cumsum(
    [0, P, P, P, P, 8, DH, E1, NB1, P, E1, 2 * NT, BT // P]).tolist()
ROOM = B * S + BT
R_TOK, R_EXP, R_W, RW = D, D + 1, D + 4, D + 8


def constants():
    c = np.zeros((P, C_END), np.float32)
    p = np.arange(P)
    c[:, C_ID:C_TRI] = np.eye(P)
    c[:, C_TRI:C_ONE] = p[:, None] < p[None, :]
    c[:, C_ONE:C_CAUSAL] = 1.0
    c[:, C_CAUSAL:C_HEAD] = np.where(p[None, :] <= p[:, None], 0.0, -1e30)
    c[:, C_HEAD:C_FOLD] = p[:, None] // DH == np.arange(8)[None, :]
    c[:, C_FOLD:C_IE] = p[:, None] % DH == np.arange(DH)[None, :]
    c[:, C_IE:C_IB] = 1 + np.arange(E1)[None, :]
    c[:, C_IB:C_SEL] = np.arange(NB1)[None, :]
    c[:, C_SEL:C_PLACE] = np.arange(P)[None, :] % SLOTW == DH
    c[:, C_PLACE:C_TOK] = ROOM * np.arange(E1)[None, :]
    for i, k in enumerate((K0, K1)):
        c[:, C_TOK + i * NT:C_TOK + (i + 1) * NT] = BT + k * (np.arange(NT)[None, :] * P + p[:, None])
    c[:, C_SPARE:C_END] = BT // P * p[:, None] + np.arange(BT // P)[None, :]
    return c


class Chain:

    def __init__(self, engine, sem):
        self.engine, self.sem, self.base, self.turn, self.per, self.n = engine, sem, 0, 0, 0, 0

    def enter(self, turn, per):
        self.base, self.turn, self.per, self.n = self.base + self.n, turn, per, 0

    def leave(self, turns):
        assert self.n == self.per, (self.n, self.per)
        self.base, self.turn, self.per, self.n = self.base + turns * self.per, 0, 0, 0

    def link(self, ins):
        self.n += 1
        ins.then_inc(self.sem, 1)
        self.engine.wait_ge(self.sem, self.turn * self.per + (self.base + self.n))


STOP = 9
RANKS = 128


def build(nc, A, out):
    with ExitStack() as ctx:
        def sb(name, shape, dt=F32):
            return ctx.enter_context(nc.sbuf_tensor(name, shape, dt))

        def sem(name):
            return ctx.enter_context(nc.semaphore(name))

        bank = [ctx.enter_context(nc.psum_tensor(f"bank{i}", [P, 512], F32)) for i in range(8)]
        sorted_x = nc.dram_tensor("sorted_x", (E1 * ROOM + BT, RW), F32, kind="Internal").ap()
        token_y = nc.dram_tensor("token_y", (BT + K1 * B * S, D), F32, kind="Internal").ap()

        con = sb("con", [P, C_END])
        ident = con[:, C_ID:C_TRI]
        before = con[:, C_TRI:C_ONE]
        ones = con[:, C_ONE:C_CAUSAL]
        headmask = con[:, C_HEAD:C_FOLD]
        fold = con[:, C_FOLD:C_IE]
        ident_b = sb("ident_b", [P, P], BF16)
        before_b, ones_b = sb("before_b", [P, P], BF16), sb("ones_b", [P, P], BF16)
        causal_b = sb("causal_b", [P, P], BF16)
        eps = sb("eps", [P, 1])
        zeros = sb("zeros", [P, BT // P, RW])
        wq0, wk0, wv0 = sb("wq0", [P, KC, DH]), sb("wk0", [P, KC, DH]), sb("wv0", [P, KC, DH])
        wc0, wo0 = sb("wc0", [P, KC, D]), sb("wo0", [P, KC, D])
        bq0, bk0 = sb("bq0", [DH, 1]), sb("bk0", [DH, 1])
        bv0 = sb("bv0", [P, DH])
        bo0 = sb("bo0", [1, D])
        bc0 = sb("bc0", [P, KC])
        wcT = sb("wcT", [P, KC, P])
        weff = sb("weff", [P, D])
        gw0 = sb("gw0", [P, KC, E0])
        eb0 = sb("eb0", [P, E0])
        wq1, wk1, wv1, wo1 = (sb(n, [P, KC, D]) for n in ("wq1", "wk1", "wv1", "wo1"))
        bq1, bk1 = sb("bq1", [P, KC]), sb("bk1", [P, KC])
        bv1, bo1 = sb("bv1", [P, D]), sb("bo1", [P, D])
        gw1 = sb("gw1", [P, KC, E1])

        x = sb("x", [P, NT, D])
        xn = sb("xn", [P, NT, RW])
        def pair(name, shape, dt=F32):
            return [sb(f"{name}{i}", shape, dt) for i in range(2)]

        stats, mv = pair("stats", [P, TB, 6]), pair("mv", [P, TB, 2])
        std, rstd = pair("std", [P, TB]), pair("rstd", [P, TB])
        rowsum, rinv = pair("rowsum", [P, TB]), pair("rinv", [P, TB])
        negmax = sb("negmax", [P, 2, TB])

        logits, keys = pair("logits", [P, TB, E1]), pair("keys", [P, TB, E1])
        top8 = pair("top8", [P, TB, 8])
        topk = sb("topk", [P, NT, K1])
        idx8, idxf = pair("idx8", [P, TB, 8], U32), pair("idxf", [P, TB, K1])
        hot = [pair(f"hot{k}_", [P, TB, E1]) for k in range(K1)]
        sel = pair("sel", [P, (TB + 1) * E1], BF16)
        slot = sb("slot", [P, TB, E1])
        work = sb("work", [P, TB, E1])
        wtop = sb("wtop", [P, K1, NT])
        wsum = sb("wsum", [P, NT])
        slotf = sb("slotf", [P, K1, TB])
        sloti = sb("sloti", [P, K1, NT], I32)
        place = sb("place", [P, E1])
        placei = sb("placei", [1, E1], I32)
        nblk = sb("nblk", [P, E1])
        nblki = sb("nblki", [P, E1], I32)
        upto = [sb(f"upto{i}", [P, 8 + E1]) for i in range(2)]
        past = sb("past", [P, NB1, E1])
        owner = sb("owner", [P, NB1])
        start = sb("start", [P, NB1])
        owneri = sb("owneri", [1, NB1], I32)
        starti = sb("starti", [1, NB1], I32)

        with ExitStack() as scope:
            def ab(name, shape, dt=F32):
                return scope.enter_context(nc.sbuf_tensor(name, shape, dt))

            regA = ab("regA", [P, 16 * S])
            kz = regA[:, :].rearrange("p (h k) -> p h k", h=NH)
            PW = S * (TB + 1) // 2
            pT1 = ab("pT1", [P, 8, PW])
            att0 = []
            for i in range(2):
                reg = regA[:, :] if i == 0 else pT1[:, :, :].rearrange("p s w -> p (s w)")
                att0.append(dict(qT=reg[0:DH, 0:512], kT=reg[0:DH, 512:1024],
                                 v=reg[:, 1024:1024 + TB * SLOTW].rearrange("p (k d) -> p k d", k=TB),
                                 p=reg[:, 2048:4096].rearrange("p (q k) -> p q k", q=TB),
                                 pT=reg[:, 4096:6144].rearrange("p (k q) -> p k q", k=TB),
                                 oT=reg[:, 6144:6656]))
            p1 = ab("p1", [P, 2, PW])
            qT1, kT1 = ab("qT1", [P, KC, S]), ab("kT1", [P, KC, S])
            v1 = ab("v1", [P, TB, NH, SLOTW])
            oTs = ab("oTs", [P, S])
            o1 = ab("o1", [P, TB, D])
            oT1 = ab("oT1", [P, KC, S])
            orec = ab("orec", [P, TB, HG])
            ctxT = [ab(f"ctxT{i}", [P, KC, S]) for i in range(2)]
            xnb = [ab(f"xnb{i}", [P, TB, D]) for i in range(2)]
            xnT = [ab(f"xnT{i}", [P, KC, S]) for i in range(2)]

        with ExitStack() as scope:
            def mb(name, shape, dt=F32):
                return scope.enter_context(nc.sbuf_tensor(name, shape, dt))

            xT = [mb(f"xT{i}", [P, 2, 512], F32R) for i in range(2)]
            hid = [mb(f"hid{i}", [P, 2, 2048], F32R) for i in range(2)]
            hraw = [mb(f"hraw{i}", [P, 512]) for i in range(2)]
            xsc = [mb(f"xsc{i}", [P, BT // P, RW]) for i in range(2)]
            mine = mb("mine", [P, BT // P, K1])
            wrow = mb("wrow", [P, BT // P, K0])
            destf = [mb(f"destf{i}", [P, BT // P]) for i in range(2)]
            desti = [mb(f"desti{i}", [P, BT // P], I32) for i in range(2)]
            ysb = [mb(f"ysb{i}", [P, 512]) for i in range(2)]
            bup = [mb(f"bup{i}", [P, H1 // P]) for i in range(2)]
            bdn = [mb(f"bdn{i}", [P, D]) for i in range(2)]
            wraw = [mb("wraw_up", [P, 2048]), mb("wraw_down", [P, 2048])]
            wup = [mb(f"wup{i}", [P, 2, 2048], F32R) for i in range(2)]
            wdn = [mb(f"wdn{i}", [P, 2, 2048], F32R) for i in range(2)]

        with ExitStack() as scope:
            gat = scope.enter_context(nc.sbuf_tensor("gat", [P, NT, K1 * D], F32))

        weights_in = sem("weights_in")
        ctx_in, ctx_even, ctx_odd = sem("ctx_in"), sem("ctx_even"), sem("ctx_odd")
        dve_step = sem("dve_step")
        setup_done = sem("setup_done")
        dve_turn, sp_turn, pool_turn = sem("dve_turn"), sem("sp_turn"), sem("pool_turn")
        zeroed, gate_exp = sem("zeroed"), sem("gate_exp")
        fold_psum, fold_ready = sem("fold_psum"), sem("fold_ready")
        var_ready, std_ready, xn_ready = sem("var_ready"), sem("std_ready"), sem("xn_ready")
        xt_psum, xnT_ready = sem("xt_psum"), sem("xnT_ready")
        kv_psum, q_psum = sem("kv_psum"), sem("q_psum")
        k_ready, q_ready, v_ready = sem("k_ready"), sem("q_ready"), sem("v_ready")
        scores0, negmax0, probs0 = sem("scores0"), sem("negmax0"), sem("probs0")
        pt0_psum, pt0_act, pt0_dve = sem("pt0_psum"), sem("pt0_act"), sem("pt0_dve")
        o0_psum, o0_ready, attn0 = sem("o0_psum"), sem("o0_ready"), sem("attn0")
        logits_psum, logits_ready = sem("logits_psum"), sem("logits_ready")
        kv1_psum, q1_psum, k1_ready, q1_ready, v1_ready, kz_ready = (
            sem(n) for n in ("kv1_psum", "q1_psum", "k1_ready", "q1_ready", "v1_ready", "kz_ready"))
        scores1, negmax1, probs1 = sem("scores1"), sem("negmax1"), sem("probs1")
        pt1_psum, pt1_act, pt1_dve = sem("pt1_psum"), sem("pt1_act"), sem("pt1_dve")
        ot_psum, ot_taken, o_psum, o_taken = (sem(n) for n in ("ot_psum", "ot_taken", "o_psum", "o_taken"))
        on_psum, on_ready, attn1 = sem("on_psum"), sem("on_ready"), sem("attn1")
        v1_cleared = sem("v1_cleared")
        out_stored = sem("out_stored")
        route = []
        moe = []
        for i in range(2):
            route.append({n: sem(f"{n}_{i}") for n in (
                "sel_ready", "rank_psum", "slots_ready", "table_ready", "scattered", "tails",
                "exp_in", "exp_ready", "gathered0", "gathered1", "gathered2", "gathered3", "combined")})
            moe.append({n: sem(f"{n}_{i}") for n in (
                "up_even", "up_odd", "down_even", "down_odd", "x_even", "x_odd", "bias_even", "bias_odd", "dbias_even", "dbias_odd",
                "x_set", "xt_psum", "x_high", "xT_ready", "up_high", "up_ready", "down_high", "down_ready",
                "up_psum", "relu_ready", "h_raw", "h_ready", "y_psum",
                "y_ready", "y_out", "y_stored")})

        block = ctx.enter_context(nc.Block())
        x_in = A["x"].rearrange("b (t p) d -> p (b t) d", p=P)
        out_v = out.rearrange("b (t p) d -> p (b t) d", p=P)

        def row(ap, n, parts=P):
            return ap.rearrange("(a n) -> a n", a=1).broadcast_to((parts, n)) if parts > 1 else ap.rearrange("(a n) -> a n", a=1)

        loads = [
            (con[:, :], A["con"]),
            (x[:, :, :], x_in),
            (wq0[:, :, :], A["L0_xattn_Wq"].rearrange("(c p) n -> p c n", p=P)),
            (wk0[:, :, :], A["L0_xattn_Wk"].rearrange("(c p) n -> p c n", p=P)),
            (wv0[:, :, :], A["L0_xattn_Wv"].rearrange("(c p) n -> p c n", p=P)),
            (wc0[:, :, :], A["L0_xattn_Wc"].rearrange("(c p) n -> p c n", p=P)),
            (wo0[:, :, :], A["L0_xattn_Wo"].rearrange("(c p) n -> p c n", p=P)),
            (bq0[:, :], A["L0_xattn_bq"].rearrange("(p a) -> p a", a=1)),
            (bk0[:, :], A["L0_xattn_bk"].rearrange("(p a) -> p a", a=1)),
            (bv0[:, :], row(A["L0_xattn_bv"], DH)),
            (bo0[:, :], row(A["L0_xattn_bo"], D, 1)),
            (bc0[:, 0:1], A["L0_xattn_bc"][0:P].rearrange("(p a) -> p a", a=1)),
            (bc0[:, 1:2], A["L0_xattn_bc"][P:D].rearrange("(p a) -> p a", a=1)),
            (gw0[:, :, :], A["gate0T"].rearrange("(c p) n -> p c n", p=P)),
            (eb0[:, :], row(A["L0_ffn_expert_bias"], E0)),
            (wq1[:, :, :], A["L1_xattn_Wq"].rearrange("(c p) n -> p c n", p=P)),
            (wk1[:, :, :], A["L1_xattn_Wk"].rearrange("(c p) n -> p c n", p=P)),
            (wv1[:, :, :], A["L1_xattn_Wv"].rearrange("(c p) n -> p c n", p=P)),
            (wo1[:, :, :], A["L1_xattn_Wo"].rearrange("(c p) n -> p c n", p=P)),
            (bq1[:, :], A["bq1T"]),
            (bk1[:, :], A["bk1T"]),
            (bv1[:, :], row(A["L1_xattn_bv"], D)),
            (bo1[:, :], row(A["L1_xattn_bo"], D)),
            (gw1[:, :, :], A["L1_ffn_Wg"].rearrange("(c p) n -> p c n", p=P)),
        ]

        LAYERS = [dict(E=E0, K=K0, H=H0, NB=NB0, up=A["up0"], dn=A["dn0"]),
                  dict(E=E1, K=K1, H=H1, NB=NB1, up=A["up1"], dn=A["L1_ffn_Wdown"])]

        RAWS = (2, 1)

        SPLITS = {2: [[(0, 0), (0, 1)], [(1, 0), (1, 1)]],
                  4: [[], [(0, 0), (0, 1)], [(1, 0)], [(1, 1)]]}

        def raw(i, which, par):
            w = KC * LAYERS[i]["H"]
            at = par * w if RAWS[i] == 2 else 0
            return wraw[which][:, at:at + w]

        @block.sync
        def _(sp):
            for dst, src in loads:
                sp.dma_start(dst, src).then_inc(weights_in, 16)

            def ctx_load(b, place, s):
                sp.dma_start(ctxT[place][:, :, :], A["ctxT"].rearrange("(c p) n -> p c n", p=P)[:, :, bass.ts(b, S)]).then_inc(s, 16)

            ctx_load(0, 0, ctx_even)
            ctx_load(1, 1, ctx_odd)
            sp.wait_ge(setup_done, 1)

            def zero_rows(row, s):
                sp.dma_start(sorted_x[bass.ds(row, BT), :].rearrange("(p r) d -> p r d", p=P), zeros[:, :, :]).then_inc(s, 16)

            for e in (E0, E1):
                zero_rows(e * ROOM, zeroed)
            for b in range(2, B):
                sp.wait_ge(kv_psum, 2 * (b - 1))
                ctx_load(b, b % 2, (ctx_even, ctx_odd)[b % 2])

            def expert_loads(i):
                L, M, R = LAYERS[i], moe[i], route[i]
                HT, NB = L["H"] // P, L["NB"]
                CH = HT // 2

                def hold(s, value):
                    sp.wait_ge(s, value)
                    sp.sem_inc(sp_turn, 1)

                def expert(j):
                    return sp.value_load(owneri[0:1, bass.ds(j, 1)], min_val=0, max_val=L["E"] - 1)

                def load_x(j, par):
                    if not isinstance(j, int) or j >= 2:
                        hold(M["xt_psum"], j + (-1))
                    row = sp.value_load(starti[0:1, bass.ds(j, 1)], min_val=0, max_val=L["E"] * ROOM)
                    sp.dma_start(xsc[par][:, :, :], sorted_x[bass.ds(row, BT), :].rearrange("(i p) d -> p i d", p=P)).then_inc(M[("x_even", "x_odd")[par]], 16)

                def load_up(j, par):
                    first = isinstance(j, int)
                    e = expert(j)
                    if not first or j >= RAWS[i]:
                        hold(M["up_ready"], 2 * j + (2 - 2 * RAWS[i]))
                    sp.dma_start(raw(i, 0, par).rearrange("p (c n) -> p c n", c=KC),
                                 L["up"][bass.ds(e, 1)].rearrange("a (c p) n -> p (a c) n", p=P)).then_inc(M[("up_even", "up_odd")[par]], 16)

                def load_up_bias(j, par):
                    if i == 1:
                        e = expert(j)
                        if not isinstance(j, int) or j >= 2:
                            hold(M["h_raw"], j * CH)
                        sp.dma_start(bup[par][:, :], A["bup1T"][bass.ds(e, 1)].rearrange("a p n -> p (a n)")).then_inc(M[("bias_even", "bias_odd")[par]], 16)

                def load_down(j, par):
                    e = expert(j)
                    if not isinstance(j, int) or j >= RAWS[i]:
                        hold(M["down_ready"], 2 * j + (2 - 2 * RAWS[i]))
                    sp.dma_start(raw(i, 1, par).rearrange("p (c n) -> p c n", c=HT),
                                 L["dn"][bass.ds(e, 1)].rearrange("a (c p) n -> p (a c) n", p=P)).then_inc(M[("down_even", "down_odd")[par]], 16)

                def load_bias(j, par):
                    if i == 1:
                        e = expert(j)
                        hold(M["y_ready"], j + 1)
                        sp.dma_start(bdn[par][:, :], A["L1_ffn_bdown"][bass.ds(e, 1)].broadcast_to((P, D))).then_inc(M[("dbias_even", "dbias_odd")[par]], 16)

                sp.wait_ge(R["table_ready"], 1)
                for e in range(L["E"]):
                    zero_rows(sp.value_load(placei[0:1, e:e + 1], min_val=0, max_val=L["E"] * ROOM - BT), R["tails"])
                load_up(0, 0)
                load_up_bias(0, 0)
                load_up_bias(1, 1)
                load_down(0, 0)
                sp.wait_ge(R["scattered"], 16 * NT * L["K"])
                sp.wait_ge(R["tails"], 16 * L["E"])
                sp.wait_ge(zeroed, 32)
                load_x(0, 0)
                load_x(1, 1)
                load_bias(0, 0)
                load_up(1, 1)
                load_x(2, 0)
                load_up(2, 0)
                load_down(1, 1)

                def step(s, par, last=False):
                    load_up_bias(s + 2, par)
                    if not last:
                        load_x(s + 3, 1 - par)
                        load_up(s + 3, 1 - par)
                    load_down(s + 2, par)
                    load_bias(s + 1, 1 - par)

                with sp.Fori(0, (NB - 4) // 2) as t:
                    step(2 * t, 0)
                    step(2 * t + 1, 1)
                step(NB - 4, 0)
                step(NB - 3, 1, last=True)
                load_bias(NB - 1, 1)
                sp.wait_ge(M["y_out"], NB + 2)
                for b in range(B):
                    sp.dma_start(gat[:, b * TB:(b + 1) * TB, 0:L["K"] * D],
                                 token_y[BT + b * S * L["K"]:BT + (b + 1) * S * L["K"], :].rearrange(
                                     "(t p k) d -> p t (k d)", p=P, k=L["K"])).then_inc(R[f"gathered{b}"], 16)

            if STOP >= 2:
                expert_loads(0)
            if STOP >= 3:
                sp.wait_ge(route[0]["combined"], 1)
                ctx_load(0, 0, ctx_in)
                with sp.Fori(1, B) as b:
                    sp.wait_ge(k1_ready, 2 * b)
                    sp.sem_inc(sp_turn, 1)
                    sp.wait_ge(v1_ready, 2 * b)
                    sp.sem_inc(sp_turn, 1)
                    ctx_load(b, 0, ctx_in)
            if STOP >= 4:
                expert_loads(1)

        @block.tensor
        def _(pe):
            def ln_turn(n, p, banks):
                pe.wait_ge(xn_ready, n + 1)
                for c in range(KC):
                    for t in range(TB):
                        last = pe.transpose(bank[banks[c]][:, t * P:(t + 1) * P], xnb[p][:, t, c * P:(c + 1) * P], ident)
                    last.then_inc(xt_psum, 1)

            def ln_transposes(n, lo):
                ln_turn(n, 0, (lo, lo + 1))
                pe.wait_ge(xnT_ready, 2 * n + 2)

            def gate(p, gw, E, bk):
                for t in range(TB):
                    for c in range(KC):
                        last = pe.matmul(bank[bk][:, t * E:(t + 1) * E], xnT[p][:, c, t * P:(t + 1) * P], gw[:, c, :],
                                         start=(c == 0), stop=(c == KC - 1))
                last.then_inc(logits_psum, 1)

            def ranks(i, b, p, bk):
                E = LAYERS[i]["E"]
                pe.wait_ge(route[i]["sel_ready"], b + 1)
                for d in range(TB + 1):
                    last = pe.matmul(bank[bk][:, RANKS + d * E:RANKS + (TB + 1) * E], ones_b[:, :] if d else before_b[:, :],
                                     sel[p][:, 0:(TB + 1 - d) * E], start=(d == 0), stop=(d == TB))
                last.then_inc(route[i]["rank_psum"], 1)

            pe.wait_ge(weights_in, 16 * len(loads))
            pe.wait_ge(setup_done, 1)
            for n in range(KC):
                for c in range(KC):
                    last = pe.matmul(bank[n][:, 0:DH], wc0[:, c, n * P:(n + 1) * P], fold, start=(c == 0), stop=(c == KC - 1))
            last.then_inc(fold_psum, 1)
            pe.wait_ge(fold_ready, 1)
            for c in range(KC):
                pe.matmul(bank[2][:, 0:D], wcT[:, c, :], wo0[:, c, :], start=(c == 0), stop=False)
            pe.matmul(bank[2][:, 0:D], con[0:1, C_SEL:C_PLACE], bo0[:, :], start=False, stop=True).then_inc(fold_psum, 1)
            pe.wait_ge(fold_ready, 2)

            with pe.Fori(0, B // 2) as t:
                both = [(2 * t, 0), (2 * t + 1, 1)]
                for b, p in both:
                    pe.wait_ge((ctx_even, ctx_odd)[p], t * 16 + 16)
                    for c in range(KC):
                        last = pe.matmul(bank[4 * p][0:DH, :], wk0[:, c, :], ctxT[p][:, c, :], start=(c == 0), stop=(c == KC - 1))
                    last.then_inc(kv_psum, 1)
                    for k in range(TB):
                        for c in range(KC):
                            last = pe.matmul(bank[4 * p + 1][:, k * DH:(k + 1) * DH], ctxT[p][:, c, k * P:(k + 1) * P], wv0[:, c, :],
                                             start=(c == 0), stop=(c == KC - 1))
                    last.then_inc(kv_psum, 1)
                for b, p in both:
                    ln_turn(4 * t + p, p, (4 * p + 2, 4 * p + 3))
                for b, p in both:
                    pe.wait_ge(k_ready, b + 1)
                    pe.wait_ge(xnT_ready, 2 * (4 * t + p) + 2)
                    for c in range(KC):
                        last = pe.matmul(bank[4 * p][0:DH, :], wq0[:, c, :], xnT[p][:, c, :], start=(c == 0), stop=(c == KC - 1))
                    last.then_inc(q_psum, 1)
                for b, p in both:
                    pe.wait_ge(q_ready, b + 1)
                    pe.wait_ge(v_ready, b + 1)
                    for q in range(TB):
                        pe.matmul(bank[4 * p + q][:, :], att0[p]["qT"][:, q * P:(q + 1) * P], att0[p]["kT"], start=True,
                                  stop=True).then_inc(scores0, 1)
                for b, p in both:
                    for q in range(TB):
                        pe.wait_ge(probs0, 4 * b + q + 1)
                        for k in range(TB):
                            last = pe.transpose(bank[4 * p + q][:, k * P:(k + 1) * P], att0[p]["p"][:, q, k * P:(k + 1) * P], ident)
                        last.then_inc(pt0_psum, 1)
                for b, p in both:
                    pe.wait_ge(pt0_act, 2 * b + 2)
                    pe.wait_ge(pt0_dve, 2 * b + 2)
                    for k in range(TB):
                        last = pe.matmul(bank[4 * p][SLOTW * k:SLOTW * (k + 1), :], att0[p]["v"][:, k, :], att0[p]["pT"][:, k, :],
                                         start=True, stop=True)
                    last.then_inc(o0_psum, 1)
                for b, p in both:
                    pe.wait_ge(o0_ready, b + 1)
                    for q in range(TB):
                        last = pe.matmul(bank[4 * p + 1 + q // 2][:, (q % 2) * D:(q % 2 + 1) * D], att0[p]["oT"][:, q * P:(q + 1) * P],
                                         weff[:, :], start=True, stop=True)
                        if q % 2:
                            last.then_inc(attn0, 1)
                for b, p in both:
                    ln_turn(4 * t + (p + 2), p, (4 * p, 4 * p + 2))
                for b, p in both:
                    pe.wait_ge(xnT_ready, 2 * (4 * t + (p + 2)) + 2)
                    gate(p, gw0, E0, 4 * p + 3)
                for b, p in both:
                    ranks(0, b, p, 4 * p + 3)

            def experts(i):
                L, M, R = LAYERS[i], moe[i], route[i]
                HT, NB = L["H"] // P, L["NB"]
                CH = HT // 2
                PARTS = ((0, 0), (0, 1), (1, 0))
                pe.nop().then_inc(M["y_psum"], 2)
                pe.nop().then_inc(M["up_psum"], 2 * CH)

                def turn(j, par):
                    pe.wait_ge(M["x_set"], j + 1)
                    for c in range(KC):
                        for t in range(2):
                            last = pe.transpose(bank[0][:, c * BT + t * P:c * BT + (t + 1) * P],
                                                xsc[par][:, t, c * P:(c + 1) * P], ident)
                    last.then_inc(M["xt_psum"], 1)

                def up(j, par):
                    pe.wait_ge(M["xT_ready"], j + 1)
                    pe.wait_ge(M["up_ready"], 2 * j + 2)
                    for ch in range(CH):
                        pe.wait_ge(M["h_raw"], j * CH + (ch + 1))
                        for m in range(2):
                            h = 2 * ch + m
                            for c in range(KC):
                                for w, v in PARTS:
                                    last = pe.matmul(bank[1 + ch][:, m * BT:(m + 1) * BT],
                                                     wup[par][:, w, c * L["H"] + h * P:c * L["H"] + (h + 1) * P],
                                                     xT[par][:, v, c * BT:(c + 1) * BT],
                                                     start=(c == 0 and w + v == 0), stop=(c == KC - 1 and w == 1))
                        last.then_inc(M["up_psum"], 1)

                def down(j, par):
                    pe.wait_ge(M["down_ready"], 2 * j + 2)
                    pe.wait_ge(M["h_ready"], j * CH + (CH + 2))
                    pe.wait_ge(M["y_ready"], j + 1)
                    for t in range(2):
                        for h in range(HT):
                            for v, w in PARTS:
                                last = pe.matmul(bank[5 + par][:, t * D:(t + 1) * D],
                                                 hid[par][:, v, h * BT + t * P:h * BT + (t + 1) * P],
                                                 wdn[par][:, w, h * D:(h + 1) * D],
                                                 start=(h == 0 and w + v == 0), stop=(h == HT - 1 and v == 1))
                    last.then_inc(M["y_psum"], 1)

                turn(0, 0)
                up(0, 0)
                turn(1, 1)
                with pe.Fori(0, NB // 2 - 1) as t:
                    up(2 * t + 1, 1)
                    turn(2 * t + 2, 0)
                    down(2 * t, 0)
                    up(2 * t + 2, 0)
                    turn(2 * t + 3, 1)
                    down(2 * t + 1, 1)
                up(NB - 1, 1)
                down(NB - 2, 0)
                down(NB - 1, 1)

            if STOP >= 2:
                experts(0)
            if STOP >= 3:
                pe.nop().then_inc(pt1_psum, 6)
                pe.nop().then_inc(ot_psum, 2)
                with pe.Fori(0, B) as b:
                    pe.wait_ge(ctx_in, b * 16 + 16)
                    for c in range(KC):
                        for kc in range(KC):
                            last = pe.matmul(bank[5 + c][:, :], wk1[:, kc, c * P:(c + 1) * P], ctxT[0][:, kc, :],
                                             start=(kc == 0), stop=(kc == KC - 1))
                        last.then_inc(kv1_psum, 1)
                    for k in range(TB):
                        for kc in range(KC):
                            last = pe.matmul(bank[k // 2][:, (k % 2) * D:(k % 2 + 1) * D], ctxT[0][:, kc, k * P:(k + 1) * P],
                                             wv1[:, kc, :], start=(kc == 0), stop=(kc == KC - 1))
                        if k % 2:
                            last.then_inc(kv1_psum, 1)
                    ln_transposes(2 * b + 2 * B, 3)
                    for c in range(KC):
                        for kc in range(KC):
                            last = pe.matmul(bank[7 if c else 2][:, :], wq1[:, kc, c * P:(c + 1) * P], xnT[0][:, kc, :],
                                             start=(kc == 0), stop=(kc == KC - 1))
                        last.then_inc(q1_psum, 1)
                    pe.wait_ge(q1_ready, 2 * b + 2)
                    pe.wait_ge(k1_ready, 2 * b + 2)
                    pe.wait_ge(v1_ready, 2 * b + 2)

                    def scores(h):
                        c = h // 8
                        pe.wait_ge(kz_ready, b * NH + (h + 1))
                        for part, tiles in enumerate(((3,), (2,), (1, 0))):
                            pe.wait_ge(probs1, b * (3 * NH) + (3 * h + part + 1))
                            at = 0
                            for q in tiles:
                                w = (q + 1) * P
                                pe.matmul(bank[part][:, at:at + w], qT1[:, c, q * P:(q + 1) * P], kz[:, h, 0:w], start=True, stop=False)
                                last = pe.matmul(bank[part][:, at + q * P:at + w], ident_b[:, :], causal_b[:, :], start=False, stop=True)
                                at += w
                            last.then_inc(scores1, 1)

                    def turn_probs(h):
                        pe.wait_ge(probs1, b * (3 * NH) + (3 * h + 6))
                        pe.wait_ge(pt1_dve, b * NH + (h + 1))
                        for k in range(TB):
                            if k == 1:
                                pe.wait_ge(pt1_act, b * (2 * NH) + (2 * h + 2))
                            at = (k == 3) * 256
                            for q in range(k, TB):
                                src = p1[:, h % 2, QOFF[q] + k * P:QOFF[q] + (k + 1) * P]
                                last = pe.transpose(bank[3 + min(k, 2)][:, at + (q - k) * P:at + (q - k + 1) * P], src, ident)
                            if k != 2:
                                last.then_inc(pt1_psum, 1)

                    def values(g):
                        pe.wait_ge(pt1_dve, b * NH + (4 * g + 5))
                        pe.wait_ge(pt1_act, b * (2 * NH) + (8 * g + 10))
                        pe.wait_ge(ot_taken, b * 4 + (g + 1))
                        for k in range(TB):
                            for i in range(HG):
                                last = pe.matmul(bank[6][32 * i:32 * i + 32, k * P:S], v1[:, k, HG * g + i, :],
                                                 pT1[:, (g % 2) * HG + i, QOFF2[k]:QOFF2[k] + S - k * P],
                                                 start=(k == 0), stop=(k == TB - 1))
                        last.then_inc(ot_psum, 1)

                    def turn_out(g):
                        pe.wait_ge(ot_taken, b * 4 + (g + 2))
                        pe.wait_ge(o_taken, b * 4 + (g + 1))
                        for q in range(TB):
                            last = pe.transpose(bank[7][:, q * P:(q + 1) * P], oTs[:, q * P:(q + 1) * P], ident)
                        last.then_inc(o_psum, 1)

                    QOFF = {3: 0, 2: 512, 1: 896, 0: 1152}
                    QOFF2 = {0: 0, 1: 512, 2: 896, 3: 1152}
                    scores(0)
                    for h in range(NH):
                        if h < NH - 1:
                            scores(h + 1)
                        turn_probs(h)
                        if h % HG == 0 and h:
                            values(h // HG - 1)
                        if h % HG == 1 and h > 1:
                            turn_out(h // HG - 1)
                    values(3)
                    turn_out(3)
                    pe.wait_ge(o_taken, b * 4 + 5)
                    for c in range(KC):
                        for q in range(TB):
                            last = pe.transpose(bank[3 + c][:, q * P:(q + 1) * P], o1[:, q, c * P:(c + 1) * P], ident)
                        last.then_inc(on_psum, 1)
                    pe.wait_ge(on_ready, 2 * b + 2)
                    for q in range(TB):
                        for c in range(KC):
                            last = pe.matmul(bank[5 + q // 2][:, (q % 2) * D:(q % 2 + 1) * D], oT1[:, c, q * P:(q + 1) * P],
                                             wo1[:, c, :], start=(c == 0), stop=(c == KC - 1))
                        if q % 2:
                            last.then_inc(attn1, 1)
                    ln_transposes(2 * b + (2 * B + 1), 3)
                    gate(0, gw1, E1, 7)
                    ranks(1, b, 0, 7)
            if STOP >= 4:
                experts(1)

        @block.scalar
        def _(act):
            def ln_std(n, p=0):
                act.wait_ge(var_ready, n + 1)
                act.activation(std[p][:, :], mv[p][:, :, 1], ACT.Sqrt, bias=eps[:, :]).then_inc(std_ready, 1)

            def ln_turned(n, banks, p=0):
                for c in range(KC):
                    act.wait_ge(xt_psum, 2 * n + (c + 1))
                    act.activation(xnT[p][:, c, :], bank[banks[c]][:, :], ACT.Copy).then_inc(xnT_ready, 1)

            act.wait_ge(setup_done, 1)
            with act.Fori(0, B // 2) as t:
                both = [(2 * t, 0), (2 * t + 1, 1)]
                for b, p in both:
                    act.wait_ge(kv_psum, 2 * b + 1)
                    act.activation(att0[p]["kT"], bank[4 * p][0:DH, :], ACT.Identity, bias=bk0[:, :]).then_inc(k_ready, 1)
                for b, p in both:
                    ln_std(4 * t + p, p)
                for b, p in both:
                    ln_turned(4 * t + p, (4 * p + 2, 4 * p + 3), p)
                for b, p in both:
                    act.wait_ge(q_psum, b + 1)
                    act.activation(att0[p]["qT"], bank[4 * p][0:DH, :], ACT.Identity, bias=bq0[:, :], scale=0.25).then_inc(q_ready, 1)
                for b, p in both:
                    for q in range(TB):
                        act.wait_ge(negmax0, 4 * b + q + 1)
                        act.activation(att0[p]["p"][:, q, :], bank[4 * p + q][:, :], ACT.Exp, bias=negmax[:, p, q:q + 1],
                                       accum_out=rowsum[p][:, q:q + 1]).then_inc(probs0, 1)
                for b, p in both:
                    for q in range(2):
                        act.wait_ge(pt0_psum, 4 * b + q + 1)
                        act.activation(att0[p]["pT"][:, :, q * P:(q + 1) * P], bank[4 * p + q][:, :].rearrange("p (k q) -> p k q", k=TB),
                                       ACT.Copy).then_inc(pt0_act, 1)
                for b, p in both:
                    act.wait_ge(o0_psum, b + 1)
                    act.activation(att0[p]["oT"], bank[4 * p][:, :], ACT.Copy).then_inc(o0_ready, 1)
                for b, p in both:
                    ln_std(4 * t + (p + 2), p)
                for b, p in both:
                    ln_turned(4 * t + (p + 2), (4 * p, 4 * p + 2), p)
                for b, p in both:
                    act.wait_ge(logits_psum, b + 1)
                    act.activation(keys[p][:, :, 0:E0], bank[4 * p + 3][:, 0:TB * E0].rearrange("p (t e) -> p t e", t=TB), ACT.Exp,
                                   scale=-1.0).then_inc(gate_exp, 1)

            def experts(i):
                L, M = LAYERS[i], moe[i]
                HT, NB = L["H"] // P, L["NB"]
                CH = HT // 2
                HALF = KC * L["H"] // 2

                def high_up(j, n, par, half):
                    if half == 0:
                        act.wait_ge(M[("up_even", "up_odd")[par]], n * 16 + 16)
                        act.wait_ge(M["up_psum"], j * CH + CH)
                    cols = slice(half * HALF, (half + 1) * HALF)
                    act.activation(wup[par][:, 0, cols], raw(i, 0, par)[:, cols], ACT.Copy).then_inc(M["up_high"], 1)

                def high_down(j, n, par, half):
                    if half == 0:
                        act.wait_ge(M[("down_even", "down_odd")[par]], n * 16 + 16)
                        act.wait_ge(M["y_psum"], j + 1)
                    cols = slice(half * HALF, (half + 1) * HALF)
                    act.activation(wdn[par][:, 0, cols], raw(i, 1, par)[:, cols], ACT.Copy).then_inc(M["down_high"], 1)

                def high_x(j, par):
                    act.wait_ge(M["xt_psum"], j + 1)
                    act.activation(xT[par][:, 0, :], bank[0][:, :], ACT.Copy).then_inc(M["x_high"], 1)

                def hidden(j, n, par, ch):
                    act.wait_ge(M["up_psum"], j * CH + (2 * CH + ch + 1))
                    act.wait_ge(M["h_ready"], j * CH + (ch + 1))
                    if i == 0:
                        act.activation(hraw[ch % 2][:, :], bank[1 + ch][:, :], ACT.Relu).then_inc(M["relu_ready"], 1)
                        act.wait_ge(M["relu_ready"], j * CH + (ch + 1))
                        act.activation(hraw[ch % 2][:, :], hraw[ch % 2][:, :], ACT.Square).then_inc(M["h_raw"], 1)
                    else:
                        if ch == 0:
                            act.wait_ge(M[("bias_even", "bias_odd")[par]], n * 16 + 16)
                        for m in range(2):
                            h = 2 * ch + m
                            last = act.activation(hraw[ch % 2][:, m * BT:(m + 1) * BT], bank[1 + ch][:, m * BT:(m + 1) * BT],
                                                  ACT.Gelu, bias=bup[par][:, h:h + 1])
                        last.then_inc(M["h_raw"], 1)

                def step(j, n, par, more=True):
                    m = n if par else n + 1
                    for ch in range(CH):
                        for down, half in SPLITS[CH][ch]:
                            if down:
                                high_down(j + 1, n, 1 - par, half)
                            elif more:
                                high_up(j + 2, m, par, half)
                        hidden(j + 1, n, 1 - par, ch)
                        if more and ch == CH // 2 - 1:
                            high_x(j + 2, par)

                act.nop().then_inc(M["h_raw"], CH)
                high_up(0, 0, 0, 0)
                high_up(0, 0, 0, 1)
                high_x(0, 0)
                step(-1, 0, 1)
                with act.Fori(0, NB // 2 - 1) as t:
                    step(2 * t, t, 0)
                    step(2 * t + 1, t + 1, 1)
                step(NB - 2, NB // 2 - 1, 0, more=False)

            if STOP >= 2:
                experts(0)
            if STOP >= 3:
                act.nop().then_inc(probs1, 3)
                act.nop().then_inc(pt1_act, 2)
                act.nop().then_inc(ot_taken, 1)
                with act.Fori(0, B) as b:
                    for c in range(KC):
                        act.wait_ge(kv1_psum, 4 * b + (c + 1))
                        act.activation(kT1[:, c, :], bank[5 + c][:, :], ACT.Identity, bias=bk1[:, c:c + 1]).then_inc(k1_ready, 1)
                    ln_std(2 * b + 2 * B)
                    ln_turned(2 * b + 2 * B, (3, 4))
                    for c in range(KC):
                        act.wait_ge(q1_psum, 2 * b + (c + 1))
                        act.activation(qT1[:, c, :], bank[7 if c else 2][:, :], ACT.Identity, bias=bq1[:, c:c + 1],
                                       scale=0.25).then_inc(q1_ready, 1)
                    QOFF = {3: 0, 2: 512, 1: 896, 0: 1152}

                    def exps(h):
                        act.wait_ge(pt1_psum, b * (3 * NH) + (3 * h + 3))
                        for part, tiles in enumerate(((3,), (2,), (1, 0))):
                            act.wait_ge(negmax1, b * (3 * NH) + (3 * h + part + 1))
                            at = 0
                            for q in tiles:
                                w = (q + 1) * P
                                last = act.activation(p1[:, h % 2, QOFF[q]:QOFF[q] + w], bank[part][:, at:at + w], ACT.Exp,
                                                      bias=negmax[:, h % 2, q:q + 1])
                                at += w
                            last.then_inc(probs1, 1)

                    def take_probs(h):
                        s = (h // HG % 2) * HG + h % HG
                        act.wait_ge(ot_psum, b * 4 + (h // HG + 1))
                        for part in (1, 2):
                            act.wait_ge(pt1_psum, b * (3 * NH) + (3 * h + part + 7))
                            at = 512 + (part - 1) * 384
                            act.activation(pT1[:, s, at:at + 384], bank[3 + part][:, 0:384], ACT.Copy).then_inc(pt1_act, 1)

                    def take_out(g):
                        act.wait_ge(ot_psum, b * 4 + (g + 3))
                        act.activation(oTs[:, :], bank[6][:, :], ACT.Copy).then_inc(ot_taken, 1)

                    exps(0)
                    for h in range(NH):
                        if h < NH - 1:
                            exps(h + 1)
                        take_probs(h)
                        if h % HG == 0 and h:
                            take_out(h // HG - 1)
                    take_out(3)
                    for c in range(KC):
                        act.wait_ge(on_psum, 2 * b + (c + 1))
                        act.activation(oT1[:, c, :], bank[3 + c][:, :], ACT.Copy).then_inc(on_ready, 1)
                    ln_std(2 * b + (2 * B + 1))
                    ln_turned(2 * b + (2 * B + 1), (3, 4))
            if STOP >= 4:
                act.wait_ge(route[1]["exp_in"], 1)
                act.activation(wtop[:, :, :], wtop[:, :, :], ACT.Exp).then_inc(route[1]["exp_ready"], 1)
                experts(1)
            for b in range(B):
                act.wait_ge(route[1]["combined"], (b + 1) * TB)
                act.dma_start(out_v[:, b * TB:(b + 1) * TB, :], x[:, b * TB:(b + 1) * TB, :]).then_inc(out_stored, 16)
            act.wait_ge(out_stored, 16 * B)

        @block.gpsimd
        def _(pool):
            def scatter(i):
                K, R = LAYERS[i]["K"], route[i]
                for b in range(B):
                    pool.wait_ge(R["slots_ready"], b + 1)
                    for t in range(b * TB, (b + 1) * TB):
                        for k in range(K):
                            pool.indirect_dma_start(sorted_x, bass.IndirectOffsetOnAxis(sloti[:, k, t:t + 1].bitcast(U32), 0),
                                                    xn[:, t, :], None).then_inc(R["scattered"], 16)

            def results(i):
                M = moe[i]
                pool.sem_inc(M["y_out"], 2)
                with pool.Fori(0, LAYERS[i]["NB"] // 2) as t:
                    for par in range(2):
                        pool.wait_ge(M["y_ready"], 2 * t + (par + 3))
                        pool.sem_inc(pool_turn, 1)
                        for r in range(2):
                            pool.indirect_dma_start(token_y, bass.IndirectOffsetOnAxis(desti[par][:, r:r + 1].bitcast(U32), 0),
                                                    ysb[par][:, r * D:(r + 1) * D], None).then_inc(M["y_stored"], 16)
                        pool.wait_ge(M["y_stored"], 64 * t + 32 * (par + 1))
                        pool.sem_inc(M["y_out"], 1)

            if STOP >= 2:
                scatter(0)
                results(0)
            if STOP >= 4:
                scatter(1)
                results(1)

        @block.vector
        def _(dve):
            chn = Chain(dve, dve_step)

            def norm_stats(p, src):
                dve.sem_inc(dve_turn, 1)
                for t in range(TB):
                    last = dve.bn_stats(stats[p][:, t, :], src(t))
                chn.link(last)
                dve.sem_inc(dve_turn, 1)
                for t in range(TB):
                    last = dve.bn_aggr(mv[p][:, t, :], stats[p][:, t, :])
                last.then_inc(var_ready, 1)

            def norm(n, p, src, also=None):
                dve.wait_ge(std_ready, n + 1)
                chn.link(dve.reciprocal(rstd[p][:, :], std[p][:, :]))
                for dst in [also] * (also is not None) + [lambda t: xnb[p][:, t, :]]:
                    for t in range(TB):
                        last = dve.tensor_scalar(dst(t), src(t), mv[p][:, t, 0:1], rstd[p][:, t:t + 1], ALU.subtract, ALU.mult)
                last.then_inc(xn_ready, 1)

            def tile_of(b):
                return lambda t: x[:, bass.ds(b * TB + t, 1), :].rearrange("p a d -> p (a d)")

            def row_of(b):
                return lambda t: xn[:, bass.ds(b * TB + t, 1), 0:D].rearrange("p a d -> p (a d)")

            def choose(i, b, p, bk):
                L, R = LAYERS[i], route[i]
                E, K = L["E"], L["K"]
                ts = bass.ds(b * TB, TB)
                lg, ky, wk = (t[:, :, 0:E] for t in (logits[p], keys[p], work))
                hots = [h[p][:, :, 0:E] for h in hot]
                se = sel[p][:, 0:TB * E].rearrange("p (t e) -> p t e", t=TB)
                psum = bank[bk][:, 0:TB * E].rearrange("p (t e) -> p t e", t=TB)
                if i == 0:
                    dve.wait_ge(gate_exp, b + 1)
                    chn.link(dve.tensor_scalar(ky, ky, 1.0, None, ALU.add))
                    chn.link(dve.reciprocal(ky, ky))
                    chn.link(dve.tensor_tensor(lg, ky, eb0[:, :].unsqueeze(1).broadcast_to((P, TB, E)), ALU.add))
                else:
                    dve.wait_ge(logits_psum, b + (B + 1))
                    chn.link(dve.tensor_copy(lg, psum))
                dve.sem_inc(dve_turn, 1)
                for t in range(TB):
                    last = dve.max(top8[p][:, t, :], lg[:, t, :])
                chn.link(last)
                dve.sem_inc(dve_turn, 1)
                for t in range(TB):
                    last = dve.max_index(idx8[p][:, t, :], top8[p][:, t, :], lg[:, t, :])
                if i == 1:
                    dve.tensor_copy(topk[:, ts, :], top8[p][:, :, 0:K1])
                chn.link(last)
                dve.tensor_copy(xn[:, ts, R_TOK], con[:, bass.ds(b * TB + (C_TOK + i * NT), TB)])
                chn.link(dve.tensor_copy(idxf[p][:, :, :], idx8[p][:, :, 0:K1]))
                chn.link(dve.tensor_scalar(xn[:, ts, R_EXP:R_EXP + K], idxf[p][:, :, 0:K], 1.0, None, ALU.add))
                for k in range(K):
                    last = dve.tensor_tensor(hots[k], con[:, C_IE:C_IE + E].unsqueeze(1).broadcast_to((P, TB, E)),
                                             xn[:, ts, R_EXP + k:R_EXP + k + 1].broadcast_to((P, TB, E)), ALU.is_equal)
                chn.link(last)
                chn.link(dve.tensor_tensor(se, hots[0], hots[1], ALU.add))
                if K == 3:
                    chn.link(dve.tensor_tensor(se, se, hots[2], ALU.add))
                dve.nop().then_inc(R["sel_ready"], 1)
                if i == 0:
                    for k in range(K):
                        chn.link(dve.tensor_tensor(wk, hots[k], ky, ALU.mult))
                        chn.link(dve.tensor_reduce(xn[:, ts, R_W + k], wk, AX.X, ALU.add))

            def places(i, b, p, bk):
                L, R = LAYERS[i], route[i]
                E, K = L["E"], L["K"]
                ts = bass.ds(b * TB, TB)
                sl, wk = slot[:, :, 0:E], work[:, :, 0:E]
                hots = [h[p][:, :, 0:E] for h in hot]
                dve.wait_ge(R["rank_psum"], b + 1)
                dve.sem_inc(dve_turn, 1)
                chn.link(dve.tensor_tensor(sl, bank[bk][:, RANKS:RANKS + TB * E].rearrange("p (t e) -> p t e", t=TB),
                                           place[:, 0:E].unsqueeze(1).broadcast_to((P, TB, E)), ALU.add))
                for k in range(K):
                    chn.link(dve.tensor_tensor(wk, hots[k], sl, ALU.mult))
                    chn.link(dve.tensor_reduce(slotf[:, k, :], wk, AX.X, ALU.add))
                dve.tensor_copy(sloti[:, 0:K, ts], slotf[:, 0:K, :]).then_inc(R["slots_ready"], 1)
                chn.link(dve.tensor_tensor(place[:, 0:E], bank[bk][:, RANKS + TB * E:RANKS + (TB + 1) * E], place[:, 0:E], ALU.add))

            def blocks(i):
                L, R = LAYERS[i], route[i]
                E, K, NB = L["E"], L["K"], L["NB"]
                dve.tensor_copy(placei[:, 0:E], place[0:1, 0:E])
                chn.link(dve.tensor_tensor(nblk[:, 0:E], place[:, 0:E], con[:, C_PLACE:C_PLACE + E], ALU.subtract))
                chn.link(dve.tensor_scalar(nblki[:, 0:E], nblk[:, 0:E], 1.0 / BT, (BT / 2 - 0.5) / BT, ALU.mult, ALU.add))
                dve.tensor_copy(nblk[:, 0:E], nblki[:, 0:E])
                chn.link(dve.tensor_copy(upto[0][:, 8:8 + E], nblki[:, 0:E]))
                for n, d in enumerate((1, 2, 4, 8)):
                    old, new = upto[n % 2], upto[1 - n % 2]
                    chn.link(dve.tensor_tensor(new[:, 8:8 + E], old[:, 8:8 + E], old[:, 8 - d:8 + E - d], ALU.add))
                pa = past[:, 0:NB, 0:E]
                chn.link(dve.tensor_tensor(pa, con[:, C_IB:C_IB + NB].unsqueeze(2).broadcast_to((P, NB, E)),
                                           upto[0][:, 8:8 + E].unsqueeze(1).broadcast_to((P, NB, E)), ALU.is_ge))
                chn.link(dve.tensor_reduce(owner[:, 0:NB], pa, AX.X, ALU.add))
                dve.tensor_scalar(owneri[:, 0:NB], owner[0:1, 0:NB], float(E - 1), None, ALU.min)
                chn.link(dve.tensor_tensor(pa, pa, nblk[:, 0:E].unsqueeze(1).broadcast_to((P, NB, E)), ALU.mult))
                chn.link(dve.tensor_reduce(start[:, 0:NB], pa, AX.X, ALU.add))
                chn.link(dve.tensor_tensor(start[:, 0:NB], con[:, C_IB:C_IB + NB], start[:, 0:NB], ALU.subtract))
                chn.link(dve.tensor_scalar(start[:, 0:NB], start[:, 0:NB], float(BT), None, ALU.mult))
                chn.link(dve.scalar_tensor_tensor(start[:, 0:NB], owner[:, 0:NB], float(ROOM), start[:, 0:NB], ALU.mult, ALU.add))
                dve.tensor_scalar(starti[:, 0:NB], start[0:1, 0:NB], float(E * ROOM), None, ALU.min).then_inc(R["table_ready"], 1)
                chn.link(dve.tensor_scalar(owner[:, 0:NB], owner[:, 0:NB], 1.0, None, ALU.add))
                if i == 1:
                    for k in range(K):
                        last = dve.tensor_tensor(wtop[:, k, :], topk[:, :, k], topk[:, :, 0], ALU.subtract)
                    last.then_inc(R["exp_in"], 1)
                    dve.wait_ge(R["exp_ready"], 1)
                    chn.link(dve.tensor_tensor(wsum[:, :], wtop[:, 0, :], wtop[:, 1, :], ALU.add))
                    chn.link(dve.tensor_tensor(wsum[:, :], wsum[:, :], wtop[:, 2, :], ALU.add))
                    chn.link(dve.reciprocal(wsum[:, :], wsum[:, :]))
                    chn.link(dve.tensor_tensor(wtop[:, :, :], wtop[:, :, :], wsum[:, :].unsqueeze(1).broadcast_to((P, K1, NT)), ALU.mult))
                else:
                    dve.tensor_copy(place[:, :], con[:, C_PLACE:C_TOK])

            dve.memset(eps[:, :], EPS)
            for u in upto:
                dve.memset(u[:, :], 0.0)
            dve.memset(xn[:, :, R_TOK:RW], 0.0)
            chn.link(dve.memset(zeros[:, :, :], 0.0))
            dve.memset(wcT[:, :, :], 0.0)
            for p in range(2):
                dve.memset(sel[p][:, :], 0.0)
                last = dve.memset(att0[p]["v"], 0.0)
            chn.link(last)
            for p in range(2):
                dve.memset(att0[p]["v"][:, :, DH:DH + 1], 1.0)
            dve.wait_ge(weights_in, 16 * len(loads))
            dve.tensor_copy(place[:, :], con[:, C_PLACE:C_TOK])
            dve.tensor_copy(zeros[:, :, R_TOK], con[:, C_SPARE:C_END])
            dve.tensor_copy(ident_b[:, :], ident)
            dve.tensor_copy(before_b[:, :], before)
            dve.tensor_copy(ones_b[:, :], ones)
            dve.tensor_copy(causal_b[:, :], con[:, C_CAUSAL:C_HEAD])
            dve.tensor_scalar(bq1[:, :], bq1[:, :], 0.25, None, ALU.mult)
            dve.tensor_scalar(bq0[:, :], bq0[:, :], 0.25, None, ALU.mult).then_inc(setup_done, 1)
            dve.wait_ge(fold_psum, 1)
            for c in range(KC):
                for k in range(TB):
                    dve.tensor_copy(wcT[:, c, k * SLOTW + DH:k * SLOTW + DH + 1], bc0[:, c:c + 1])
                    last = dve.tensor_copy(wcT[:, c, k * SLOTW:k * SLOTW + DH], bank[c][:, 0:DH])
            last.then_inc(fold_ready, 1)
            dve.wait_ge(fold_psum, 2)
            dve.tensor_copy(weff[:, :], bank[2][:, 0:D]).then_inc(fold_ready, 1)

            with dve.Fori(0, B // 2) as t:
                chn.enter(t, STEPS_ATTN0)
                both = [(2 * t, 0), (2 * t + 1, 1)]
                for b, p in both:
                    norm_stats(p, tile_of(b))
                for b, p in both:
                    norm(4 * t + p, p, tile_of(b))
                for b, p in both:
                    dve.wait_ge(kv_psum, 2 * b + 2)
                    dve.tensor_tensor(att0[p]["v"][:, :, 0:DH], bank[4 * p + 1][:, 0:TB * DH].rearrange("p (k d) -> p k d", k=TB),
                                      bv0[:, :].unsqueeze(1).broadcast_to((P, TB, DH)), ALU.add).then_inc(v_ready, 1)
                for b, p in both:
                    for q in range(TB):
                        dve.wait_ge(scores0, 4 * b + q + 1)
                        dve.tensor_reduce(negmax[:, p, q:q + 1], bank[4 * p + q][:, :], AX.X, ALU.max, negate=True).then_inc(negmax0, 1)
                for b, p in both:
                    for q in range(2, 4):
                        dve.wait_ge(pt0_psum, 4 * b + q + 1)
                        dve.tensor_copy(att0[p]["pT"][:, :, q * P:(q + 1) * P],
                                        bank[4 * p + q][:, :].rearrange("p (k q) -> p k q", k=TB)).then_inc(pt0_dve, 1)
                for b, p in both:
                    dve.wait_ge(probs0, 4 * b + 4)
                    last = dve.reciprocal(rinv[p][:, :], rowsum[p][:, :])
                chn.link(last)
                for b, p in both:
                    tile = tile_of(b)
                    for q in range(TB):
                        if q % 2 == 0:
                            dve.wait_ge(attn0, 2 * b + (q // 2 + 1))
                        last = dve.scalar_tensor_tensor(tile(q), bank[4 * p + 1 + q // 2][:, (q % 2) * D:(q % 2 + 1) * D],
                                                        rinv[p][:, q:q + 1], tile(q), ALU.mult, ALU.add)
                    chn.link(last)
                    norm_stats(p, tile)
                for b, p in both:
                    norm(4 * t + (p + 2), p, tile_of(b), row_of(b))
                for b, p in both:
                    choose(0, b, p, 4 * p + 3)
                for b, p in both:
                    places(0, b, p, 4 * p + 3)
            chn.leave(B // 2)

            def experts(i):
                L, M, R = LAYERS[i], moe[i], route[i]
                HT, NB = L["H"] // P, L["NB"]
                CH = HT // 2
                HALF = KC * L["H"] // 2
                dve.nop().then_inc(M["y_ready"], 2)
                dve.nop().then_inc(M["h_ready"], 2)

                def low_up(j, par, half):
                    cols = slice(half * HALF, (half + 1) * HALF)
                    dve.wait_ge(M["up_high"], 2 * j + (half + 1))
                    dve.tensor_tensor(wup[par][:, 1, cols], raw(i, 0, par)[:, cols], wup[par][:, 0, cols].bitcast(F32),
                                      ALU.subtract).then_inc(M["up_ready"], 1)

                def low_down(j, par, half):
                    cols = slice(half * HALF, (half + 1) * HALF)
                    dve.wait_ge(M["down_high"], 2 * j + (half + 1))
                    dve.tensor_tensor(wdn[par][:, 1, cols], raw(i, 1, par)[:, cols], wdn[par][:, 0, cols].bitcast(F32),
                                      ALU.subtract).then_inc(M["down_ready"], 1)

                def low_x(j, par):
                    dve.wait_ge(M["x_high"], j + 1)
                    dve.tensor_tensor(xT[par][:, 1, :], bank[0][:, :], xT[par][:, 0, :].bitcast(F32), ALU.subtract).then_inc(M["xT_ready"], 1)

                def hidden(j, par, ch):
                    cols = slice(ch * 512, (ch + 1) * 512)
                    dve.wait_ge(M["h_raw"], j * CH + (CH + ch + 1))
                    dve.wait_ge(M["y_psum"], j + 1)
                    chn.link(dve.tensor_copy(hid[par][:, 0, cols], hraw[ch % 2][:, :]))
                    dve.tensor_tensor(hid[par][:, 1, cols], hraw[ch % 2][:, :], hid[par][:, 0, cols].bitcast(F32),
                                      ALU.subtract).then_inc(M["h_ready"], 1)

                def set_dest(j, par):
                    dve.wait_ge(M["y_out"], j + 1)
                    dve.sem_inc(dve_turn, 1)
                    dve.tensor_copy(desti[par][:, :], destf[par][:, :])

                def set_x(j, n, par, first=False):
                    if not first:
                        set_dest(j + (-2), par)
                    dve.wait_ge(M[("x_even", "x_odd")[par]], n * 16 + 16)
                    dve.sem_inc(dve_turn, 1)
                    chn.link(dve.tensor_tensor(mine[:, :, :], xsc[par][:, :, R_EXP:R_EXP + K1],
                                               owner[:, bass.ds(j, 1)].unsqueeze(2).broadcast_to((P, 2, K1)), ALU.is_equal))
                    last = dve.tensor_tensor(destf[par][:, :], mine[:, :, 1], xsc[par][:, :, R_TOK], ALU.add)
                    if i == 0:
                        chn.link(dve.tensor_tensor(wrow[:, :, :], mine[:, :, 0:K0], xsc[par][:, :, R_W:R_W + K0], ALU.mult))
                        chn.link(dve.tensor_tensor(wrow[:, :, 0], wrow[:, :, 0], wrow[:, :, 1], ALU.add))
                        dve.tensor_tensor(xsc[par][:, :, 0:D], xsc[par][:, :, 0:D],
                                          wrow[:, :, 0:1].broadcast_to((P, 2, D)), ALU.mult).then_inc(M["x_set"], 1)
                    else:
                        chn.link(last)
                        dve.scalar_tensor_tensor(destf[par][:, :], mine[:, :, 2], 2.0, destf[par][:, :], ALU.mult,
                                                 ALU.add).then_inc(M["x_set"], 1)

                def take_y(j, n, par):
                    dve.wait_ge(M["y_psum"], j + 3)
                    if i == 0:
                        last = dve.tensor_copy(ysb[par][:, :], bank[5 + par][:, :])
                    else:
                        dve.wait_ge(M[("dbias_even", "dbias_odd")[par]], n * 16 + 16)
                        last = dve.tensor_tensor(ysb[par][:, :].rearrange("p (i d) -> p i d", i=2),
                                                 bank[5 + par][:, :].rearrange("p (i d) -> p i d", i=2),
                                                 bdn[par][:, :].unsqueeze(1).broadcast_to((P, 2, D)), ALU.add)
                    last.then_inc(M["y_ready"], 1)

                def step(j, n, par, first=False, taken=True, more=True):
                    if more:
                        set_x(j + 2, n + 1, par, first=first)
                    if taken:
                        take_y(j + (-1), n if par else n + (-1), 1 - par)
                    if not more:
                        set_dest(j, par)
                    for ch in range(CH):
                        for down, half in SPLITS[CH][ch]:
                            if down:
                                low_down(j + 1, 1 - par, half)
                            elif more:
                                low_up(j + 2, par, half)
                        hidden(j + 1, 1 - par, ch)
                        if more and ch == CH // 2 - 1:
                            low_x(j + 2, par)

                set_x(0, 0, 0, first=True)
                low_up(0, 0, 0)
                low_up(0, 0, 1)
                low_x(0, 0)
                step(-1, -1, 1, first=True, taken=False)
                step(0, 0, 0, taken=False)
                step(1, 0, 1)
                with dve.Fori(1, NB // 2 - 1) as t:
                    chn.enter(t + (-1), 2 * (CH + (3 if i == 0 else 2)))
                    step(2 * t, t, 0)
                    step(2 * t + 1, t, 1)
                chn.leave(NB // 2 - 2)
                step(NB - 2, NB // 2 - 1, 0, more=False)
                take_y(NB - 2, NB // 2 - 1, 0)
                set_dest(NB - 1, 1)
                take_y(NB - 1, NB // 2 - 1, 1)

            def combine(i):
                L, R = LAYERS[i], route[i]
                K = L["K"]
                for t in range(NT):
                    if t % TB == 0:
                        dve.wait_ge(R[f"gathered{t // TB}"], 16)
                    for k in range(K):
                        g = gat[:, t, k * D:(k + 1) * D]
                        if i == 0:
                            last = dve.tensor_tensor(x[:, t, :], x[:, t, :], g, ALU.add)
                        else:
                            last = dve.scalar_tensor_tensor(x[:, t, :], g, wtop[:, k, t:t + 1], x[:, t, :], ALU.mult, ALU.add)
                        if k < K - 1:
                            chn.link(last)
                    last.then_inc(R["combined"], 1)
                dve.wait_ge(R["combined"], NT)

            if STOP >= 2:
                blocks(0)
                experts(0)
                combine(0)
            if STOP >= 3:
                dve.memset(v1[:, :, :, :], 0.0).then_inc(v1_cleared, 1)
                dve.wait_ge(v1_cleared, 1)
                dve.memset(v1[:, :, :, DH:DH + 1], 1.0)
                dve.nop().then_inc(pt1_dve, 1)
                dve.nop().then_inc(o_taken, 1)
                with dve.Fori(0, B) as b:
                    chn.enter(b, STEPS_ATTN1)
                    tile = tile_of(b)
                    norm_stats(0, tile)
                    norm(2 * b + 2 * B, 0, tile)
                    for k in range(2):
                        dve.wait_ge(kv1_psum, 4 * b + (3 + k))
                        for j in range(2):
                            last = dve.tensor_tensor(v1[:, 2 * k + j, :, 0:DH],
                                                     bank[k][:, j * D:(j + 1) * D].rearrange("p (h d) -> p h d", h=NH),
                                                     bv1[:, :].rearrange("p (h d) -> p h d", h=NH), ALU.add)
                        last.then_inc(v1_ready, 1)
                    dve.wait_ge(k1_ready, 2 * b + 2)
                    for h in range(NH):
                        dve.tensor_scalar(kz[:, h, :], kT1[:, h // 8, :], headmask[:, h % 8:h % 8 + 1], None, ALU.mult).then_inc(kz_ready, 1)

                    def maxima(h):
                        for part, tiles in enumerate(((3,), (2,), (1, 0))):
                            dve.wait_ge(scores1, b * (3 * NH) + (3 * h + part + 1))
                            at = 0
                            for q in tiles:
                                w = (q + 1) * P
                                last = dve.tensor_reduce(negmax[:, h % 2, q:q + 1], bank[part][:, at:at + w], AX.X, ALU.max, negate=True)
                                at += w
                            last.then_inc(negmax1, 1)

                    def take_probs(h):
                        s = (h // HG % 2) * HG + h % HG
                        dve.wait_ge(ot_psum, b * 4 + (h // HG + 1))
                        dve.wait_ge(pt1_psum, b * (3 * NH) + (3 * h + 7))
                        dve.tensor_copy(pT1[:, s, 0:512], bank[3][:, :]).then_inc(pt1_dve, 1)

                    def normalise(g):
                        dve.wait_ge(o_psum, b * 4 + (g + 1))
                        o = bank[7][:, :].rearrange("p (q i d) -> p q i d", q=TB, i=HG)
                        chn.link(dve.reciprocal(orec[:, :, :], o[:, :, :, DH]))
                        dve.tensor_tensor(o1[:, :, g * HG * DH:(g + 1) * HG * DH].rearrange("p q (i d) -> p q i d", i=HG),
                                          o[:, :, :, 0:DH], orec[:, :, :].unsqueeze(3).broadcast_to((P, TB, HG, DH)),
                                          ALU.mult).then_inc(o_taken, 1)

                    maxima(0)
                    for h in range(NH):
                        if h < NH - 1:
                            maxima(h + 1)
                        take_probs(h)
                        if h % HG == 1 and h > 1:
                            normalise(h // HG - 1)
                    normalise(3)
                    for q in range(TB):
                        if q % 2 == 0:
                            dve.wait_ge(attn1, 2 * b + (q // 2 + 1))
                        last = dve.tensor_tensor(tile(q), bank[5 + q // 2][:, (q % 2) * D:(q % 2 + 1) * D], tile(q), ALU.add)
                    chn.link(last)
                    for q in range(TB):
                        last = dve.tensor_tensor(tile(q), tile(q), bo1[:, :], ALU.add)
                    chn.link(last)
                    norm_stats(0, tile)
                    norm(2 * b + (2 * B + 1), 0, tile, row_of(b))
                    choose(1, b, 0, 7)
                    places(1, b, 0, 7)
                chn.leave(B)
            if STOP >= 4:
                blocks(1)
                experts(1)
                combine(1)


STEPS_ATTN0 = 49
STEPS_ATTN1 = 26


def kernel(**inputs):
    import numpy as np
    import concourse.bacc as bacc
    from concourse import mybir as mb
    from concourse.bass_utils import run_bass_kernel_spmd as run

    a = {k: np.ascontiguousarray(v) for k, v in inputs.items()}
    a["con"] = constants()
    a["ctxT"] = np.ascontiguousarray(a.pop("ctx_1024").reshape(B * S, D).T)
    a["gate0T"] = np.ascontiguousarray(a.pop("L0_ffn_gate_w").T)
    a["up0"] = np.ascontiguousarray(a.pop("L0_ffn_w_up").transpose(0, 2, 1))
    a["dn0"] = np.ascontiguousarray(a.pop("L0_ffn_w_down").transpose(0, 2, 1))
    a["up1"] = a.pop("L1_ffn_Wup")
    a["bup1T"] = np.ascontiguousarray(a.pop("L1_ffn_bup").reshape(E1, H1 // P, P).transpose(0, 2, 1))
    a["bq1T"] = np.ascontiguousarray(a.pop("L1_xattn_bq").reshape(KC, P).T)
    a["bk1T"] = np.ascontiguousarray(a.pop("L1_xattn_bk").reshape(KC, P).T)

    nc = bacc.Bacc("TRN2", target_bir_lowering=False, num_devices=1)
    aps = {k: nc.dram_tensor(f"in_{k}", v.shape, mb.dt.from_np(v.dtype), kind="ExternalInput").ap() for k, v in a.items()}
    out = nc.dram_tensor("out_0", (B, S, D), F32, kind="ExternalOutput").ap()
    build(nc, aps, out)
    r = run(nc, [{f"in_{k}": v for k, v in a.items()}], core_ids=[0])
    return r.results[0]["out_0"]
```

```python
from contextlib import ExitStack

import numpy as np

import concourse.bass as bass
from concourse import mybir

F32 = mybir.dt.float32
F32R = mybir.dt.float32r
BF16 = mybir.dt.bfloat16
I32 = mybir.dt.int32
U32 = mybir.dt.uint32
ALU = mybir.AluOpType
ACT = mybir.ActivationFunctionType
AX = mybir.AxisListType

P = 128
B, S, D = 4, 512, 256
NT = B * S // P
TB = S // P
KC = D // P
NH = 16
DH = D // NH
HG = 4
SLOTW = 32
EPS = 1e-5
BT = 256
E0, K0, H0 = 8, 2, 512
E1, K1, H1 = 12, 3, 1024
NB0 = B * S * K0 // BT + E0 - 1
NB1 = B * S * K1 // BT + E1 - 1
assert NB0 % 2 and NB1 % 2

C_ID, C_TRI, C_ONE, C_CAUSAL, C_HEAD, C_FOLD, C_IE, C_IB, C_SEL, C_PLACE, C_TOK, C_SPARE, C_END = np.cumsum(
    [0, P, P, P, P, 8, DH, E1, NB1, P, E1, 2 * NT, BT // P]).tolist()
ROOM = B * S + BT
R_TOK, R_EXP, R_W, RW = D, D + 1, D + 4, D + 8


def constants():
    c = np.zeros((P, C_END), np.float32)
    p = np.arange(P)
    c[:, C_ID:C_TRI] = np.eye(P)
    c[:, C_TRI:C_ONE] = p[:, None] < p[None, :]
    c[:, C_ONE:C_CAUSAL] = 1.0
    c[:, C_CAUSAL:C_HEAD] = np.where(p[None, :] <= p[:, None], 0.0, -1e30)
    c[:, C_HEAD:C_FOLD] = p[:, None] // DH == np.arange(8)[None, :]
    c[:, C_FOLD:C_IE] = p[:, None] % DH == np.arange(DH)[None, :]
    c[:, C_IE:C_IB] = 1 + np.arange(E1)[None, :]
    c[:, C_IB:C_SEL] = np.arange(NB1)[None, :]
    c[:, C_SEL:C_PLACE] = np.arange(P)[None, :] % SLOTW == DH
    c[:, C_PLACE:C_TOK] = ROOM * np.arange(E1)[None, :]
    for i, k in enumerate((K0, K1)):
        c[:, C_TOK + i * NT:C_TOK + (i + 1) * NT] = BT + k * (np.arange(NT)[None, :] * P + p[:, None])
    c[:, C_SPARE:C_END] = BT // P * p[:, None] + np.arange(BT // P)[None, :]
    return c


class Chain:

    def __init__(self, engine, sem):
        self.engine, self.sem, self.base, self.turn, self.per, self.n = engine, sem, 0, 0, 0, 0

    def enter(self, turn, per):
        self.base, self.turn, self.per, self.n = self.base + self.n, turn, per, 0

    def leave(self, turns):
        assert self.n == self.per, (self.n, self.per)
        self.base, self.turn, self.per, self.n = self.base + turns * self.per, 0, 0, 0

    def link(self, ins):
        self.n += 1
        ins.then_inc(self.sem, 1)
        self.engine.wait_ge(self.sem, self.turn * self.per + (self.base + self.n))


STEPS_ATTN0 = 49
STEPS_ATTN1 = 26
LN_HEAD = 12
RANKS = 128


def build(nc, A, out):
    with ExitStack() as ctx:
        def sb(name, shape, dt=F32):
            return ctx.enter_context(nc.sbuf_tensor(name, shape, dt))

        def sem(name):
            return ctx.enter_context(nc.semaphore(name))

        bank = [ctx.enter_context(nc.psum_tensor(f"bank{i}", [P, 512], F32)) for i in range(8)]
        sorted_x = nc.dram_tensor("sorted_x", (E1 * ROOM + BT, RW), F32, kind="Internal").ap()
        token_y = nc.dram_tensor("token_y", (BT + K1 * B * S, D), F32, kind="Internal").ap()

        con = sb("con", [P, C_END])
        ident = con[:, C_ID:C_TRI]
        before = con[:, C_TRI:C_ONE]
        ones = con[:, C_ONE:C_CAUSAL]
        headmask = con[:, C_HEAD:C_FOLD]
        fold = con[:, C_FOLD:C_IE]
        ident_b = sb("ident_b", [P, P], BF16)
        before_b, ones_b = sb("before_b", [P, P], BF16), sb("ones_b", [P, P], BF16)
        causal_b = sb("causal_b", [P, P], BF16)
        eps = sb("eps", [P, 1])
        zeros = sb("zeros", [P, BT // P, RW])
        wq0, wk0, wv0 = sb("wq0", [P, KC, DH]), sb("wk0", [P, KC, DH]), sb("wv0", [P, KC, DH])
        wc0, wo0 = sb("wc0", [P, KC, D]), sb("wo0", [P, KC, D])
        bq0, bk0 = sb("bq0", [DH, 1]), sb("bk0", [DH, 1])
        bv0 = sb("bv0", [P, DH])
        bo0 = sb("bo0", [1, D])
        bc0 = sb("bc0", [P, KC])
        wcT = sb("wcT", [P, KC, P])
        weff = sb("weff", [P, D])
        gw0 = sb("gw0", [P, KC, E0])
        eb0 = sb("eb0", [P, E0])
        wq1, wk1, wv1, wo1 = (sb(n, [P, KC, D]) for n in ("wq1", "wk1", "wv1", "wo1"))
        bq1, bk1 = sb("bq1", [P, KC]), sb("bk1", [P, KC])
        bv1, bo1 = sb("bv1", [P, D]), sb("bo1", [P, D])
        gw1 = sb("gw1", [P, KC, E1])

        x = sb("x", [P, NT, D])
        xn = sb("xn", [P, NT, RW])
        def pair(name, shape, dt=F32):
            return [sb(f"{name}{i}", shape, dt) for i in range(2)]

        stats, mv = pair("stats", [P, TB, 6]), pair("mv", [P, TB, 2])
        std, rstd = pair("std", [P, TB]), pair("rstd", [P, TB])
        rowsum, rinv = pair("rowsum", [P, TB]), pair("rinv", [P, TB])
        negmax = sb("negmax", [P, 2, TB])

        logits, keys = pair("logits", [P, TB, E1]), pair("keys", [P, TB, E1])
        top8 = pair("top8", [P, TB, 8])
        topk = sb("topk", [P, NT, K1])
        idx8, idxf = pair("idx8", [P, TB, 8], U32), pair("idxf", [P, TB, K1])
        hot = [pair(f"hot{k}_", [P, TB, E1]) for k in range(K1)]
        sel = pair("sel", [P, (TB + 1) * E1], BF16)
        slot = sb("slot", [P, TB, E1])
        work = sb("work", [P, TB, E1])
        wtop = sb("wtop", [P, K1, NT])
        wsum = sb("wsum", [P, NT])
        slotf = sb("slotf", [P, K1, TB])
        sloti = sb("sloti", [P, K1, NT], I32)
        place = sb("place", [P, E1])
        placei = sb("placei", [1, E1], I32)
        nblk = sb("nblk", [P, E1])
        reach = sb("reach", [P, E1, B * S // BT])
        upto = [sb(f"upto{i}", [P, 8 + E1]) for i in range(2)]
        past = sb("past", [P, NB1, E1])
        owner = sb("owner", [P, NB1])
        start = sb("start", [P, NB1])
        owneri = sb("owneri", [1, NB1], I32)
        starti = sb("starti", [1, NB1], I32)

        with ExitStack() as scope:
            def ab(name, shape, dt=F32):
                return scope.enter_context(nc.sbuf_tensor(name, shape, dt))

            regA = ab("regA", [P, 16 * S])
            kz = regA[:, :].rearrange("p (h k) -> p h k", h=NH)
            PW = S * (TB + 1) // 2
            pT1 = ab("pT1", [P, 8, PW])
            att0 = []
            for i in range(2):
                reg = regA[:, :] if i == 0 else pT1[:, :, :].rearrange("p s w -> p (s w)")
                att0.append(dict(qT=reg[0:DH, 0:512], kT=reg[0:DH, 512:1024],
                                 v=reg[:, 1024:1024 + TB * SLOTW].rearrange("p (k d) -> p k d", k=TB),
                                 p=reg[:, 2048:4096].rearrange("p (q k) -> p q k", q=TB),
                                 pT=reg[:, 4096:6144].rearrange("p (k q) -> p k q", k=TB),
                                 oT=reg[:, 6144:6656]))
            p1 = ab("p1", [P, 2, PW])
            qT1, kT1 = ab("qT1", [P, KC, S]), ab("kT1", [P, KC, S])
            v1 = ab("v1", [P, TB, NH, SLOTW])
            oTs = ab("oTs", [P, S])
            o1 = ab("o1", [P, TB, D])
            oT1 = ab("oT1", [P, KC, S])
            orec = ab("orec", [P, TB, HG])
            ctxT = [ab(f"ctxT{i}", [P, KC, S]) for i in range(2)]
            xnb = [ab(f"xnb{i}", [P, TB, D]) for i in range(2)]
            xnT = [ab(f"xnT{i}", [P, KC, S]) for i in range(2)]

        with ExitStack() as scope:
            def mb(name, shape, dt=F32):
                return scope.enter_context(nc.sbuf_tensor(name, shape, dt))

            xT = [mb(f"xT{i}", [P, 2, 512], F32R) for i in range(2)]
            hid = [mb(f"hid{i}", [P, 2, 2048], F32R) for i in range(2)]
            hraw = [mb(f"hraw{i}", [P, 512]) for i in range(2)]
            xsc = [mb(f"xsc{i}", [P, BT // P, RW]) for i in range(2)]
            mine = mb("mine", [P, BT // P, K1])
            wrow = mb("wrow", [P, BT // P, K0])
            destf = [mb(f"destf{i}", [P, BT // P]) for i in range(2)]
            desti = [mb(f"desti{i}", [P, BT // P], I32) for i in range(2)]
            ysb = [mb(f"ysb{i}", [P, 512]) for i in range(2)]
            bup = [mb(f"bup{i}", [P, H1 // P]) for i in range(2)]
            bdn = [mb(f"bdn{i}", [P, D]) for i in range(2)]
            wraw = [mb("wraw_up", [P, 2048]), mb("wraw_down", [P, 2048])]
            wup = [mb(f"wup{i}", [P, 2, 2048], F32R) for i in range(2)]
            wdn = [mb(f"wdn{i}", [P, 2, 2048], F32R) for i in range(2)]

        with ExitStack() as scope:
            gat = scope.enter_context(nc.sbuf_tensor("gat", [P, NT, K1 * D], F32))

        weights_in, weights1_in, x_loaded = sem("weights_in"), sem("weights1_in"), sem("x_loaded")
        ctx_in, ctx_even, ctx_odd = sem("ctx_in"), sem("ctx_even"), sem("ctx_odd")
        dve_step = sem("dve_step")
        setup_done = sem("setup_done")
        dve_turn, sp_turn, pool_turn = sem("dve_turn"), sem("sp_turn"), sem("pool_turn")
        zeroed, gate_exp = sem("zeroed"), sem("gate_exp")
        fold_psum, fold_ready = sem("fold_psum"), sem("fold_ready")
        var_ready, std_ready, xn_ready = sem("var_ready"), sem("std_ready"), sem("xn_ready")
        xt_psum, xnT_ready = sem("xt_psum"), sem("xnT_ready")
        kv_psum, q_psum = sem("kv_psum"), sem("q_psum")
        k_ready, q_ready, v_ready = sem("k_ready"), sem("q_ready"), sem("v_ready")
        scores0, negmax0, probs0 = sem("scores0"), sem("negmax0"), sem("probs0")
        pt0_psum, pt0_act, pt0_dve = sem("pt0_psum"), sem("pt0_act"), sem("pt0_dve")
        o0_psum, o0_ready, attn0 = sem("o0_psum"), sem("o0_ready"), sem("attn0")
        logits_psum = sem("logits_psum")
        kv1_psum, q1_psum, k1_ready, q1_ready, v1_ready, kz_ready = (
            sem(n) for n in ("kv1_psum", "q1_psum", "k1_ready", "q1_ready", "v1_ready", "kz_ready"))
        scores1, negmax1, probs1 = sem("scores1"), sem("negmax1"), sem("probs1")
        pt1_psum, pt1_act, pt1_dve = sem("pt1_psum"), sem("pt1_act"), sem("pt1_dve")
        ot_psum, ot_taken, o_psum, o_taken = (sem(n) for n in ("ot_psum", "ot_taken", "o_psum", "o_taken"))
        on_psum, on_ready, attn1 = sem("on_psum"), sem("on_ready"), sem("attn1")
        v1_cleared = sem("v1_cleared")
        out_stored = sem("out_stored")
        route = []
        moe = []
        for i in range(2):
            route.append({n: sem(f"{n}_{i}") for n in (
                "sel_ready", "rank_psum", "slots_ready", "place_ready", "table_ready", "scattered", "tails",
                "exp_in", "exp_ready", "gathered0", "gathered1", "gathered2", "gathered3", "combined")})
            moe.append({n: sem(f"{n}_{i}") for n in (
                "up_even", "up_odd", "down_even", "down_odd", "x_even", "x_odd", "bias_even", "bias_odd", "dbias_even", "dbias_odd",
                "x_set", "xt_psum", "x_high", "xT_ready", "up_high", "up_ready", "down_high", "down_ready",
                "up_psum", "relu_ready", "h_raw", "h_ready", "y_psum",
                "y_ready", "dest_ready", "y_out", "y_stored")})

        block = ctx.enter_context(nc.Block())
        x_in = A["x"].rearrange("b (t p) d -> p (b t) d", p=P)
        out_v = out.rearrange("b (t p) d -> p (b t) d", p=P)

        def row(ap, n, parts=P):
            return ap.rearrange("(a n) -> a n", a=1).broadcast_to((parts, n)) if parts > 1 else ap.rearrange("(a n) -> a n", a=1)

        loads = [
            (con[:, :], A["con"]),
            (wq0[:, :, :], A["L0_xattn_Wq"].rearrange("(c p) n -> p c n", p=P)),
            (wk0[:, :, :], A["L0_xattn_Wk"].rearrange("(c p) n -> p c n", p=P)),
            (wv0[:, :, :], A["L0_xattn_Wv"].rearrange("(c p) n -> p c n", p=P)),
            (wc0[:, :, :], A["L0_xattn_Wc"].rearrange("(c p) n -> p c n", p=P)),
            (wo0[:, :, :], A["L0_xattn_Wo"].rearrange("(c p) n -> p c n", p=P)),
            (bq0[:, :], A["L0_xattn_bq"].rearrange("(p a) -> p a", a=1)),
            (bk0[:, :], A["L0_xattn_bk"].rearrange("(p a) -> p a", a=1)),
            (bv0[:, :], row(A["L0_xattn_bv"], DH)),
            (bo0[:, :], row(A["L0_xattn_bo"], D, 1)),
            (bc0[:, 0:1], A["L0_xattn_bc"][0:P].rearrange("(p a) -> p a", a=1)),
            (bc0[:, 1:2], A["L0_xattn_bc"][P:D].rearrange("(p a) -> p a", a=1)),
            (gw0[:, :, :], A["gate0T"].rearrange("(c p) n -> p c n", p=P)),
            (eb0[:, :], row(A["L0_ffn_expert_bias"], E0)),
        ]
        loads1 = [
            (wq1[:, :, :], A["L1_xattn_Wq"].rearrange("(c p) n -> p c n", p=P)),
            (wk1[:, :, :], A["L1_xattn_Wk"].rearrange("(c p) n -> p c n", p=P)),
            (wv1[:, :, :], A["L1_xattn_Wv"].rearrange("(c p) n -> p c n", p=P)),
            (wo1[:, :, :], A["L1_xattn_Wo"].rearrange("(c p) n -> p c n", p=P)),
            (bq1[:, :], A["bq1T"]),
            (bk1[:, :], A["bk1T"]),
            (bv1[:, :], row(A["L1_xattn_bv"], D)),
            (bo1[:, :], row(A["L1_xattn_bo"], D)),
            (gw1[:, :, :], A["L1_ffn_Wg"].rearrange("(c p) n -> p c n", p=P)),
        ]

        LAYERS = [dict(E=E0, K=K0, H=H0, NB=NB0, up=A["up0"], dn=A["dn0"]),
                  dict(E=E1, K=K1, H=H1, NB=NB1, up=A["up1"], dn=A["L1_ffn_Wdown"])]

        def norm_no(f):
            return 2 * B if isinstance(f, int) and f == 0 else 2 * f + (2 * B - 1)

        def zero_rows(engine, row, s):
            engine.dma_start(sorted_x[bass.ds(row, BT), :].rearrange("(p r) d -> p r d", p=P), zeros[:, :, :]).then_inc(s, 16)

        def tails(engine, i, experts):
            engine.wait_ge(route[i]["place_ready"], 1)
            for e in experts:
                row = engine.value_load(placei[0:1, e:e + 1], min_val=0, max_val=LAYERS[i]["E"] * ROOM - BT)
                zero_rows(engine, row, route[i]["tails"])

        RAWS = (2, 1)

        SPLITS = {2: [[(0, 0), (0, 1)], [(1, 0), (1, 1)]],
                  4: [[], [(0, 0), (0, 1)], [(1, 0)], [(1, 1)]]}

        def raw(i, which, par):
            w = KC * LAYERS[i]["H"]
            at = par * w if RAWS[i] == 2 else 0
            return wraw[which][:, at:at + w]

        @block.sync
        def _(sp):
            def ctx_load(b, place, s):
                sp.dma_start(ctxT[place][:, :, :], A["ctxT"].rearrange("(c p) n -> p c n", p=P)[:, :, bass.ts(b, S)]).then_inc(s, 16)

            for dst, src in loads:
                sp.dma_start(dst, src).then_inc(weights_in, 16)
            ctx_load(0, 0, ctx_even)
            ctx_load(1, 1, ctx_odd)
            for dst, src in loads1:
                sp.dma_start(dst, src).then_inc(weights1_in, 16)
            sp.wait_ge(setup_done, 1)

            for e in (E0, E1):
                zero_rows(sp, e * ROOM, zeroed)
            for b in range(2, B):
                sp.wait_ge(kv_psum, 2 * (b - 1))
                ctx_load(b, b % 2, (ctx_even, ctx_odd)[b % 2])

            def expert_loads(i):
                L, M, R = LAYERS[i], moe[i], route[i]
                HT, NB = L["H"] // P, L["NB"]
                CH = HT // 2

                def hold(s, value):
                    sp.wait_ge(s, value)
                    sp.sem_inc(sp_turn, 1)

                def expert(j):
                    return sp.value_load(owneri[0:1, bass.ds(j, 1)], min_val=0, max_val=L["E"] - 1)

                def load_x(j, par):
                    if not isinstance(j, int) or j >= 2:
                        hold(M["xt_psum"], j + (-1))
                    row = sp.value_load(starti[0:1, bass.ds(j, 1)], min_val=0, max_val=L["E"] * ROOM)
                    sp.dma_start(xsc[par][:, :, :], sorted_x[bass.ds(row, BT), :].rearrange("(i p) d -> p i d", p=P)).then_inc(M[("x_even", "x_odd")[par]], 16)

                def load_up(j, par):
                    first = isinstance(j, int)
                    e = expert(j)
                    if not first or j >= RAWS[i]:
                        hold(M["up_ready"], 2 * j + (2 - 2 * RAWS[i]))
                    sp.dma_start(raw(i, 0, par).rearrange("p (c n) -> p c n", c=KC),
                                 L["up"][bass.ds(e, 1)].rearrange("a (c p) n -> p (a c) n", p=P)).then_inc(M[("up_even", "up_odd")[par]], 16)

                def load_up_bias(j, par):
                    if i == 1:
                        e = expert(j)
                        if not isinstance(j, int) or j >= 2:
                            hold(M["h_raw"], j * CH)
                        sp.dma_start(bup[par][:, :], A["bup1T"][bass.ds(e, 1)].rearrange("a p n -> p (a n)")).then_inc(M[("bias_even", "bias_odd")[par]], 16)

                def load_down(j, par):
                    e = expert(j)
                    if not isinstance(j, int) or j >= RAWS[i]:
                        hold(M["down_ready"], 2 * j + (2 - 2 * RAWS[i]))
                    sp.dma_start(raw(i, 1, par).rearrange("p (c n) -> p c n", c=HT),
                                 L["dn"][bass.ds(e, 1)].rearrange("a (c p) n -> p (a c) n", p=P)).then_inc(M[("down_even", "down_odd")[par]], 16)

                def load_bias(j, par):
                    if i == 1:
                        e = expert(j)
                        hold(M["y_ready"], j + 1)
                        sp.dma_start(bdn[par][:, :], A["L1_ffn_bdown"][bass.ds(e, 1)].broadcast_to((P, D))).then_inc(M[("dbias_even", "dbias_odd")[par]], 16)

                tails(sp, i, range(0, L["E"], 2))
                sp.wait_ge(R["table_ready"], 1)
                load_up(0, 0)
                load_up_bias(0, 0)
                load_up_bias(1, 1)
                sp.wait_ge(R["scattered"], 16 * NT * L["K"])
                sp.wait_ge(R["tails"], 16 * L["E"])
                sp.wait_ge(zeroed, 32)
                load_x(0, 0)
                load_down(0, 0)
                load_x(1, 1)
                load_bias(0, 0)
                load_up(1, 1)
                load_x(2, 0)
                load_up(2, 0)
                load_down(1, 1)

                def step(s, par, last=False):
                    load_up_bias(s + 2, par)
                    if not last:
                        load_x(s + 3, 1 - par)
                        load_up(s + 3, 1 - par)
                    load_down(s + 2, par)
                    load_bias(s + 1, 1 - par)

                with sp.Fori(0, (NB - 3) // 2) as t:
                    step(2 * t, 0)
                    step(2 * t + 1, 1)
                step(NB - 3, 0, last=True)
                load_bias(NB - 1, 0)
                sp.wait_ge(M["y_out"], NB + 2)
                for b in range(B):
                    sp.dma_start(gat[:, b * TB:(b + 1) * TB, 0:L["K"] * D],
                                 token_y[BT + b * S * L["K"]:BT + (b + 1) * S * L["K"], :].rearrange(
                                     "(t p k) d -> p t (k d)", p=P, k=L["K"])).then_inc(R[f"gathered{b}"], 16)
                    if i == 0 and b == 0:
                        ctx_load(0, 0, ctx_in)

            expert_loads(0)
            with sp.Fori(1, B) as b:
                sp.wait_ge(k1_ready, 2 * b)
                sp.sem_inc(sp_turn, 1)
                sp.wait_ge(v1_ready, 2 * b)
                sp.sem_inc(sp_turn, 1)
                ctx_load(b, 0, ctx_in)
            expert_loads(1)

        @block.tensor
        def _(pe):
            def ln_turn(n, p, banks):
                pe.wait_ge(xn_ready, n + 1)
                for c in range(KC):
                    for t in range(TB):
                        last = pe.transpose(bank[banks[c]][:, t * P:(t + 1) * P], xnb[p][:, t, c * P:(c + 1) * P], ident)
                    last.then_inc(xt_psum, 1)

            def gate(p, gw, E, bk):
                for t in range(TB):
                    for c in range(KC):
                        last = pe.matmul(bank[bk][:, t * E:(t + 1) * E], xnT[p][:, c, t * P:(t + 1) * P], gw[:, c, :],
                                         start=(c == 0), stop=(c == KC - 1))
                last.then_inc(logits_psum, 1)

            def ranks(i, b, p, bk):
                E = LAYERS[i]["E"]
                pe.wait_ge(route[i]["sel_ready"], b + 1)
                for d in range(TB + 1):
                    last = pe.matmul(bank[bk][:, RANKS + d * E:RANKS + (TB + 1) * E], ones_b[:, :] if d else before_b[:, :],
                                     sel[p][:, 0:(TB + 1 - d) * E], start=(d == 0), stop=(d == TB))
                last.then_inc(route[i]["rank_psum"], 1)

            pe.wait_ge(weights_in, 16 * len(loads))
            pe.wait_ge(setup_done, 1)
            for n in range(KC):
                for c in range(KC):
                    last = pe.matmul(bank[n][:, 0:DH], wc0[:, c, n * P:(n + 1) * P], fold, start=(c == 0), stop=(c == KC - 1))
            last.then_inc(fold_psum, 1)
            pe.wait_ge(fold_ready, 1)
            for c in range(KC):
                pe.matmul(bank[2][:, 0:D], wcT[:, c, :], wo0[:, c, :], start=(c == 0), stop=False)
            pe.matmul(bank[2][:, 0:D], con[0:1, C_SEL:C_PLACE], bo0[:, :], start=False, stop=True).then_inc(fold_psum, 1)
            pe.wait_ge(fold_ready, 2)

            with pe.Fori(0, B // 2) as t:
                both = [(2 * t, 0), (2 * t + 1, 1)]
                for b, p in both:
                    pe.wait_ge((ctx_even, ctx_odd)[p], t * 16 + 16)
                    for c in range(KC):
                        last = pe.matmul(bank[4 * p][0:DH, :], wk0[:, c, :], ctxT[p][:, c, :], start=(c == 0), stop=(c == KC - 1))
                    last.then_inc(kv_psum, 1)
                    for k in range(TB):
                        for c in range(KC):
                            last = pe.matmul(bank[4 * p + 1][:, k * DH:(k + 1) * DH], ctxT[p][:, c, k * P:(k + 1) * P], wv0[:, c, :],
                                             start=(c == 0), stop=(c == KC - 1))
                    last.then_inc(kv_psum, 1)
                for b, p in both:
                    ln_turn(4 * t + p, p, (4 * p + 2, 4 * p + 3))
                for b, p in both:
                    pe.wait_ge(k_ready, b + 1)
                    pe.wait_ge(xnT_ready, 2 * (4 * t + p) + 2)
                    for c in range(KC):
                        last = pe.matmul(bank[4 * p][0:DH, :], wq0[:, c, :], xnT[p][:, c, :], start=(c == 0), stop=(c == KC - 1))
                    last.then_inc(q_psum, 1)
                for b, p in both:
                    pe.wait_ge(q_ready, b + 1)
                    pe.wait_ge(v_ready, b + 1)
                    for q in range(TB):
                        pe.matmul(bank[4 * p + q][:, :], att0[p]["qT"][:, q * P:(q + 1) * P], att0[p]["kT"], start=True,
                                  stop=True).then_inc(scores0, 1)
                for b, p in both:
                    for q in range(TB):
                        pe.wait_ge(probs0, 4 * b + q + 1)
                        for k in range(TB):
                            last = pe.transpose(bank[4 * p + q][:, k * P:(k + 1) * P], att0[p]["p"][:, q, k * P:(k + 1) * P], ident)
                        last.then_inc(pt0_psum, 1)
                for b, p in both:
                    pe.wait_ge(pt0_act, 2 * b + 2)
                    pe.wait_ge(pt0_dve, 2 * b + 2)
                    for k in range(TB):
                        last = pe.matmul(bank[4 * p][SLOTW * k:SLOTW * (k + 1), :], att0[p]["v"][:, k, :], att0[p]["pT"][:, k, :],
                                         start=True, stop=True)
                    last.then_inc(o0_psum, 1)
                for b, p in both:
                    pe.wait_ge(o0_ready, b + 1)
                    for q in range(TB):
                        last = pe.matmul(bank[4 * p + 1 + q // 2][:, (q % 2) * D:(q % 2 + 1) * D], att0[p]["oT"][:, q * P:(q + 1) * P],
                                         weff[:, :], start=True, stop=True)
                        if q % 2:
                            last.then_inc(attn0, 1)
                for b, p in both:
                    ln_turn(4 * t + (p + 2), p, (4 * p, 4 * p + 2))
                for b, p in both:
                    pe.wait_ge(xnT_ready, 2 * (4 * t + (p + 2)) + 2)
                    gate(p, gw0, E0, 4 * p + 3)
                for b, p in both:
                    ranks(0, b, p, 4 * p + 3)

            def experts(i):
                L, M, R = LAYERS[i], moe[i], route[i]
                HT, NB = L["H"] // P, L["NB"]
                CH = HT // 2
                PARTS = ((0, 0), (0, 1), (1, 0))
                pe.nop().then_inc(M["y_psum"], 2)
                pe.nop().then_inc(M["up_psum"], 2 * CH)

                def turn(j, par):
                    pe.wait_ge(M["x_set"], j + 1)
                    for c in range(KC):
                        for t in range(2):
                            last = pe.transpose(bank[0][:, c * BT + t * P:c * BT + (t + 1) * P],
                                                xsc[par][:, t, c * P:(c + 1) * P], ident)
                    last.then_inc(M["xt_psum"], 1)

                def up(j, par):
                    pe.wait_ge(M["xT_ready"], j + 1)
                    pe.wait_ge(M["up_ready"], 2 * j + 2)
                    for ch in range(CH):
                        pe.wait_ge(M["h_raw"], j * CH + (ch + 1))
                        for m in range(2):
                            h = 2 * ch + m
                            for c in range(KC):
                                for w, v in PARTS:
                                    last = pe.matmul(bank[1 + ch][:, m * BT:(m + 1) * BT],
                                                     wup[par][:, w, c * L["H"] + h * P:c * L["H"] + (h + 1) * P],
                                                     xT[par][:, v, c * BT:(c + 1) * BT],
                                                     start=(c == 0 and w + v == 0), stop=(c == KC - 1 and w == 1))
                        last.then_inc(M["up_psum"], 1)

                def down(j, par):
                    pe.wait_ge(M["down_ready"], 2 * j + 2)
                    pe.wait_ge(M["h_ready"], j * CH + (CH + 2))
                    pe.wait_ge(M["y_ready"], j + 1)
                    for t in range(2):
                        for h in range(HT):
                            for v, w in PARTS:
                                last = pe.matmul(bank[5 + par][:, t * D:(t + 1) * D],
                                                 hid[par][:, v, h * BT + t * P:h * BT + (t + 1) * P],
                                                 wdn[par][:, w, h * D:(h + 1) * D],
                                                 start=(h == 0 and w + v == 0), stop=(h == HT - 1 and v == 1))
                    last.then_inc(M["y_psum"], 1)

                turn(0, 0)
                up(0, 0)
                turn(1, 1)
                with pe.Fori(0, (NB - 3) // 2) as t:
                    up(2 * t + 1, 1)
                    turn(2 * t + 2, 0)
                    down(2 * t, 0)
                    up(2 * t + 2, 0)
                    turn(2 * t + 3, 1)
                    down(2 * t + 1, 1)
                up(NB - 2, 1)
                turn(NB - 1, 0)
                down(NB - 3, 0)
                up(NB - 1, 0)
                down(NB - 2, 1)
                down(NB - 1, 0)

            experts(0)
            pe.wait_ge(weights1_in, 16 * len(loads1))
            pe.nop().then_inc(pt1_psum, 6)
            pe.nop().then_inc(ot_psum, 2)
            def front_keys(f):
                pe.wait_ge(ctx_in, f * 16 + 16)
                for c in range(KC):
                    for kc in range(KC):
                        last = pe.matmul(bank[c][:, :], wk1[:, kc, c * P:(c + 1) * P], ctxT[0][:, kc, :],
                                         start=(kc == 0), stop=(kc == KC - 1))
                    last.then_inc(kv1_psum, 1)

            def front_values(f):
                for k in range(TB):
                    for kc in range(KC):
                        last = pe.matmul(bank[6 if k // 2 else 2][:, (k % 2) * D:(k % 2 + 1) * D], ctxT[0][:, kc, k * P:(k + 1) * P],
                                         wv1[:, kc, :], start=(kc == 0), stop=(kc == KC - 1))
                    if k % 2:
                        last.then_inc(kv1_psum, 1)

            def front_norm(f):
                pe.wait_ge(k1_ready, 2 * f + 2)
                ln_turn(norm_no(f), 1, (0, 1))

            def front_queries(f):
                pe.wait_ge(xnT_ready, 2 * norm_no(f) + 2)
                for c in range(KC):
                    for kc in range(KC):
                        last = pe.matmul(bank[3 + c][:, :], wq1[:, kc, c * P:(c + 1) * P], xnT[1][:, kc, :],
                                         start=(kc == 0), stop=(kc == KC - 1))
                    last.then_inc(q1_psum, 1)

            def scores(b, h):
                c = h // 8
                pe.wait_ge(kz_ready, b * NH + (h + 1))
                for part, tiles in enumerate(((3,), (2,), (1, 0))):
                    pe.wait_ge(probs1, b * (3 * NH) + (3 * h + part + 1))
                    at = 0
                    for q in tiles:
                        w = (q + 1) * P
                        pe.matmul(bank[part][:, at:at + w], qT1[:, c, q * P:(q + 1) * P], kz[:, h, 0:w], start=True, stop=False)
                        last = pe.matmul(bank[part][:, at + q * P:at + w], ident_b[:, :], causal_b[:, :], start=False, stop=True)
                        at += w
                    last.then_inc(scores1, 1)

            def batch(b, first=False, last_one=False):
                def turn_probs(h):
                    pe.wait_ge(probs1, b * (3 * NH) + (3 * h + 6))
                    pe.wait_ge(pt1_dve, b * NH + (h + 1))
                    for k in range(TB):
                        if k == 1:
                            pe.wait_ge(pt1_act, b * (2 * NH) + (2 * h + 2))
                        at = (k == 3) * 256
                        for q in range(k, TB):
                            src = p1[:, h % 2, QOFF[q] + k * P:QOFF[q] + (k + 1) * P]
                            last = pe.transpose(bank[3 + min(k, 2)][:, at + (q - k) * P:at + (q - k + 1) * P], src, ident)
                        if k != 2:
                            last.then_inc(pt1_psum, 1)

                def values(g):
                    pe.wait_ge(pt1_dve, b * NH + (4 * g + 5))
                    pe.wait_ge(pt1_act, b * (2 * NH) + (8 * g + 10))
                    pe.wait_ge(ot_taken, b * 4 + (g + 1))
                    for k in range(TB):
                        for i in range(HG):
                            last = pe.matmul(bank[6][32 * i:32 * i + 32, k * P:S], v1[:, k, HG * g + i, :],
                                             pT1[:, (g % 2) * HG + i, QOFF2[k]:QOFF2[k] + S - k * P],
                                             start=(k == 0), stop=(k == TB - 1))
                    last.then_inc(ot_psum, 1)

                def turn_out(g):
                    pe.wait_ge(ot_taken, b * 4 + (g + 2))
                    pe.wait_ge(o_taken, b * 4 + (g + 1))
                    for q in range(TB):
                        last = pe.transpose(bank[7][:, q * P:(q + 1) * P], oTs[:, q * P:(q + 1) * P], ident)
                    last.then_inc(o_psum, 1)

                QOFF = {3: 0, 2: 512, 1: 896, 0: 1152}
                QOFF2 = {0: 0, 1: 512, 2: 896, 3: 1152}
                for h in range(NH):
                    if h < NH - 1:
                        scores(b, h + 1)
                    if h == 1 and not first:
                        ranks(1, b + (-1), 0, 7)
                    turn_probs(h)
                    if h % HG == 0 and h:
                        values(h // HG - 1)
                    if h % HG == 1 and h > 1:
                        turn_out(h // HG - 1)
                values(3)
                if not last_one:
                    front_keys(b + 1)
                turn_out(3)
                if not last_one:
                    front_values(b + 1)
                pe.wait_ge(o_taken, b * 4 + 5)
                for c in range(KC):
                    for q in range(TB):
                        last = pe.transpose(bank[3 + c][:, q * P:(q + 1) * P], o1[:, q, c * P:(c + 1) * P], ident)
                    last.then_inc(on_psum, 1)
                if not last_one:
                    front_norm(b + 1)
                pe.wait_ge(on_ready, 2 * b + 2)
                for q in range(TB):
                    for c in range(KC):
                        last = pe.matmul(bank[7 if q // 2 else 5][:, (q % 2) * D:(q % 2 + 1) * D], oT1[:, c, q * P:(q + 1) * P],
                                         wo1[:, c, :], start=(c == 0), stop=(c == KC - 1))
                    if q % 2:
                        last.then_inc(attn1, 1)
                if not last_one:
                    front_queries(b + 1)
                    pe.wait_ge(q1_ready, 2 * b + 4)
                    pe.wait_ge(v1_ready, 2 * b + 4)
                    scores(b + 1, 0)
                n = 2 * b + (2 * B + 2 - last_one)
                ln_turn(n, 0, (3, 4))
                pe.wait_ge(xnT_ready, 2 * n + 2)
                gate(0, gw1, E1, 7)
                if last_one:
                    ranks(1, b, 0, 7)

            front_keys(0)
            front_values(0)
            front_norm(0)
            front_queries(0)
            pe.wait_ge(q1_ready, 2)
            pe.wait_ge(v1_ready, 2)
            scores(0, 0)
            batch(0, first=True)
            with pe.Fori(1, B - 1) as b:
                batch(b)
            batch(B - 1, last_one=True)
            experts(1)

        @block.scalar
        def _(act):
            def ln_std(n, p=0):
                act.wait_ge(var_ready, n + 1)
                act.activation(std[p][:, :], mv[p][:, :, 1], ACT.Sqrt, bias=eps[:, :]).then_inc(std_ready, 1)

            def ln_turned(n, banks, p=0):
                for c in range(KC):
                    act.wait_ge(xt_psum, 2 * n + (c + 1))
                    act.activation(xnT[p][:, c, :], bank[banks[c]][:, :], ACT.Copy).then_inc(xnT_ready, 1)

            act.dma_start(x[:, :, :], x_in).then_inc(x_loaded, 16)
            act.wait_ge(setup_done, 1)
            with act.Fori(0, B // 2) as t:
                both = [(2 * t, 0), (2 * t + 1, 1)]
                for b, p in both:
                    act.wait_ge(kv_psum, 2 * b + 1)
                    act.activation(att0[p]["kT"], bank[4 * p][0:DH, :], ACT.Identity, bias=bk0[:, :]).then_inc(k_ready, 1)
                for b, p in both:
                    ln_std(4 * t + p, p)
                for b, p in both:
                    ln_turned(4 * t + p, (4 * p + 2, 4 * p + 3), p)
                for b, p in both:
                    act.wait_ge(q_psum, b + 1)
                    act.activation(att0[p]["qT"], bank[4 * p][0:DH, :], ACT.Identity, bias=bq0[:, :], scale=0.25).then_inc(q_ready, 1)
                for b, p in both:
                    for q in range(TB):
                        act.wait_ge(negmax0, 4 * b + q + 1)
                        act.activation(att0[p]["p"][:, q, :], bank[4 * p + q][:, :], ACT.Exp, bias=negmax[:, p, q:q + 1],
                                       accum_out=rowsum[p][:, q:q + 1]).then_inc(probs0, 1)
                for b, p in both:
                    for q in range(2):
                        act.wait_ge(pt0_psum, 4 * b + q + 1)
                        act.activation(att0[p]["pT"][:, :, q * P:(q + 1) * P], bank[4 * p + q][:, :].rearrange("p (k q) -> p k q", k=TB),
                                       ACT.Copy).then_inc(pt0_act, 1)
                for b, p in both:
                    act.wait_ge(o0_psum, b + 1)
                    act.activation(att0[p]["oT"], bank[4 * p][:, :], ACT.Copy).then_inc(o0_ready, 1)
                for b, p in both:
                    ln_std(4 * t + (p + 2), p)
                for b, p in both:
                    ln_turned(4 * t + (p + 2), (4 * p, 4 * p + 2), p)
                for b, p in both:
                    act.wait_ge(logits_psum, b + 1)
                    act.activation(keys[p][:, :, 0:E0], bank[4 * p + 3][:, 0:TB * E0].rearrange("p (t e) -> p t e", t=TB), ACT.Exp,
                                   scale=-1.0).then_inc(gate_exp, 1)

            def experts(i):
                L, M = LAYERS[i], moe[i]
                HT, NB = L["H"] // P, L["NB"]
                CH = HT // 2
                HALF = KC * L["H"] // 2

                def high_up(j, n, par, half):
                    if half == 0:
                        act.wait_ge(M[("up_even", "up_odd")[par]], n * 16 + 16)
                        act.wait_ge(M["up_psum"], j * CH + CH)
                    cols = slice(half * HALF, (half + 1) * HALF)
                    act.activation(wup[par][:, 0, cols], raw(i, 0, par)[:, cols], ACT.Copy).then_inc(M["up_high"], 1)

                def high_down(j, n, par, half):
                    if half == 0:
                        act.wait_ge(M[("down_even", "down_odd")[par]], n * 16 + 16)
                        act.wait_ge(M["y_psum"], j + 1)
                    cols = slice(half * HALF, (half + 1) * HALF)
                    act.activation(wdn[par][:, 0, cols], raw(i, 1, par)[:, cols], ACT.Copy).then_inc(M["down_high"], 1)

                def high_x(j, par):
                    act.wait_ge(M["xt_psum"], j + 1)
                    act.activation(xT[par][:, 0, :], bank[0][:, :], ACT.Copy).then_inc(M["x_high"], 1)

                def hidden(j, n, par, ch):
                    act.wait_ge(M["up_psum"], j * CH + (2 * CH + ch + 1))
                    act.wait_ge(M["h_ready"], j * CH + (ch + 1))
                    if i == 0:
                        act.activation(hraw[ch % 2][:, :], bank[1 + ch][:, :], ACT.Relu).then_inc(M["relu_ready"], 1)
                        act.wait_ge(M["relu_ready"], j * CH + (ch + 1))
                        act.activation(hraw[ch % 2][:, :], hraw[ch % 2][:, :], ACT.Square).then_inc(M["h_raw"], 1)
                    else:
                        if ch == 0:
                            act.wait_ge(M[("bias_even", "bias_odd")[par]], n * 16 + 16)
                        for m in range(2):
                            h = 2 * ch + m
                            last = act.activation(hraw[ch % 2][:, m * BT:(m + 1) * BT], bank[1 + ch][:, m * BT:(m + 1) * BT],
                                                  ACT.Gelu, bias=bup[par][:, h:h + 1])
                        last.then_inc(M["h_raw"], 1)

                def take_y(j, par):
                    act.wait_ge(M["y_psum"], j + 3)
                    act.wait_ge(M["y_out"], j + 1)
                    act.activation(ysb[par][:, :], bank[5 + par][:, :], ACT.Copy).then_inc(M["y_ready"], 1)

                def step(j, n, par, taken=True, more=True):
                    m = n if par else n + 1
                    for ch in range(CH):
                        for down, half in SPLITS[CH][ch]:
                            if down:
                                high_down(j + 1, n, 1 - par, half)
                            elif more:
                                high_up(j + 2, m, par, half)
                        if i == 0 and ch == 0 and taken:
                            take_y(j + (-1), 1 - par)
                        hidden(j + 1, n, 1 - par, ch)
                        if more and ch == CH // 2 - 1:
                            high_x(j + 2, par)

                act.nop().then_inc(M["h_raw"], CH)
                high_up(0, 0, 0, 0)
                high_up(0, 0, 0, 1)
                high_x(0, 0)
                step(-1, 0, 1, taken=False)
                step(0, 0, 0, taken=False)
                step(1, 1, 1)
                with act.Fori(1, (NB - 3) // 2) as t:
                    step(2 * t, t, 0)
                    step(2 * t + 1, t + 1, 1)
                step(NB - 3, (NB - 3) // 2, 0)
                step(NB - 2, (NB - 1) // 2, 1, more=False)
                if i == 0:
                    take_y(NB - 2, 1)
                    take_y(NB - 1, 0)

            tails(act, 0, range(1, E0, 2))
            experts(0)
            act.wait_ge(weights1_in, 16 * len(loads1))
            act.nop().then_inc(probs1, 3)
            act.nop().then_inc(pt1_act, 2)
            act.nop().then_inc(ot_taken, 1)
            def front_keys(f):
                for c in range(KC):
                    act.wait_ge(kv1_psum, 4 * f + (c + 1))
                    act.activation(kT1[:, c, :], bank[c][:, :], ACT.Identity, bias=bk1[:, c:c + 1]).then_inc(k1_ready, 1)

            def front_queries(f):
                for c in range(KC):
                    act.wait_ge(q1_psum, 2 * f + (c + 1))
                    act.activation(qT1[:, c, :], bank[3 + c][:, :], ACT.Identity, bias=bq1[:, c:c + 1],
                                   scale=0.25).then_inc(q1_ready, 1)

            def batch(b, last_one=False):
                QOFF = {3: 0, 2: 512, 1: 896, 0: 1152}

                def exps(h):
                    act.wait_ge(pt1_psum, b * (3 * NH) + (3 * h + 3))
                    for part, tiles in enumerate(((3,), (2,), (1, 0))):
                        act.wait_ge(negmax1, b * (3 * NH) + (3 * h + part + 1))
                        at = 0
                        for q in tiles:
                            w = (q + 1) * P
                            last = act.activation(p1[:, h % 2, QOFF[q]:QOFF[q] + w], bank[part][:, at:at + w], ACT.Exp,
                                                  bias=negmax[:, h % 2, q:q + 1])
                            at += w
                        last.then_inc(probs1, 1)

                def take_probs(h):
                    s = (h // HG % 2) * HG + h % HG
                    act.wait_ge(ot_psum, b * 4 + (h // HG + 1))
                    for part in (1, 2):
                        act.wait_ge(pt1_psum, b * (3 * NH) + (3 * h + part + 7))
                        at = 512 + (part - 1) * 384
                        act.activation(pT1[:, s, at:at + 384], bank[3 + part][:, 0:384], ACT.Copy).then_inc(pt1_act, 1)

                def take_out(g):
                    act.wait_ge(ot_psum, b * 4 + (g + 3))
                    act.activation(oTs[:, :], bank[6][:, :], ACT.Copy).then_inc(ot_taken, 1)

                exps(0)
                for h in range(NH):
                    if h < NH - 1:
                        exps(h + 1)
                    take_probs(h)
                    if h % HG == 0 and h:
                        take_out(h // HG - 1)
                    if h == LN_HEAD and not last_one:
                        ln_std(2 * b + (2 * B + 1), 1)
                take_out(3)
                if not last_one:
                    front_keys(b + 1)
                for c in range(KC):
                    act.wait_ge(on_psum, 2 * b + (c + 1))
                    act.activation(oT1[:, c, :], bank[3 + c][:, :], ACT.Copy).then_inc(on_ready, 1)
                if last_one:
                    ln_std(2 * b + (2 * B + 1))
                    ln_turned(2 * b + (2 * B + 1), (3, 4))
                else:
                    ln_turned(norm_no(b + 1), (0, 1), 1)
                    front_queries(b + 1)
                    ln_std(2 * b + (2 * B + 2))
                    ln_turned(2 * b + (2 * B + 2), (3, 4))

            ln_std(2 * B, 1)
            front_keys(0)
            ln_turned(norm_no(0), (0, 1), 1)
            front_queries(0)
            batch(0)
            with act.Fori(1, B - 1) as b:
                batch(b)
            batch(B - 1, last_one=True)
            tails(act, 1, range(1, E1, 2))
            act.wait_ge(route[1]["exp_in"], 1)
            act.activation(wtop[:, :, :], wtop[:, :, :], ACT.Exp).then_inc(route[1]["exp_ready"], 1)
            experts(1)
            for b in range(B):
                act.wait_ge(route[1]["combined"], (b + 1) * TB)
                act.dma_start(out_v[:, b * TB:(b + 1) * TB, :], x[:, b * TB:(b + 1) * TB, :]).then_inc(out_stored, 16)
            act.wait_ge(out_stored, 16 * B)

        @block.gpsimd
        def _(pool):
            def scatter(i):
                K, R = LAYERS[i]["K"], route[i]
                for b in range(B):
                    pool.wait_ge(R["slots_ready"], b + 1)
                    for t in range(b * TB, (b + 1) * TB):
                        for k in range(K):
                            pool.indirect_dma_start(sorted_x, bass.IndirectOffsetOnAxis(sloti[:, k, t:t + 1].bitcast(U32), 0),
                                                    xn[:, t, :], None).then_inc(R["scattered"], 16)

            def results(i):
                M = moe[i]
                pool.sem_inc(M["y_out"], 2)

                def store(t, par):
                    pool.wait_ge(M["y_ready"], 2 * t + (par + 3))
                    pool.sem_inc(pool_turn, 1)
                    pool.wait_ge(M["dest_ready"], 2 * t + (par + 1))
                    pool.sem_inc(pool_turn, 1)
                    for r in range(2):
                        pool.indirect_dma_start(token_y, bass.IndirectOffsetOnAxis(desti[par][:, r:r + 1].bitcast(U32), 0),
                                                ysb[par][:, r * D:(r + 1) * D], None).then_inc(M["y_stored"], 16)
                    pool.wait_ge(M["y_stored"], 64 * t + 32 * (par + 1))
                    pool.sem_inc(M["y_out"], 1)

                NB = LAYERS[i]["NB"]
                with pool.Fori(0, NB // 2) as t:
                    store(t, 0)
                    store(t, 1)
                store(NB // 2, 0)

            scatter(0)
            results(0)
            scatter(1)
            results(1)

        @block.vector
        def _(dve):
            chn = Chain(dve, dve_step)

            def norm_stats(p, src):
                dve.sem_inc(dve_turn, 1)
                for t in range(TB):
                    last = dve.bn_stats(stats[p][:, t, :], src(t))
                chn.link(last)
                dve.sem_inc(dve_turn, 1)
                for t in range(TB):
                    last = dve.bn_aggr(mv[p][:, t, :], stats[p][:, t, :])
                last.then_inc(var_ready, 1)

            def norm(n, p, src):
                dve.wait_ge(std_ready, n + 1)
                chn.link(dve.reciprocal(rstd[p][:, :], std[p][:, :]))
                for t in range(TB):
                    last = dve.tensor_scalar(xnb[p][:, t, :], src(t), mv[p][:, t, 0:1], rstd[p][:, t:t + 1], ALU.subtract, ALU.mult)
                last.then_inc(xn_ready, 1)

            def norm_rows(p, src, dst):
                for t in range(TB):
                    dve.tensor_scalar(dst(t), src(t), mv[p][:, t, 0:1], rstd[p][:, t:t + 1], ALU.subtract, ALU.mult)

            def tile_of(b):
                return lambda t: x[:, bass.ds(b * TB + t, 1), :].rearrange("p a d -> p (a d)")

            def row_of(b):
                return lambda t: xn[:, bass.ds(b * TB + t, 1), 0:D].rearrange("p a d -> p (a d)")

            def choose(i, b, p, bk):
                L, R = LAYERS[i], route[i]
                E, K = L["E"], L["K"]
                ts = bass.ds(b * TB, TB)
                lg, ky, wk = (t[:, :, 0:E] for t in (logits[p], keys[p], work))
                hots = [h[p][:, :, 0:E] for h in hot]
                se = sel[p][:, 0:TB * E].rearrange("p (t e) -> p t e", t=TB)
                psum = bank[bk][:, 0:TB * E].rearrange("p (t e) -> p t e", t=TB)
                if i == 0:
                    dve.wait_ge(gate_exp, b + 1)
                    chn.link(dve.tensor_scalar(ky, ky, 1.0, None, ALU.add))
                    chn.link(dve.reciprocal(ky, ky))
                    chn.link(dve.tensor_tensor(lg, ky, eb0[:, :].unsqueeze(1).broadcast_to((P, TB, E)), ALU.add))
                else:
                    dve.wait_ge(logits_psum, b + (B + 1))
                    chn.link(dve.tensor_copy(lg, psum))
                dve.sem_inc(dve_turn, 1)
                for t in range(TB):
                    last = dve.max(top8[p][:, t, :], lg[:, t, :])
                chn.link(last)
                dve.sem_inc(dve_turn, 1)
                for t in range(TB):
                    last = dve.max_index(idx8[p][:, t, :], top8[p][:, t, :], lg[:, t, :])
                if i == 1:
                    dve.tensor_copy(topk[:, ts, :], top8[p][:, :, 0:K1])
                chn.link(last)
                dve.tensor_copy(xn[:, ts, R_TOK], con[:, bass.ds(b * TB + (C_TOK + i * NT), TB)])
                chn.link(dve.tensor_copy(idxf[p][:, :, :], idx8[p][:, :, 0:K1]))
                chn.link(dve.tensor_scalar(xn[:, ts, R_EXP:R_EXP + K], idxf[p][:, :, 0:K], 1.0, None, ALU.add))
                for k in range(K):
                    last = dve.tensor_tensor(hots[k], con[:, C_IE:C_IE + E].unsqueeze(1).broadcast_to((P, TB, E)),
                                             xn[:, ts, R_EXP + k:R_EXP + k + 1].broadcast_to((P, TB, E)), ALU.is_equal)
                chn.link(last)
                chn.link(dve.tensor_tensor(se, hots[0], hots[1], ALU.add))
                if K == 3:
                    chn.link(dve.tensor_tensor(se, se, hots[2], ALU.add))
                dve.nop().then_inc(R["sel_ready"], 1)
                if i == 0:
                    for k in range(K):
                        chn.link(dve.tensor_tensor(wk, hots[k], ky, ALU.mult))
                        chn.link(dve.tensor_reduce(xn[:, ts, R_W + k], wk, AX.X, ALU.add))

            def places(i, b, p, bk):
                L, R = LAYERS[i], route[i]
                E, K = L["E"], L["K"]
                ts = bass.ds(b * TB, TB)
                sl, wk = slot[:, :, 0:E], work[:, :, 0:E]
                hots = [h[p][:, :, 0:E] for h in hot]
                dve.wait_ge(R["rank_psum"], b + 1)
                dve.sem_inc(dve_turn, 1)
                chn.link(dve.tensor_tensor(sl, bank[bk][:, RANKS:RANKS + TB * E].rearrange("p (t e) -> p t e", t=TB),
                                           place[:, 0:E].unsqueeze(1).broadcast_to((P, TB, E)), ALU.add))
                for k in range(K):
                    chn.link(dve.tensor_tensor(wk, hots[k], sl, ALU.mult))
                    chn.link(dve.tensor_reduce(slotf[:, k, :], wk, AX.X, ALU.add))
                dve.tensor_copy(sloti[:, 0:K, ts], slotf[:, 0:K, :]).then_inc(R["slots_ready"], 1)
                chn.link(dve.tensor_tensor(place[:, 0:E], bank[bk][:, RANKS + TB * E:RANKS + (TB + 1) * E], place[:, 0:E], ALU.add))

            def blocks(i):
                L, R = LAYERS[i], route[i]
                E, K, NB = L["E"], L["K"], L["NB"]
                dve.tensor_copy(placei[:, 0:E], place[0:1, 0:E]).then_inc(R["place_ready"], 1)
                chn.link(dve.tensor_tensor(nblk[:, 0:E], place[:, 0:E], con[:, C_PLACE:C_PLACE + E], ALU.subtract))
                chn.link(dve.tensor_scalar(nblk[:, 0:E], nblk[:, 0:E], 1.0 / BT, None, ALU.mult))
                n = B * S // BT
                chn.link(dve.tensor_tensor(reach[:, 0:E, :], nblk[:, 0:E].unsqueeze(2).broadcast_to((P, E, n)),
                                           con[:, C_IB:C_IB + n].unsqueeze(1).broadcast_to((P, E, n)), ALU.is_gt))
                chn.link(dve.tensor_reduce(nblk[:, 0:E], reach[:, 0:E, :], AX.X, ALU.add))
                chn.link(dve.tensor_copy(upto[0][:, 8:8 + E], nblk[:, 0:E]))
                for n, d in enumerate((1, 2, 4, 8)):
                    old, new = upto[n % 2], upto[1 - n % 2]
                    chn.link(dve.tensor_tensor(new[:, 8:8 + E], old[:, 8:8 + E], old[:, 8 - d:8 + E - d], ALU.add))
                pa = past[:, 0:NB, 0:E]
                chn.link(dve.tensor_tensor(pa, con[:, C_IB:C_IB + NB].unsqueeze(2).broadcast_to((P, NB, E)),
                                           upto[0][:, 8:8 + E].unsqueeze(1).broadcast_to((P, NB, E)), ALU.is_ge))
                chn.link(dve.tensor_reduce(owner[:, 0:NB], pa, AX.X, ALU.add))
                dve.tensor_scalar(owneri[:, 0:NB], owner[0:1, 0:NB], float(E - 1), None, ALU.min)
                chn.link(dve.tensor_tensor(pa, pa, nblk[:, 0:E].unsqueeze(1).broadcast_to((P, NB, E)), ALU.mult))
                chn.link(dve.tensor_reduce(start[:, 0:NB], pa, AX.X, ALU.add))
                chn.link(dve.tensor_tensor(start[:, 0:NB], con[:, C_IB:C_IB + NB], start[:, 0:NB], ALU.subtract))
                chn.link(dve.tensor_scalar(start[:, 0:NB], start[:, 0:NB], float(BT), None, ALU.mult))
                chn.link(dve.scalar_tensor_tensor(start[:, 0:NB], owner[:, 0:NB], float(ROOM), start[:, 0:NB], ALU.mult, ALU.add))
                dve.tensor_scalar(starti[:, 0:NB], start[0:1, 0:NB], float(E * ROOM), None, ALU.min).then_inc(R["table_ready"], 1)
                chn.link(dve.tensor_scalar(owner[:, 0:NB], owner[:, 0:NB], 1.0, None, ALU.add))
                if i == 1:
                    for k in range(K):
                        last = dve.tensor_tensor(wtop[:, k, :], topk[:, :, k], topk[:, :, 0], ALU.subtract)
                    last.then_inc(R["exp_in"], 1)
                    dve.wait_ge(R["exp_ready"], 1)
                    chn.link(dve.tensor_tensor(wsum[:, :], wtop[:, 0, :], wtop[:, 1, :], ALU.add))
                    chn.link(dve.tensor_tensor(wsum[:, :], wsum[:, :], wtop[:, 2, :], ALU.add))
                    chn.link(dve.reciprocal(wsum[:, :], wsum[:, :]))
                    chn.link(dve.tensor_tensor(wtop[:, :, :], wtop[:, :, :], wsum[:, :].unsqueeze(1).broadcast_to((P, K1, NT)), ALU.mult))
                else:
                    dve.tensor_copy(place[:, :], con[:, C_PLACE:C_TOK])

            dve.memset(eps[:, :], EPS)
            for u in upto:
                dve.memset(u[:, :], 0.0)
            dve.memset(xn[:, :, R_TOK:RW], 0.0)
            chn.link(dve.memset(zeros[:, :, :], 0.0))
            dve.memset(wcT[:, :, :], 0.0)
            for p in range(2):
                dve.memset(sel[p][:, :], 0.0)
                last = dve.memset(att0[p]["v"], 0.0)
            chn.link(last)
            for p in range(2):
                dve.memset(att0[p]["v"][:, :, DH:DH + 1], 1.0)
            dve.wait_ge(weights_in, 16 * len(loads))
            dve.tensor_copy(place[:, :], con[:, C_PLACE:C_TOK])
            dve.tensor_copy(zeros[:, :, R_TOK], con[:, C_SPARE:C_END])
            dve.tensor_copy(ident_b[:, :], ident)
            dve.tensor_copy(before_b[:, :], before)
            dve.tensor_copy(ones_b[:, :], ones)
            dve.tensor_copy(causal_b[:, :], con[:, C_CAUSAL:C_HEAD])
            dve.tensor_scalar(bq0[:, :], bq0[:, :], 0.25, None, ALU.mult).then_inc(setup_done, 1)
            dve.wait_ge(fold_psum, 1)
            for c in range(KC):
                for k in range(TB):
                    dve.tensor_copy(wcT[:, c, k * SLOTW + DH:k * SLOTW + DH + 1], bc0[:, c:c + 1])
                    last = dve.tensor_copy(wcT[:, c, k * SLOTW:k * SLOTW + DH], bank[c][:, 0:DH])
            last.then_inc(fold_ready, 1)
            dve.wait_ge(fold_psum, 2)
            dve.tensor_copy(weff[:, :], bank[2][:, 0:D]).then_inc(fold_ready, 1)

            dve.wait_ge(x_loaded, 16)
            with dve.Fori(0, B // 2) as t:
                chn.enter(t, STEPS_ATTN0)
                both = [(2 * t, 0), (2 * t + 1, 1)]
                for b, p in both:
                    norm_stats(p, tile_of(b))
                for b, p in both:
                    norm(4 * t + p, p, tile_of(b))
                for b, p in both:
                    dve.wait_ge(kv_psum, 2 * b + 2)
                    dve.tensor_tensor(att0[p]["v"][:, :, 0:DH], bank[4 * p + 1][:, 0:TB * DH].rearrange("p (k d) -> p k d", k=TB),
                                      bv0[:, :].unsqueeze(1).broadcast_to((P, TB, DH)), ALU.add).then_inc(v_ready, 1)
                for b, p in both:
                    for q in range(TB):
                        dve.wait_ge(scores0, 4 * b + q + 1)
                        dve.tensor_reduce(negmax[:, p, q:q + 1], bank[4 * p + q][:, :], AX.X, ALU.max, negate=True).then_inc(negmax0, 1)
                for b, p in both:
                    for q in range(2, 4):
                        dve.wait_ge(pt0_psum, 4 * b + q + 1)
                        dve.tensor_copy(att0[p]["pT"][:, :, q * P:(q + 1) * P],
                                        bank[4 * p + q][:, :].rearrange("p (k q) -> p k q", k=TB)).then_inc(pt0_dve, 1)
                for b, p in both:
                    dve.wait_ge(probs0, 4 * b + 4)
                    last = dve.reciprocal(rinv[p][:, :], rowsum[p][:, :])
                chn.link(last)
                for b, p in both:
                    tile = tile_of(b)
                    for q in range(TB):
                        if q % 2 == 0:
                            dve.wait_ge(attn0, 2 * b + (q // 2 + 1))
                        last = dve.scalar_tensor_tensor(tile(q), bank[4 * p + 1 + q // 2][:, (q % 2) * D:(q % 2 + 1) * D],
                                                        rinv[p][:, q:q + 1], tile(q), ALU.mult, ALU.add)
                    chn.link(last)
                    norm_stats(p, tile)
                for b, p in both:
                    norm(4 * t + (p + 2), p, tile_of(b))
                for b, p in both:
                    norm_rows(p, tile_of(b), row_of(b))
                for b, p in both:
                    choose(0, b, p, 4 * p + 3)
                for b, p in both:
                    places(0, b, p, 4 * p + 3)
            chn.leave(B // 2)

            def experts(i):
                L, M, R = LAYERS[i], moe[i], route[i]
                HT, NB = L["H"] // P, L["NB"]
                CH = HT // 2
                HALF = KC * L["H"] // 2
                dve.nop().then_inc(M["y_ready"], 2)
                dve.nop().then_inc(M["h_ready"], 2)

                def low_up(j, par, half):
                    cols = slice(half * HALF, (half + 1) * HALF)
                    dve.wait_ge(M["up_high"], 2 * j + (half + 1))
                    dve.tensor_tensor(wup[par][:, 1, cols], raw(i, 0, par)[:, cols], wup[par][:, 0, cols].bitcast(F32),
                                      ALU.subtract).then_inc(M["up_ready"], 1)

                def low_down(j, par, half):
                    cols = slice(half * HALF, (half + 1) * HALF)
                    dve.wait_ge(M["down_high"], 2 * j + (half + 1))
                    dve.tensor_tensor(wdn[par][:, 1, cols], raw(i, 1, par)[:, cols], wdn[par][:, 0, cols].bitcast(F32),
                                      ALU.subtract).then_inc(M["down_ready"], 1)

                def low_x(j, par):
                    dve.wait_ge(M["x_high"], j + 1)
                    dve.tensor_tensor(xT[par][:, 1, :], bank[0][:, :], xT[par][:, 0, :].bitcast(F32), ALU.subtract).then_inc(M["xT_ready"], 1)

                def hidden(j, par, ch):
                    cols = slice(ch * 512, (ch + 1) * 512)
                    dve.wait_ge(M["h_raw"], j * CH + (CH + ch + 1))
                    dve.wait_ge(M["y_psum"], j + 1)
                    chn.link(dve.tensor_copy(hid[par][:, 0, cols], hraw[ch % 2][:, :]))
                    dve.tensor_tensor(hid[par][:, 1, cols], hraw[ch % 2][:, :], hid[par][:, 0, cols].bitcast(F32),
                                      ALU.subtract).then_inc(M["h_ready"], 1)

                def set_dest(j, par):
                    dve.wait_ge(M["y_out"], j + 1)
                    dve.sem_inc(dve_turn, 1)
                    dve.tensor_copy(desti[par][:, :], destf[par][:, :]).then_inc(M["dest_ready"], 1)

                def set_x(j, n, par, first=False):
                    if not first:
                        set_dest(j + (-2), par)
                    dve.wait_ge(M[("x_even", "x_odd")[par]], n * 16 + 16)
                    dve.sem_inc(dve_turn, 1)
                    chn.link(dve.tensor_tensor(mine[:, :, :], xsc[par][:, :, R_EXP:R_EXP + K1],
                                               owner[:, bass.ds(j, 1)].unsqueeze(2).broadcast_to((P, 2, K1)), ALU.is_equal))
                    last = dve.tensor_tensor(destf[par][:, :], mine[:, :, 1], xsc[par][:, :, R_TOK], ALU.add)
                    if i == 0:
                        chn.link(dve.tensor_tensor(wrow[:, :, :], mine[:, :, 0:K0], xsc[par][:, :, R_W:R_W + K0], ALU.mult))
                        chn.link(dve.tensor_tensor(wrow[:, :, 0], wrow[:, :, 0], wrow[:, :, 1], ALU.add))
                        dve.tensor_tensor(xsc[par][:, :, 0:D], xsc[par][:, :, 0:D],
                                          wrow[:, :, 0:1].broadcast_to((P, 2, D)), ALU.mult).then_inc(M["x_set"], 1)
                    else:
                        chn.link(last)
                        dve.scalar_tensor_tensor(destf[par][:, :], mine[:, :, 2], 2.0, destf[par][:, :], ALU.mult,
                                                 ALU.add).then_inc(M["x_set"], 1)

                def take_y(j, n, par):
                    if i == 1:
                        dve.wait_ge(M["y_psum"], j + 3)
                        dve.wait_ge(M[("dbias_even", "dbias_odd")[par]], n * 16 + 16)
                        dve.tensor_tensor(ysb[par][:, :].rearrange("p (i d) -> p i d", i=2),
                                          bank[5 + par][:, :].rearrange("p (i d) -> p i d", i=2),
                                          bdn[par][:, :].unsqueeze(1).broadcast_to((P, 2, D)), ALU.add).then_inc(M["y_ready"], 1)

                def step(j, n, par, first=False, taken=True, more=True):
                    if more:
                        set_x(j + 2, n + 1, par, first=first)
                    if taken:
                        take_y(j + (-1), n if par else n + (-1), 1 - par)
                    if not more:
                        set_dest(j, par)
                    for ch in range(CH):
                        for down, half in SPLITS[CH][ch]:
                            if down:
                                low_down(j + 1, 1 - par, half)
                            elif more:
                                low_up(j + 2, par, half)
                        hidden(j + 1, 1 - par, ch)
                        if more and ch == CH // 2 - 1:
                            low_x(j + 2, par)

                set_x(0, 0, 0, first=True)
                low_up(0, 0, 0)
                low_up(0, 0, 1)
                low_x(0, 0)
                step(-1, -1, 1, first=True, taken=False)
                step(0, 0, 0, taken=False)
                step(1, 0, 1)
                with dve.Fori(1, (NB - 3) // 2) as t:
                    chn.enter(t + (-1), 2 * (CH + (3 if i == 0 else 2)))
                    step(2 * t, t, 0)
                    step(2 * t + 1, t, 1)
                chn.leave((NB - 3) // 2 - 1)
                step(NB - 3, (NB - 3) // 2, 0)
                step(NB - 2, (NB - 3) // 2, 1, more=False)
                take_y(NB - 2, (NB - 3) // 2, 1)
                set_dest(NB - 1, 0)
                take_y(NB - 1, (NB - 1) // 2, 0)

            def combine(i, batches):
                L, R = LAYERS[i], route[i]
                K = L["K"]
                for t in range(batches[0] * TB, (batches[-1] + 1) * TB):
                    if t % TB == 0:
                        dve.wait_ge(R[f"gathered{t // TB}"], 16)
                    for k in range(K):
                        g = gat[:, t, k * D:(k + 1) * D]
                        if i == 0:
                            last = dve.tensor_tensor(x[:, t, :], x[:, t, :], g, ALU.add)
                        else:
                            last = dve.scalar_tensor_tensor(x[:, t, :], g, wtop[:, k, t:t + 1], x[:, t, :], ALU.mult, ALU.add)
                        if k < K - 1:
                            chn.link(last)
                    last.then_inc(R["combined"], 1)
                dve.wait_ge(R["combined"], t + 1)

            blocks(0)
            experts(0)
            dve.wait_ge(weights1_in, 16 * len(loads1))
            dve.tensor_scalar(bq1[:, :], bq1[:, :], 0.25, None, ALU.mult)
            dve.memset(v1[:, :, :, :], 0.0).then_inc(v1_cleared, 1)
            dve.wait_ge(v1_cleared, 1)
            dve.memset(v1[:, :, :, DH:DH + 1], 1.0)
            dve.nop().then_inc(pt1_dve, 1)
            dve.nop().then_inc(o_taken, 1)
            def front_values(f):
                for k in range(2):
                    dve.wait_ge(kv1_psum, 4 * f + (3 + k))
                    for j in range(2):
                        last = dve.tensor_tensor(v1[:, 2 * k + j, :, 0:DH],
                                                 bank[6 if k else 2][:, j * D:(j + 1) * D].rearrange("p (h d) -> p h d", h=NH),
                                                 bv1[:, :].rearrange("p (h d) -> p h d", h=NH), ALU.add)
                    last.then_inc(v1_ready, 1)

            def front_keys(heads):
                for h in heads:
                    dve.tensor_scalar(kz[:, h, :], kT1[:, h // 8, :], headmask[:, h % 8:h % 8 + 1], None, ALU.mult).then_inc(kz_ready, 1)

            def batch(b, first=False, last_one=False):
                tile = tile_of(b)

                def maxima(h):
                    for part, tiles in enumerate(((3,), (2,), (1, 0))):
                        dve.wait_ge(scores1, b * (3 * NH) + (3 * h + part + 1))
                        at = 0
                        for q in tiles:
                            w = (q + 1) * P
                            last = dve.tensor_reduce(negmax[:, h % 2, q:q + 1], bank[part][:, at:at + w], AX.X, ALU.max, negate=True)
                            at += w
                        last.then_inc(negmax1, 1)

                def take_probs(h):
                    s = (h // HG % 2) * HG + h % HG
                    dve.wait_ge(ot_psum, b * 4 + (h // HG + 1))
                    dve.wait_ge(pt1_psum, b * (3 * NH) + (3 * h + 7))
                    dve.tensor_copy(pT1[:, s, 0:512], bank[3][:, :]).then_inc(pt1_dve, 1)

                def normalise(g):
                    dve.wait_ge(o_psum, b * 4 + (g + 1))
                    o = bank[7][:, :].rearrange("p (q i d) -> p q i d", q=TB, i=HG)
                    chn.link(dve.reciprocal(orec[:, :, :], o[:, :, :, DH]))
                    dve.tensor_tensor(o1[:, :, g * HG * DH:(g + 1) * HG * DH].rearrange("p q (i d) -> p q i d", i=HG),
                                      o[:, :, :, 0:DH], orec[:, :, :].unsqueeze(3).broadcast_to((P, TB, HG, DH)),
                                      ALU.mult).then_inc(o_taken, 1)

                maxima(0)
                for h in range(NH):
                    if h < NH - 1:
                        maxima(h + 1)
                    if h == 0 and not first:
                        choose(1, b + (-1), 0, 7)
                    if h == 1 and not first:
                        places(1, b + (-1), 0, 7)
                    if h + HG < NH:
                        front_keys([h + HG])
                    take_probs(h)
                    if h % HG == 1 and h > 1:
                        normalise(h // HG - 1)
                    if h == LN_HEAD and not last_one:
                        norm_stats(1, tile_of(b + 1))
                    if h == LN_HEAD + 1 and not last_one:
                        norm(2 * b + (2 * B + 1), 1, tile_of(b + 1))
                normalise(3)
                if not last_one:
                    dve.wait_ge(k1_ready, 2 * b + 4)
                    front_keys(range(HG))
                    front_values(b + 1)
                for q in range(TB):
                    if q % 2 == 0:
                        dve.wait_ge(attn1, 2 * b + (q // 2 + 1))
                    last = dve.tensor_tensor(tile(q), bank[7 if q // 2 else 5][:, (q % 2) * D:(q % 2 + 1) * D], tile(q), ALU.add)
                chn.link(last)
                for q in range(TB):
                    last = dve.tensor_tensor(tile(q), tile(q), bo1[:, :], ALU.add)
                chn.link(last)
                norm_stats(0, tile)
                norm(2 * b + (2 * B + 2 - last_one), 0, tile)
                norm_rows(0, tile, row_of(b))
                if last_one:
                    choose(1, b, 0, 7)
                    places(1, b, 0, 7)

            combine(0, range(1))
            norm_stats(1, tile_of(0))
            norm(2 * B, 1, tile_of(0))
            dve.wait_ge(k1_ready, 2)
            front_keys(range(HG))
            combine(0, range(1, 2))
            front_values(0)
            combine(0, range(2, B))
            batch(0, first=True)
            with dve.Fori(1, B - 1) as b:
                chn.enter(b + (-1), STEPS_ATTN1)
                batch(b)
            chn.leave(B - 2)
            batch(B - 1, last_one=True)
            blocks(1)
            experts(1)
            combine(1, range(B))


def kernel(**inputs):
    import numpy as np
    import concourse.bacc as bacc
    from concourse import mybir as mb
    from concourse.bass_utils import run_bass_kernel_spmd as run

    a = {k: np.ascontiguousarray(v) for k, v in inputs.items()}
    a["con"] = constants()
    a["ctxT"] = np.ascontiguousarray(a.pop("ctx_1024").reshape(B * S, D).T)
    a["gate0T"] = np.ascontiguousarray(a.pop("L0_ffn_gate_w").T)
    a["up0"] = np.ascontiguousarray(a.pop("L0_ffn_w_up").transpose(0, 2, 1))
    a["dn0"] = np.ascontiguousarray(a.pop("L0_ffn_w_down").transpose(0, 2, 1))
    a["up1"] = a.pop("L1_ffn_Wup")
    a["bup1T"] = np.ascontiguousarray(a.pop("L1_ffn_bup").reshape(E1, H1 // P, P).transpose(0, 2, 1))
    a["bq1T"] = np.ascontiguousarray(a.pop("L1_xattn_bq").reshape(KC, P).T)
    a["bk1T"] = np.ascontiguousarray(a.pop("L1_xattn_bk").reshape(KC, P).T)

    nc = bacc.Bacc("TRN2", target_bir_lowering=False, num_devices=1)
    aps = {k: nc.dram_tensor(f"in_{k}", v.shape, mb.dt.from_np(v.dtype), kind="ExternalInput").ap() for k, v in a.items()}
    out = nc.dram_tensor("out_0", (B, S, D), F32, kind="ExternalOutput").ap()
    build(nc, aps, out)
    r = run(nc, [{f"in_{k}": v for k, v in a.items()}], core_ids=[0])
    return r.results[0]["out_0"]
```
